# Optimizing a Trainium2 kernel written in Bass

```python
import numpy as np
import jax
import jax.numpy as jnp

def _softmax(x, axis=-1):
    return jax.nn.softmax(x, axis=axis)

def _gelu(x):
    return jax.nn.gelu(x, approximate=True)

def _silu(x):
    return jax.nn.silu(x)

def _sigmoid(x):
    return jax.nn.sigmoid(x)

def _layernorm(x, axis=-1, eps=1e-05):
    m = jnp.mean(x, axis=axis, keepdims=True)
    v = jnp.var(x, axis=axis, keepdims=True)
    return (x - m) / jnp.sqrt(v + eps)

def _scatter_add(tgt, idx, src, axis=0):
    return tgt.at[idx].add(src)

def _segment_sum(src, seg, n):
    return jax.ops.segment_sum(src, seg, n)
kernel_name = 'mk_seq_preln_d2_jaxref_r8_ee3305'

def setup_inputs(seed: int=0):
    np.random.seed(seed)
    _w = jnp.asarray

    def _L0_attn_setup():
        import jax, jax.numpy as jnp
        import numpy as np
        import math
        D_MODEL, N_HEADS, D_K, D_C, D_HR = (128, 8, 128, 32, 32)
        B, S = (4, 256)
        key = jax.random.key(seed)
        ks = jax.random.split(key, 17)

        def lin(k, fan_in, fan_out):
            lim = 1.0 / math.sqrt(fan_in)
            kw, kb = jax.random.split(k)
            W = jax.random.uniform(kw, (fan_in, fan_out), jnp.float32, -lim, lim)
            b = jax.random.uniform(kb, (fan_out,), jnp.float32, -lim, lim)
            return (W, b)
        W_DQ, b_DQ = lin(ks[0], D_MODEL, D_C)
        W_UQ, b_UQ = lin(ks[1], D_C, N_HEADS * D_K)
        W_DKV, b_DKV = lin(ks[2], D_MODEL, D_C)
        W_UK, b_UK = lin(ks[3], D_C, N_HEADS * D_K)
        W_UV, b_UV = lin(ks[4], D_C, N_HEADS * D_K)
        W_QR, b_QR = lin(ks[5], D_C, N_HEADS * D_HR)
        W_KR, b_KR = lin(ks[6], D_MODEL, D_HR)
        W_O, b_O = lin(ks[7], N_HEADS * D_K, D_MODEL)
        h_t = jax.random.normal(ks[8], (B, S, D_MODEL), jnp.float32)
        return {'h_t': h_t, 'W_DQ': W_DQ, 'b_DQ': b_DQ, 'W_UQ': W_UQ, 'b_UQ': b_UQ, 'W_DKV': W_DKV, 'b_DKV': b_DKV, 'W_UK': W_UK, 'b_UK': b_UK, 'W_UV': W_UV, 'b_UV': b_UV, 'W_QR': W_QR, 'b_QR': b_QR, 'W_KR': W_KR, 'b_KR': b_KR, 'W_O': W_O, 'b_O': b_O}
    _L0_attn_in = _L0_attn_setup()

    def _L0_ffn_setup():
        import jax, jax.numpy as jnp
        import numpy as np
        TOP_K = 2
        key = jax.random.key(seed)
        ks = jax.random.split(key, 6)
        B, S, D, BN, E = (32, 256, 128, 64, 8)
        return {'x': jax.random.normal(ks[0], (B, S, D), dtype=jnp.float32), 'gate_w': jax.random.normal(ks[1], (E, D), dtype=jnp.float32) * 0.02, 'down_w': jax.random.normal(ks[2], (E, BN, D), dtype=jnp.float32) * 0.02, 'down_b': jax.random.normal(ks[3], (E, BN), dtype=jnp.float32) * 0.02, 'up_w': jax.random.normal(ks[4], (E, D, BN), dtype=jnp.float32) * 0.02, 'up_b': jax.random.normal(ks[5], (E, D), dtype=jnp.float32) * 0.02}
    _L0_ffn_in = _L0_ffn_setup()

    def _L1_attn_setup():
        import jax, jax.numpy as jnp
        import numpy as np
        HEADS = 16
        DIM_HEAD = 64
        ANCHORS = 64
        DIM = 128
        INNER = HEADS * DIM_HEAD
        SCALE = DIM_HEAD ** (-0.5)
        key = jax.random.key(seed)
        ks = jax.random.split(key, 5)
        b, n = (8, 512)
        x = jax.random.normal(ks[0], (b, n, DIM), dtype=jnp.float32)
        W_emb = jax.random.normal(ks[1], (2 * INNER, DIM), dtype=jnp.float32) * DIM ** (-0.5)
        W_anchor = jax.random.normal(ks[2], (ANCHORS, DIM_HEAD), dtype=jnp.float32) * DIM_HEAD ** (-0.5)
        W_out = jax.random.normal(ks[3], (DIM, INNER), dtype=jnp.float32) * INNER ** (-0.5)
        b_out = jnp.zeros((DIM,), dtype=jnp.float32)
        return {'x': x, 'W_emb': W_emb, 'W_anchor': W_anchor, 'W_out': W_out, 'b_out': b_out}
    _L1_attn_in = _L1_attn_setup()

    def _L1_ffn_setup():
        import jax, jax.numpy as jnp
        import numpy as np
        B, S, D, M, E, K = (2, 256, 128, 176, 8, 2)
        key = jax.random.key(seed)
        k0, k1, k2, k3, k4 = jax.random.split(key, 5)
        scale = 0.02
        return {'x': jax.random.normal(k0, (B, S, D), dtype=jnp.float32), 'w_gate': jax.random.normal(k1, (D, E), dtype=jnp.float32) * scale, 'w_g': jax.random.normal(k2, (E, D, M), dtype=jnp.float32) * scale, 'w_u': jax.random.normal(k3, (E, D, M), dtype=jnp.float32) * scale, 'w_d': jax.random.normal(k4, (E, M, D), dtype=jnp.float32) * scale}
    _L1_ffn_in = _L1_ffn_setup()
    _d = {'L0_attn_h_t': _L0_attn_in['h_t'], 'L0_attn_W_DQ': _L0_attn_in['W_DQ'], 'L0_attn_b_DQ': _L0_attn_in['b_DQ'], 'L0_attn_W_UQ': _L0_attn_in['W_UQ'], 'L0_attn_b_UQ': _L0_attn_in['b_UQ'], 'L0_attn_W_DKV': _L0_attn_in['W_DKV'], 'L0_attn_b_DKV': _L0_attn_in['b_DKV'], 'L0_attn_W_UK': _L0_attn_in['W_UK'], 'L0_attn_b_UK': _L0_attn_in['b_UK'], 'L0_attn_W_UV': _L0_attn_in['W_UV'], 'L0_attn_b_UV': _L0_attn_in['b_UV'], 'L0_attn_W_QR': _L0_attn_in['W_QR'], 'L0_attn_b_QR': _L0_attn_in['b_QR'], 'L0_attn_W_KR': _L0_attn_in['W_KR'], 'L0_attn_b_KR': _L0_attn_in['b_KR'], 'L0_attn_W_O': _L0_attn_in['W_O'], 'L0_attn_b_O': _L0_attn_in['b_O'], 'L0_ffn_gate_w': _L0_ffn_in['gate_w'], 'L0_ffn_down_w': _L0_ffn_in['down_w'], 'L0_ffn_down_b': _L0_ffn_in['down_b'], 'L0_ffn_up_w': _L0_ffn_in['up_w'], 'L0_ffn_up_b': _L0_ffn_in['up_b'], 'L1_attn_W_emb': _L1_attn_in['W_emb'], 'L1_attn_W_anchor': _L1_attn_in['W_anchor'], 'L1_attn_W_out': _L1_attn_in['W_out'], 'L1_attn_b_out': _L1_attn_in['b_out'], 'L1_ffn_w_gate': _L1_ffn_in['w_gate'], 'L1_ffn_w_g': _L1_ffn_in['w_g'], 'L1_ffn_w_u': _L1_ffn_in['w_u'], 'L1_ffn_w_d': _L1_ffn_in['w_d']}
    _x0 = _d['L0_attn_h_t']
    _d['L0_attn_h_t'] = jax.random.normal(jax.random.fold_in(jax.random.key(seed), 1), (1, 2048, 128), dtype=_x0.dtype)
    del _x0
    return _d

def reference(L0_attn_h_t, L0_attn_W_DQ, L0_attn_b_DQ, L0_attn_W_UQ, L0_attn_b_UQ, L0_attn_W_DKV, L0_attn_b_DKV, L0_attn_W_UK, L0_attn_b_UK, L0_attn_W_UV, L0_attn_b_UV, L0_attn_W_QR, L0_attn_b_QR, L0_attn_W_KR, L0_attn_b_KR, L0_attn_W_O, L0_attn_b_O, L0_ffn_gate_w, L0_ffn_down_w, L0_ffn_down_b, L0_ffn_up_w, L0_ffn_up_b, L1_attn_W_emb, L1_attn_W_anchor, L1_attn_W_out, L1_attn_b_out, L1_ffn_w_gate, L1_ffn_w_g, L1_ffn_w_u, L1_ffn_w_d):

    def _L0_attn_ref(h_t, W_DQ, b_DQ, W_UQ, b_UQ, W_DKV, b_DKV, W_UK, b_UK, W_UV, b_UV, W_QR, b_QR, W_KR, b_KR, W_O, b_O):
        import jax, jax.numpy as jnp
        import numpy as np
        import math
        D_MODEL, N_HEADS, D_K, D_C, D_HR = (128, 8, 128, 32, 32)
        B, S = (4, 256)
        b, s, _ = h_t.shape
        c_q = h_t @ W_DQ + b_DQ
        c_kv = h_t @ W_DKV + b_DKV
        q_c = (c_q @ W_UQ + b_UQ).reshape(b, s, N_HEADS, D_K).transpose(0, 2, 1, 3)
        k_c = (c_kv @ W_UK + b_UK).reshape(b, s, N_HEADS, D_K).transpose(0, 2, 1, 3)
        v_c = (c_kv @ W_UV + b_UV).reshape(b, s, N_HEADS, D_K).transpose(0, 2, 1, 3)
        q_r = (c_q @ W_QR + b_QR).reshape(b, s, N_HEADS, D_HR).transpose(0, 2, 1, 3)
        k_r = (h_t @ W_KR + b_KR)[:, None, :, :]
        k_r = jnp.broadcast_to(k_r, (b, N_HEADS, s, D_HR))
        q = jnp.concatenate([q_c, q_r], axis=-1)
        k = jnp.concatenate([k_c, k_r], axis=-1)
        scale = 1.0 / math.sqrt(D_K + D_HR)
        scores = jnp.einsum('bhsd,bhtd->bhst', q, k) * scale
        attn = jax.nn.softmax(scores, axis=-1)
        o = jnp.einsum('bhst,bhtd->bhsd', attn, v_c)
        o = o.transpose(0, 2, 1, 3).reshape(b, s, N_HEADS * D_K)
        return o @ W_O + b_O

    def _L0_ffn_ref(x, gate_w, down_w, down_b, up_w, up_b):
        import jax, jax.numpy as jnp
        import numpy as np
        TOP_K = 2
        pooled = x.mean(axis=1)
        gate = jax.nn.softmax(pooled @ gate_w.T, axis=-1)
        top_w, top_i = jax.lax.top_k(gate, TOP_K)
        top_w = top_w / (top_w.sum(axis=-1, keepdims=True) + 1e-08)
        Wd = down_w[top_i]
        bd = down_b[top_i]
        Wu = up_w[top_i]
        bu = up_b[top_i]
        h = jax.nn.gelu(jnp.einsum('bsd,bkcd->bksc', x, Wd) + bd[:, :, None, :], approximate=False)
        h = h * top_w[:, :, None, None]
        out = jnp.einsum('bksc,bkdc->bsd', h, Wu)
        out = out + (top_w[:, :, None] * bu).sum(axis=1)[:, None, :]
        return out

    def _L1_attn_ref(x, W_emb, W_anchor, W_out, b_out):
        import jax, jax.numpy as jnp
        import numpy as np
        HEADS = 16
        DIM_HEAD = 64
        ANCHORS = 64
        DIM = 128
        INNER = HEADS * DIM_HEAD
        SCALE = DIM_HEAD ** (-0.5)
        b, n, _ = x.shape
        emb = x @ W_emb.T
        qk, v = jnp.split(emb, 2, axis=-1)
        qk = qk.reshape(b, n, HEADS, DIM_HEAD).transpose(0, 2, 1, 3)
        v = v.reshape(b, n, HEADS, DIM_HEAD).transpose(0, 2, 1, 3)
        anchor_B = qk @ W_anchor.T * SCALE
        attn = jax.nn.softmax(anchor_B, axis=-1)
        s = jnp.sum(attn, axis=-2)
        recip = s ** (-1.0)
        recip = jnp.where(jnp.isinf(recip), 0.0, recip)
        out = jnp.einsum('bhna,bhnd->bhad', attn, v)
        out = recip[..., None] * out
        out = jnp.einsum('bhna,bhad->bhnd', attn, out)
        out = out.transpose(0, 2, 1, 3).reshape(b, n, INNER)
        return out @ W_out.T + b_out

    def _L1_ffn_ref(x, w_gate, w_g, w_u, w_d):
        import jax, jax.numpy as jnp
        import numpy as np
        B, S, D, M, E, K = (2, 256, 128, 176, 8, 2)
        scores = x @ w_gate
        topk_scores, topk_idx = jax.lax.top_k(scores, K)
        topk_probs = jax.nn.softmax(topk_scores, axis=-1)
        gating = jnp.sum(jax.nn.one_hot(topk_idx, E, dtype=topk_probs.dtype) * topk_probs[..., None], axis=-2)
        hidden = jax.nn.silu(jnp.einsum('bsd,edm->ebsm', x, w_g)) * jnp.einsum('bsd,edm->ebsm', x, w_u)
        expert_out = jnp.einsum('ebsm,emd->ebsd', hidden, w_d)
        y = jnp.einsum('bse,ebsd->bsd', gating, expert_out)
        return y
    x = L0_attn_h_t
    x = x + _L0_attn_ref(_layernorm(x, axis=-1), L0_attn_W_DQ, L0_attn_b_DQ, L0_attn_W_UQ, L0_attn_b_UQ, L0_attn_W_DKV, L0_attn_b_DKV, L0_attn_W_UK, L0_attn_b_UK, L0_attn_W_UV, L0_attn_b_UV, L0_attn_W_QR, L0_attn_b_QR, L0_attn_W_KR, L0_attn_b_KR, L0_attn_W_O, L0_attn_b_O)
    x = x + _L0_ffn_ref(_layernorm(x, axis=-1), L0_ffn_gate_w, L0_ffn_down_w, L0_ffn_down_b, L0_ffn_up_w, L0_ffn_up_b)
    x = x + _L1_attn_ref(_layernorm(x, axis=-1), L1_attn_W_emb, L1_attn_W_anchor, L1_attn_W_out, L1_attn_b_out)
    x = x + _L1_ffn_ref(_layernorm(x, axis=-1), L1_ffn_w_gate, L1_ffn_w_g, L1_ffn_w_u, L1_ffn_w_d)
    return x

_drawn_inputs = setup_inputs


def setup_inputs(seed=0):
    import zlib

    import numpy as np

    out = dict(_drawn_inputs(seed))
    spreads = {'L1_attn_b_out': (0.0, 0.1)}
    factors = {'L0_attn_W_DQ': 8.0,
     'L0_attn_b_DQ': 8.0,
     'L0_attn_W_UQ': 8.0,
     'L0_attn_b_UQ': 8.0,
     'L0_attn_W_DKV': 8.0,
     'L0_attn_b_DKV': 2.761,
     'L0_attn_W_UK': 8.0,
     'L0_attn_b_UK': 8.0,
     'L0_attn_W_QR': 8.0,
     'L0_attn_b_QR': 8.0,
     'L0_attn_W_KR': 8.0,
     'L0_attn_b_KR': 8.0,
     'L0_ffn_gate_w': 2.871,
     'L0_ffn_down_w': 4.33,
     'L0_ffn_down_b': 8.0,
     'L0_ffn_up_w': 4.204,
     'L0_ffn_up_b': 2.973,
     'L1_attn_W_anchor': 8.0,
     'L1_ffn_w_gate': 8.0,
     'L1_ffn_w_g': 8.0,
     'L1_ffn_w_u': 8.0,
     'L1_ffn_w_d': 8.0}
    for name, (base, spread) in spreads.items():
        noise = np.random.default_rng([zlib.crc32(name.encode()), seed]).standard_normal(out[name].shape)
        drawn = base * np.exp(spread * noise) if base else spread * noise
        out[name] = jnp.asarray(drawn.astype(out[name].dtype))
    for name, factor in factors.items():
        out[name] = (out[name] * factor).astype(out[name].dtype)
    return out
```

```python
from contextlib import ExitStack

import concourse.bass as bass
from concourse import mybir

ALU = mybir.AluOpType
ACT = mybir.ActivationFunctionType
AX = mybir.AxisListType
F32 = mybir.dt.float32
F32R = mybir.dt.float32r
U32 = mybir.dt.uint32

P = 128
BLK = 512
TPB = BLK // P
EPS = 1e-5


def build_kernel(nc, d, out):
    S, D = d["L0_attn_h_t"].shape[1:]
    NT = S // P
    NB = S // BLK
    C = d["L0_attn_W_DQ"].shape[1]
    H = d["L0_attn_W_QR"].shape[1] // C
    DK = d["L0_attn_W_UQ"].shape[1] // H
    C1 = C + 1
    KW = 2 * C
    SCALE = float(DK + C) ** -0.5
    assert D == P and DK == P and NT == 16 and H == 8 and C == 32

    ctx = ExitStack()
    with ctx:
        def sb(name, shape, dt=F32):
            return ctx.enter_context(nc.sbuf_tensor(name, shape, dt))

        def sem(name):
            return ctx.enter_context(nc.semaphore(name))

        ps = ctx.enter_context(nc.psum_tensor("ps", [P, 8, BLK], F32))

        X = sb("X", [P, NT, D])
        ident = sb("ident", [P, P])
        ones_row = sb("ones_row", [1, P])
        mhalf = sb("mhalf", [P, TPB])

        E = d["L0_ffn_gate_w"].shape[0]
        BN = d["L0_ffn_down_w"].shape[1]
        A = d["L1_attn_W_anchor"].shape[0]
        H1 = d["L1_attn_W_out"].shape[1] // A
        HP = H1 // 2
        M1 = d["L1_ffn_w_g"].shape[2]
        CH = E * M1 // P
        assert E == 8 and 2 * BN == P and 2 * A == P and E * M1 == CH * P
        gate0 = sb("gate0", [E, D])
        down0 = sb("down0", [P, E, D])
        down0_b = sb("down0_b", [P, E])
        up0 = sb("up0", [P, E, BN])
        up0_b = sb("up0_b", [E, D])
        emb = sb("emb", [P, 2 * HP, D])
        anchor = sb("anchor", [A, A])
        w_out = sb("w_out", [P, H1 * A])
        b_out = sb("b_out", [1, D])
        gate1 = sb("gate1", [P, E])
        w_g = sb("w_g", [P, E, M1])
        w_u = sb("w_u", [P, E, M1])
        w_d = sb("w_d", [P, CH, D])
        g_w = sb("g_w", [P, 2, D])
        g_b = sb("g_b", [1, D])
        stats = sb("stats", [P, 2, TPB, 6])
        mv = sb("mv", [P, 2, TPB, 2])
        rstd = sb("rstd", [P, 2, TPB])
        vare = sb("vare", [P, 2, TPB])
        ua = sb("ua", [P, NT, H * C])
        ld_l0, ld_l1a, ld_l1f = sem("ld_l0"), sem("ld_l1a"), sem("ld_l1f")

        attn = ctx.enter_context(ExitStack())

        def sb(name, shape, dt=F32, stack=attn):
            return stack.enter_context(nc.sbuf_tensor(name, shape, dt))

        wa_hi = sb("wa_hi", [P, H + 1, P], F32R)
        wa_lo = sb("wa_lo", [P, H + 1, P], F32R)
        fold = sb("fold", [2 * C + 1, C1])
        key1 = sb("key1", [P, S], F32R)
        key2 = sb("key2", [P, S], F32R)
        cq = sb("cq", [P, S], F32R)
        val = sb("val", [P, NT, 2 * C + 1], F32R)
        w_head = sb("w_head", [P, 2, P], F32R)
        q_hi = sb("q_hi", [P, NB, BLK], F32R)
        q_lo = sb("q_lo", [P, NB, BLK], F32R)

        folding = ctx.enter_context(ExitStack())

        def sb(name, shape, dt=F32, stack=folding):
            return stack.enter_context(nc.sbuf_tensor(name, shape, dt))

        w_dq = sb("w_dq", [P, C])
        w_kk = sb("w_kk", [P, KW])
        b_q = sb("b_q", [C, 1])
        b_kk = sb("b_kk", [KW, 1])
        b_v = sb("b_v", [P, C])
        uq = sb("uq", [C1, H * DK])
        uk = sb("uk", [C1, H * DK])
        uv = sb("uv", [C1, H * DK])
        qr = sb("qr", [C1, H, C])
        w_o = sb("w_o", [P, H, D])
        b_o = sb("b_o", [1, D])
        uqT = sb("uqT", [P, H, C1])
        ukT = sb("ukT", [P, H, C1])
        uvT = sb("uvT", [P, H, C1])
        wa = sb("wa", [P, H + 1, P])
        va = sb("va", [P, H + 1])
        va_hi = sb("va_hi", [P, H + 1], F32R)
        va_lo = sb("va_lo", [P, H + 1], F32R)
        hn = sb("hn", [P, 2, TPB, D])
        hT = sb("hT", [P, 2, BLK])
        k_f = sb("k_f", [KW, 2, BLK])
        c_f = sb("c_f", [C, 2, BLK])
        v_f = sb("v_f", [P, 2, TPB, C])
        sq = sb("sq", [H + 1, S], F32R)
        sq_dram = nc.dram_tensor("sq_dram", [(H + 1) * S], F32)
        sq_flat = sq_dram.ap().rearrange("(a n) -> a n", a=1)

        ld_x = [sem(f"ld_x{b}") for b in range(NB)]
        ld_w = sem("ld_w")
        s_const = sem("s_const")
        s_zero = sem("s_zero")

        s_wT_ps, s_wT = sem("s_wT_ps"), sem("s_wT")
        s_a_ps, s_a = sem("s_a_ps"), sem("s_a")
        s_wa, s_wah, s_wal = sem("s_wa"), sem("s_wah"), sem("s_wal")
        s_g_ps, s_g = sem("s_g_ps"), sem("s_g")
        s_st, s_mv, s_ve, s_rstd, s_hn = sem("s_st"), sem("s_mv"), sem("s_ve"), sem("s_rstd"), sem("s_hn")
        s_hT_ps, s_hT = sem("s_hT_ps"), sem("s_hT")
        s_proj, s_kf, s_cf, s_vf = sem("s_proj"), sem("s_kf"), sem("s_cf"), sem("s_vf")
        s_khi, s_chi, s_vhi, s_split, s_k2 = sem("s_khi"), sem("s_chi"), sem("s_vhi"), sem("s_split"), sem("s_k2")
        s_sq_ps, s_sqe, s_sqd = sem("s_sq_ps"), sem("s_sqe"), sem("s_sqd")

        HD = H * DK

        with nc.Block() as block:
            @block.sync
            def _(sp):
                x_v = d["L0_attn_h_t"].rearrange("a (t p) d -> p (a t) d", p=P)
                for b in range(NB):
                    sp.dma_start(X[:, b * TPB:(b + 1) * TPB, :], x_v[:, b * TPB:(b + 1) * TPB, :]).then_inc(ld_x[b], 16)
                for r in (0, BN):
                    sp.dma_start(down0[r:r + BN, :, :], d["L0_ffn_down_w"].rearrange("e c d -> c e d")).then_inc(ld_l0, 16)
                    with nc.allow_non_contiguous_dma("8 x 64 words"):
                        sp.dma_start(down0_b[r:r + BN, :], d["L0_ffn_down_b"].rearrange("e c -> c e")).then_inc(ld_l0, 16)
                sp.dma_start(gate0[:, :], d["L0_ffn_gate_w"]).then_inc(ld_l0, 16)
                sp.dma_start(up0[:, :, :], d["L0_ffn_up_w"].rearrange("e d c -> d e c")).then_inc(ld_l0, 16)
                sp.dma_start(up0_b[:, :], d["L0_ffn_up_b"]).then_inc(ld_l0, 16)
                sp.dma_start(emb[:, :, :], d["L1_attn_W_emb"].rearrange("(t p) d -> p t d", p=P)).then_inc(ld_l1a, 16)
                sp.dma_start(anchor[:, :], d["L1_attn_W_anchor"]).then_inc(ld_l1a, 16)
                sp.dma_start(w_out[:, :], d["L1_attn_W_out"]).then_inc(ld_l1a, 16)
                sp.dma_start(b_out[:, :], d["L1_attn_b_out"].rearrange("(a n) -> a n", a=1)).then_inc(ld_l1a, 16)
                sp.dma_start(gate1[:, :], d["L1_ffn_w_gate"]).then_inc(ld_l1f, 16)
                sp.dma_start(w_g[:, :, :], d["L1_ffn_w_g"].rearrange("e d m -> d e m")).then_inc(ld_l1f, 16)
                sp.dma_start(w_u[:, :, :], d["L1_ffn_w_u"].rearrange("e d m -> d e m")).then_inc(ld_l1f, 16)
                sp.dma_start(w_d[:, :, :], d["L1_ffn_w_d"].rearrange("e m d -> (e m) d").rearrange("(c p) d -> p c d", p=P)).then_inc(ld_l1f, 16)
                sp.wait_ge(s_sqe, NB)
                sp.dma_start(sq_dram.ap().rearrange("(h s) -> h s", h=H + 1), sq[:, :].bitcast(F32)).then_inc(s_sqd, 16)
                sp.wait_ge(s_sqd, 16)

            @block.scalar
            def _(act):
                def load(dst, src):
                    act.dma_start(dst, src).then_inc(ld_w, 16)

                def row(name):
                    return d[name].rearrange("(a n) -> a n", a=1)

                def col(name):
                    return d[name].rearrange("(n a) -> n a", a=1)

                for t, name in ((uq, "UQ"), (uk, "UK"), (uv, "UV")):
                    load(t[0:C, :], d[f"L0_attn_W_{name}"])
                    load(t[C:C1, :], row(f"L0_attn_b_{name}"))
                load(qr[0:C, :, :], d["L0_attn_W_QR"].rearrange("c (h r) -> c h r", h=H))
                load(qr[C:C1, :, :], d["L0_attn_b_QR"].rearrange("(a h r) -> a h r", a=1, h=H))
                load(w_dq[:, :], d["L0_attn_W_DQ"])
                load(w_kk[:, 0:C], d["L0_attn_W_DKV"])
                load(w_kk[:, C:KW], d["L0_attn_W_KR"])
                load(b_q[:, :], col("L0_attn_b_DQ"))
                load(b_kk[0:C, :], col("L0_attn_b_DKV"))
                load(b_kk[C:KW, :], col("L0_attn_b_KR"))
                load(b_v[:, :], row("L0_attn_b_DKV").to_broadcast([P, C]))
                load(w_o[:, :, :], d["L0_attn_W_O"].rearrange("(h k) n -> k h n", h=H))
                load(b_o[:, :], row("L0_attn_b_O"))

                act.wait_ge(s_wT_ps, 3)
                act.copy(uqT[:, :, :], ps[:, 0, 0:H * C1].rearrange("p (h c) -> p h c", h=H)).then_inc(s_wT, 1)
                act.copy(ukT[:, :, :], ps[:, 1, 0:H * C1].rearrange("p (h c) -> p h c", h=H)).then_inc(s_wT, 1)
                act.copy(uvT[:, :, :], ps[:, 2, 0:H * C1].rearrange("p (h c) -> p h c", h=H)).then_inc(s_wT, 1)
                act.wait_ge(s_a_ps, 1)
                act.wait_ge(s_zero, 1)
                a_ps = ps[0:C1, 3, 0:H * C1].rearrange("p (h c) -> p h c", h=H)
                for r in (0, 64):
                    for c0 in (0, 64):
                        act.copy(wa[r:r + C1, 0:H, c0:c0 + C], a_ps[:, :, 0:C]).then_inc(s_a, 1)
                    act.copy(va[r:r + C1, 0:H], a_ps[:, :, C:C1].rearrange("p h c -> p (h c)")).then_inc(s_a, 1)
                act.wait_ge(s_wa, 4)
                act.wait_ge(s_a, 6)
                act.copy(wa_hi[:, :, :], wa[:, :, :]).then_inc(s_wah, 1)
                act.copy(va_hi[:, :], va[:, :]).then_inc(s_wah, 1)
                act.wait_ge(s_g_ps, 1)
                act.copy(g_w[:, :, :], ps[:, 4, 0:2 * D].rearrange("p (m n) -> p m n", m=2)).then_inc(s_g, 1)
                for b in range(NB):
                    act.wait_ge(s_hT_ps, b + 1)
                    if b >= 2:
                        act.wait_ge(s_proj, b - 1)
                    act.copy(hT[:, b % 2, :], ps[:, b % 2, :]).then_inc(s_hT, 1)
                    act.wait_ge(s_proj, b + 1)
                    if b >= 2:
                        act.wait_ge(s_split, 3 * (b - 1))
                    act.activation(k_f[:, b % 2, :], ps[0:KW, 2 + b % 2, :], ACT.Identity, bias=b_kk[:, :]).then_inc(s_kf, 1)
                    act.activation(c_f[:, b % 2, :], ps[0:C, 5 + b % 2, :], ACT.Identity, bias=b_q[:, :]).then_inc(s_cf, 1)
                    act.wait_ge(s_kf, b + 1)
                    act.copy(key1[0:KW, b * BLK:(b + 1) * BLK], k_f[:, b % 2, :]).then_inc(s_khi, 1)
                    act.wait_ge(s_cf, b + 1)
                    act.copy(cq[0:C, b * BLK:(b + 1) * BLK], c_f[:, b % 2, :]).then_inc(s_chi, 1)
                for b in range(NB):
                    act.wait_ge(s_sq_ps, b + 1)
                    act.copy(sq[:, b * BLK:(b + 1) * BLK], ps[0:H + 1, b % 2, :]).then_inc(s_sqe, 1)

            @block.gpsimd
            def _(pool):
                pool.memset(ident[:, :], 0.0).then_inc(s_const, 1)
                pool.wait_ge(s_const, 1)
                pool.affine_select(out=ident[:, :], in_=ident[:, :], compare_op=ALU.not_equal, fill=1.0, base=0,
                                   pattern=[[-1, P]], channel_multiplier=1).then_inc(s_const, 1)
                pool.wait_ge(s_const, 2)
                pool.memset(ones_row[:, :], 1.0).then_inc(s_const, 1)
                pool.wait_ge(s_const, 3)
                pool.memset(mhalf[:, :], -0.5).then_inc(s_const, 1)
                pool.wait_ge(s_const, 4)
                pool.memset(fold[:, :], 0.0).then_inc(s_const, 1)
                pool.wait_ge(s_const, 5)
                for n, base in enumerate((0, -C)):
                    pool.affine_select(out=fold[0:2 * C, 0:C], in_=fold[0:2 * C, 0:C], compare_op=ALU.not_equal,
                                       fill=1.0, base=base, pattern=[[-1, C]], channel_multiplier=1).then_inc(s_const, 1)
                    pool.wait_ge(s_const, 6 + n)
                pool.memset(fold[2 * C:2 * C + 1, C:C1], 1.0).then_inc(s_const, 1)
                pool.wait_ge(s_const, 8)
                for n, (t, value) in enumerate(((cq[:, :], 0.0), (key2[KW:P, :], 0.0), (q_lo[KW:P, :, :], 0.0),
                                                (cq[C:C1, :], 1.0), (key2[64:65, :], 1.0), (key2[96:97, :], 1.0),
                                                (val[:, :, 2 * C:2 * C + 1], 1.0))):
                    pool.memset(t.bitcast(F32), value).then_inc(s_k2, 1)
                    pool.wait_ge(s_k2, n + 1)
                for b in range(NB):
                    pool.wait_ge(s_mv, TPB * (b + 1))
                    if b >= 2:
                        pool.wait_ge(s_hn, TPB * (b - 1))
                    pool.tensor_scalar(vare[:, b % 2, :], mv[:, b % 2, :, 1], EPS, None, ALU.add).then_inc(s_ve, 1)
                    pool.wait_ge(s_ve, b + 1)
                    pool.tensor_tensor(rstd[:, b % 2, :], vare[:, b % 2, :], mhalf[:, :], ALU.pow).then_inc(s_rstd, 1)
                pool.wait_ge(s_rstd, NB)
                for b in range(NB):
                    pool.wait_ge(s_khi, b + 1)
                    pool.tensor_copy(key2[0:KW, b * BLK:(b + 1) * BLK], key1[0:KW, b * BLK:(b + 1) * BLK]).then_inc(s_k2, 1)

            @block.vector
            def _(dve):
                dve.memset(wa[:, :, :], 0.0)
                dve.memset(va[:, :], 0.0).then_inc(s_zero, 1)
                dve.wait_ge(s_zero, 1)
                dve.wait_ge(ld_w, 16 * 17)
                for r in (0, 64):
                    for c0 in (C, 64 + C):
                        dve.tensor_copy(wa[r:r + C1, 0:H, c0:c0 + C], qr[:, :, :]).then_inc(s_wa, 1)
                dve.wait_ge(s_wah, 2)
                dve.tensor_tensor(wa_lo[:, :, :], wa[:, :, :], wa_hi[:, :, :].bitcast(F32), ALU.subtract).then_inc(s_wal, 1)
                dve.tensor_tensor(va_lo[:, :], va[:, :], va_hi[:, :].bitcast(F32), ALU.subtract).then_inc(s_wal, 1)
                dve.wait_ge(s_g_ps, 2)
                dve.tensor_tensor(g_b[:, :], ps[0:1, 7, 0:D], b_o[:, :], ALU.add).then_inc(s_g, 1)

                def norm_stats(b):
                    dve.wait_ge(ld_x[b], 16)
                    for i in range(TPB):
                        dve.bn_stats(stats[:, b % 2, i, :], X[:, TPB * b + i, :]).then_inc(s_st, 1)
                    for i in range(TPB):
                        dve.wait_ge(s_st, TPB * b + i + 1)
                        dve.bn_aggr(mv[:, b % 2, i, :], stats[:, b % 2, i, :]).then_inc(s_mv, 1)

                def norm(b):
                    dve.wait_ge(s_rstd, b + 1)
                    if b >= 2:
                        dve.wait_ge(s_hT_ps, b - 1)
                    for i in range(TPB):
                        dve.tensor_scalar(hn[:, b % 2, i, :], X[:, TPB * b + i, :], mv[:, b % 2, i, 0:1],
                                          rstd[:, b % 2, i:i + 1], ALU.subtract, ALU.mult).then_inc(s_hn, 1)

                norm_stats(0)
                for b in range(NB):
                    if b + 1 < NB:
                        norm_stats(b + 1)
                    norm(b)
                    dve.wait_ge(s_proj, b + 1)
                    dve.tensor_tensor(v_f[:, b % 2, :, :], ps[:, 4, 0:TPB * C].rearrange("p (i c) -> p i c", i=TPB),
                                      b_v[:, :].unsqueeze(1).to_broadcast([P, TPB, C]), ALU.add).then_inc(s_vf, 1)
                    dve.wait_ge(s_vf, b + 1)
                    dve.tensor_copy(val[:, TPB * b:TPB * (b + 1), 0:C], v_f[:, b % 2, :, :]).then_inc(s_vhi, 1)
                    dve.wait_ge(s_vhi, b + 1)
                    dve.tensor_tensor(val[:, TPB * b:TPB * (b + 1), C:2 * C], v_f[:, b % 2, :, :],
                                      val[:, TPB * b:TPB * (b + 1), 0:C].bitcast(F32), ALU.subtract).then_inc(s_split, 1)
                    cols = slice(b * BLK, (b + 1) * BLK)
                    dve.wait_ge(s_khi, b + 1)
                    dve.tensor_tensor(key1[KW:P, cols], k_f[:, b % 2, :], key1[0:KW, cols].bitcast(F32),
                                      ALU.subtract).then_inc(s_split, 1)
                    dve.wait_ge(s_chi, b + 1)
                    dve.tensor_tensor(cq[64:64 + C, cols], c_f[:, b % 2, :], cq[0:C, cols].bitcast(F32),
                                      ALU.subtract).then_inc(s_split, 1)

            @block.tensor
            def _(pe):
                pe.wait_ge(s_const, 8)
                pe.wait_ge(ld_w, 16 * 17)
                for j, w in enumerate((uq, uk, uv)):
                    for h in range(H):
                        last = pe.transpose(ps[:, j, h * C1:(h + 1) * C1], w[:, h * DK:(h + 1) * DK], ident[0:C1, 0:C1])
                    last.then_inc(s_wT_ps, 1)
                pe.wait_ge(s_wT, 3)
                for h in range(H):
                    last = pe.matmul(ps[0:C1, 3, h * C1:(h + 1) * C1], uqT[:, h, :], ukT[:, h, :], start=True, stop=True)
                last.then_inc(s_a_ps, 1)
                for h in range(H):
                    j, m = h % 4, h // 4
                    last = pe.matmul(ps[C * j:C * (j + 1), 4, m * D:(m + 1) * D], uvT[:, h, 0:C], w_o[:, h, :],
                                     start=True, stop=True)
                last.then_inc(s_g_ps, 1)
                for h in range(H):
                    last = pe.matmul(ps[0:1, 7, 0:D], uvT[:, h, C:C1], w_o[:, h, :], start=(h == 0), stop=(h == H - 1))
                last.then_inc(s_g_ps, 1)
                for b in range(NB):
                    pe.wait_ge(s_hn, TPB * (b + 1))
                    if b < 2:
                        pe.wait_ge(s_wT, 3)
                    else:
                        pe.wait_ge(s_hT, b - 1)
                    for i in range(TPB):
                        last = pe.transpose(ps[:, b % 2, i * P:(i + 1) * P], hn[:, b % 2, i, :], ident[:, :])
                    last.then_inc(s_hT_ps, 1)
                    pe.wait_ge(s_hT, b + 1)
                    if b == 0:
                        pe.wait_ge(s_a, 6)
                        pe.wait_ge(s_g, 1)
                    else:
                        pe.wait_ge(s_vf, b)
                    if b >= 2:
                        pe.wait_ge(s_cf, b - 1)
                    pe.matmul(ps[0:KW, 2 + b % 2, :], w_kk[:, :], hT[:, b % 2, :], start=True, stop=True)
                    pe.matmul(ps[0:C, 5 + b % 2, :], w_dq[:, :], hT[:, b % 2, :], start=True, stop=True)
                    for i in range(TPB):
                        last = pe.matmul(ps[:, 4, i * C:(i + 1) * C], hT[:, b % 2, i * P:(i + 1) * P], w_kk[:, 0:C],
                                         start=True, stop=True)
                    last.then_inc(s_proj, 1)
                pe.wait_ge(s_wal, 2)
                pe.wait_ge(s_k2, 7)
                for b in range(NB):
                    pe.wait_ge(s_split, 3 * (b + 1))
                    pe.wait_ge(s_hT, NB)
                    if b >= 2:
                        pe.wait_ge(s_sqe, b - 1)
                    pe.matmul(ps[0:H + 1, b % 2, :], va_hi[:, :], cq[:, b * BLK:(b + 1) * BLK], start=True, stop=False)
                    pe.matmul(ps[0:H + 1, b % 2, :], va_lo[:, :], cq[:, b * BLK:(b + 1) * BLK], start=False,
                              stop=True).then_inc(s_sq_ps, 1)

        folding.close()

        def sb(name, shape, dt=F32):
            return attn.enter_context(nc.sbuf_tensor(name, shape, dt))

        p32 = sb("p32", [P, 2, 2 * BLK])
        p_hi = sb("p_hi", [P, 4, 2 * BLK], F32R)
        p_lo = sb("p_lo", [P, 4, 2 * BLK], F32R)
        mx = sb("mx", [P, 2, TPB, 2])
        nmx = sb("nmx", [P, 2, TPB])
        u_sb = sb("u_sb", [2 * C + 1, BLK])
        rden = sb("rden", [P, TPB])

        PAIRS = NT // 2
        LAG = 3
        NBLK = H * NB
        s_wh = sem("s_wh")
        s_qps, s_qhi, s_qlo, s_qc = sem("s_qps"), sem("s_qhi"), sem("s_qlo"), sem("s_qc")
        s_mps, s_mrd, s_nmx, s_shps, s_shift = sem("s_mps"), sem("s_mrd"), sem("s_nmx"), sem("s_shps"), sem("s_shift")
        s_sc, s_exp, s_phi, s_plo, s_pv = sem("s_sc"), sem("s_exp"), sem("s_phi"), sem("s_plo"), sem("s_pv")
        s_usb, s_utps, s_rden, s_ut = sem("s_usb"), sem("s_utps"), sem("s_rden"), sem("s_ut")
        sc_ps = [ps[:, 0:2, :], ps[:, 2:4, :]]

        def chunk_of(h, k, slot):
            c = (slot + 2) % PAIRS
            ahead = 1 if slot + 2 < PAIRS else 2
            return 4 * h + k + ahead, (k + ahead) % NB, c

        with nc.Block() as block:
            @block.gpsimd
            def _(pool):
                def weights(h):
                    pool.tensor_copy(w_head[:, 0, :], wa_hi[:, h, :])
                    pool.tensor_copy(w_head[:, 1, :], wa_lo[:, h, :]).then_inc(s_wh, 1)

                pool.tensor_copy(w_head[:, 0, :], wa_hi[:, 0, :])
                pool.tensor_copy(w_head[:, 1, :], wa_lo[:, 0, :]).then_inc(s_wh, 1)
                with pool.Fori(1, H + 1) as h:
                    pool.wait_ge(s_qps, 4 * h)
                    pool.tensor_copy(w_head[:, 0, :], wa_hi[:, bass.ds(h, 1), :].rearrange("p a c -> p (a c)"))
                    pool.tensor_copy(w_head[:, 1, :], wa_lo[:, bass.ds(h, 1), :].rearrange("p a c -> p (a c)")).then_inc(s_wh, 1)

            @block.tensor
            def _(pe):
                def query(n, k, head):
                    bank = 7 - k % 2
                    pe.wait_ge(s_wh, head + 1)
                    cols = cq[:, k * BLK:(k + 1) * BLK]
                    pe.matmul(ps[:, bank, :], w_head[:, 0, :], cols, start=True, stop=False)
                    pe.matmul(ps[:, bank, :], w_head[:, 1, :], cols, start=False, stop=True).then_inc(s_qps, 1)

                def rows(n, k, c, first=False):
                    if c == 0:
                        pe.wait_ge(s_qhi, n + 1)
                    if not first:
                        pe.wait_ge(s_mrd, PAIRS * n + c)
                    i, half = c // 2, c % 2
                    for j in range(2):
                        t0 = (2 * half + j) * BLK
                        last = pe.matmul(ps[:, 4 + j, :], q_hi[0:KW, k, i * P:(i + 1) * P], key1[0:KW, t0:t0 + BLK],
                                         start=True, stop=True)
                    last.then_inc(s_mps, 1)

                def shift(n, k):
                    bank = 6 + k % 2
                    pe.wait_ge(s_nmx, n + 1)
                    pe.wait_ge(s_qlo, n + 2)
                    pe.wait_ge(s_qhi, n + 2)
                    for i in range(TPB):
                        last = pe.matmul(ps[0:1, bank, i * P:(i + 1) * P], nmx[:, k % 2, i:i + 1], ident[:, :],
                                         start=True, stop=True)
                    last.then_inc(s_shps, 1)

                def pv(n, k, p, h0):
                    g = PAIRS * n + p
                    pe.wait_ge(s_phi, g + 1)
                    pe.wait_ge(s_plo, g + 1)
                    if p == 0:
                        pe.wait_ge(s_shift, n + 1)
                        pe.wait_ge(s_qlo, n + 2)
                        pe.wait_ge(s_qhi, n + 2)
                        if h0 is None or k >= 2:
                            pe.wait_ge(s_ut, n - 1)
                    for part in (p_hi, p_lo):
                        for j in range(2):
                            t = 2 * p + j
                            last = pe.matmul(ps[0:2 * C + 1, 6 + k % 2, :], val[:, t, :],
                                             part[:, p % 4, j * BLK:(j + 1) * BLK],
                                             start=(p == 0 and part is p_hi and j == 0),
                                             stop=(p == PAIRS - 1 and part is p_lo and j == 1))
                    last.then_inc(s_pv, 1)

                def turn(n, k):
                    pe.wait_ge(s_usb, n + 1)
                    for i in range(TPB):
                        last = pe.matmul(ps[:, 6 + k % 2, i * C1:(i + 1) * C1], u_sb[:, i * P:(i + 1) * P], fold[:, :],
                                         start=True, stop=True)
                    last.then_inc(s_utps, 1)

                def head(h, h0):
                    for k in range(NB):
                        n = 4 * h + k
                        for slot in range(PAIRS):
                            g = PAIRS * n + slot
                            if slot == 7:
                                shift(n + 1, (k + 1) % NB)
                            rows(*chunk_of(h, k, slot))
                            if slot == 0:
                                pe.wait_ge(s_shift, n + 1)
                                pe.wait_ge(s_qlo, n + 1)
                                pe.wait_ge(s_qc, 16 * (n + 1))
                            if h0 is None or k > 0 or slot >= 2:
                                pe.wait_ge(s_exp, g - 1)
                            for j in range(2):
                                cols = slice((2 * slot + j) * P, (2 * slot + j + 1) * P)
                                pe.matmul(sc_ps[slot % 2][:, j, :], key1[:, cols], q_hi[:, k, :], start=True, stop=False)
                                last = pe.matmul(sc_ps[slot % 2][:, j, :], key2[:, cols], q_lo[:, k, :], start=False,
                                                 stop=True)
                            last.then_inc(s_sc, 1)
                            if slot == 0 and (h0 is None or k >= 2):
                                turn(n - 2, k)
                            if slot == 4:
                                if h0 is None or k > 0:
                                    pe.wait_ge(s_usb, n)
                                query(n + 2, (k + 2) % NB, h if k < 2 else h + 1)
                            if slot >= LAG:
                                pv(n, k, slot - LAG, h0)
                            elif h0 is None or k > 0:
                                pv(n - 1, (k - 1) % NB, slot - LAG + PAIRS, h0)

                query(0, 0, 0)
                query(1, 1, 0)
                for c in range(PAIRS):
                    rows(0, 0, c, first=(c == 0))
                rows(1, 1, 0)
                rows(1, 1, 1)
                shift(0, 0)
                head(0, 0)
                with pe.Fori(1, H) as h:
                    head(h, None)
                for p in range(PAIRS - LAG, PAIRS):
                    pv(NBLK - 1, NB - 1, p, None)
                turn(NBLK - 2, 2)
                pe.wait_ge(s_ut, NBLK - 1)
                turn(NBLK - 1, 3)

            @block.scalar
            def _(act):
                def query_hi(n, k):
                    act.wait_ge(s_qps, n + 1)
                    act.copy(q_hi[:, k, :], ps[:, 7 - k % 2, :]).then_inc(s_qhi, 1)

                def constants(n, k):
                    act.dma_start(q_lo[KW:KW + 1, k, :].bitcast(F32), sq_flat[:, bass.ds(n * BLK, BLK)]).then_inc(s_qc, 16)

                def shift_row(n, k):
                    act.wait_ge(s_shps, n + 1)
                    act.copy(q_lo[96:97, k, :], ps[0:1, 6 + k % 2, :]).then_inc(s_shift, 1)

                def sums(n, k):
                    act.wait_ge(s_pv, PAIRS * (n + 1))
                    act.copy(u_sb[:, :], ps[0:2 * C + 1, 6 + k % 2, :]).then_inc(s_usb, 1)

                def high(g, b4):
                    act.wait_ge(s_exp, g + 1)
                    act.copy(p_hi[:, b4, :], p32[:, b4 % 2, :]).then_inc(s_phi, 1)

                def head(h, h0):
                    for k in range(NB):
                        n = 4 * h + k
                        for slot in range(PAIRS):
                            g = PAIRS * n + slot
                            if slot == 4 and (h0 is None or k > 0):
                                if h0 is None or k > 1:
                                    act.wait_ge(s_utps, n - 1)
                                sums(n - 1, (k - 1) % NB)
                            if slot == 5:
                                query_hi(n + 2, (k + 2) % NB)
                            if slot == 6:
                                act.wait_ge(s_qc, 16 * (n + 2))
                                constants(n + 2, (k + 2) % NB)
                            if h0 is None or k > 0 or slot >= 1:
                                if h0 is None or k > 0 or slot >= 5:
                                    act.wait_ge(s_pv, g - 4)
                                high(g - 1, (slot - 1) % 4)
                            act.wait_ge(s_sc, g + 1)
                            if h0 is None or k > 0 or slot >= 2:
                                act.wait_ge(s_plo, g - 1)
                            act.activation(p32[:, slot % 2, :], sc_ps[slot % 2].rearrange("p a n -> p (a n)"), ACT.Exp,
                                           scale=SCALE).then_inc(s_exp, 1)
                            if slot == 7:
                                shift_row(n + 1, (k + 1) % NB)

                constants(0, 0)
                query_hi(0, 0)
                query_hi(1, 1)
                act.wait_ge(s_qc, 16)
                constants(1, 1)
                shift_row(0, 0)
                head(0, 0)
                with act.Fori(1, H) as h:
                    head(h, None)
                high(PAIRS * NBLK - 1, 3)
                act.wait_ge(s_utps, NBLK - 1)
                sums(NBLK - 1, 3)
                act.wait_ge(s_qc, 16 * (NBLK + 2))

            @block.vector
            def _(dve):
                def query_lo(n, k):
                    dve.wait_ge(s_qhi, n + 1)
                    dve.tensor_tensor(q_lo[0:KW, k, :], ps[0:KW, 7 - k % 2, :], q_hi[0:KW, k, :].bitcast(F32),
                                      ALU.subtract).then_inc(s_qlo, 1)

                def chunk_max(n, k, c):
                    dve.wait_ge(s_mps, PAIRS * n + c + 1)
                    dve.tensor_reduce(mx[:, k % 2, c // 2, c % 2:c % 2 + 1], ps[:, 4:6, :], AX.XY, ALU.max).then_inc(s_mrd, 1)

                def minus_max(n, k):
                    dve.wait_ge(s_mrd, PAIRS * (n + 1))
                    dve.tensor_reduce(nmx[:, k % 2, :], mx[:, k % 2, :, :], AX.X, ALU.max, negate=True).then_inc(s_nmx, 1)

                def low(g, b4, first=False):
                    dve.wait_ge(s_phi, g + 1)
                    dve.tensor_tensor(p_lo[:, b4, :], p32[:, b4 % 2, :], p_hi[:, b4, :].bitcast(F32),
                                      ALU.subtract).then_inc(s_plo, 1)

                def normalise(n, k, h):
                    dve.wait_ge(s_utps, n + 1)
                    u = ps[:, 6 + k % 2, 0:TPB * C1].rearrange("p (i c) -> p i c", i=TPB)
                    dve.reciprocal(rden[:, :], u[:, :, C]).then_inc(s_rden, 1)
                    dve.wait_ge(s_rden, n + 1)
                    dve.tensor_tensor(ua[:, TPB * k:TPB * (k + 1), bass.ds(h * C, C)], u[:, :, 0:C],
                                      rden[:, :].unsqueeze(2).to_broadcast([P, TPB, C]), ALU.mult).then_inc(s_ut, 1)

                def head(h, h0):
                    for k in range(NB):
                        n = 4 * h + k
                        for slot in range(PAIRS):
                            g = PAIRS * n + slot
                            if slot == 1 and (h0 is None or k >= 2):
                                normalise(n - 2, (k - 2) % NB, h if k >= 2 else h - 1)
                            if slot == 5:
                                query_lo(n + 2, (k + 2) % NB)
                            if slot == 6:
                                minus_max(n + 1, (k + 1) % NB)
                            chunk_max(*chunk_of(h, k, slot))
                            if h0 is None or k > 0 or slot >= 1:
                                low(g - 1, (slot - 1) % 4)

                query_lo(0, 0)
                query_lo(1, 1)
                for c in range(PAIRS):
                    chunk_max(0, 0, c)
                minus_max(0, 0)
                chunk_max(1, 1, 0)
                chunk_max(1, 1, 1)
                head(0, 0)
                with dve.Fori(1, H) as h:
                    head(h, None)
                low(PAIRS * NBLK - 1, 3)
                normalise(NBLK - 2, 2, H - 1)
                normalise(NBLK - 1, 3, H - 1)

        attn.close()

        def sb(name, shape, dt=F32):
            return ctx.enter_context(nc.sbuf_tensor(name, shape, dt))

        hn = sb("hn_rows", [P, NT, D])
        hT = sb("hT_cols", [P, S])
        uaT = sb("uaT", [P, 2, BLK])
        anchors2 = sb("anchors2", [P, P])
        w_a = sb("w_a", [P, H1 * A])
        w_oT = sb("w_oT", [P, HP, D])
        w_v = sb("w_v", [P, H1, D])
        gate0T = sb("gate0T", [P, E])
        mean_col = sb("mean_col", [P, 1])
        iota8 = sb("iota8", [P, E])

        def layernorm(tag, wait_x):
            names = ("st", "mv", "ve", "rstd", "hn", "ps", "hT")
            s = {n: sem(f"s_{tag}_{n}") for n in names}

            def on_vector_stats(dve, b):
                wait_x(dve, b)
                for i in range(TPB):
                    dve.bn_stats(stats[:, b % 2, i, :], X[:, TPB * b + i, :]).then_inc(s["st"], 1)
                for i in range(TPB):
                    dve.wait_ge(s["st"], TPB * b + i + 1)
                    dve.bn_aggr(mv[:, b % 2, i, :], stats[:, b % 2, i, :]).then_inc(s["mv"], 1)

            def on_gpsimd(pool, b):
                pool.wait_ge(s["mv"], TPB * (b + 1))
                if b >= 2:
                    pool.wait_ge(s["hn"], TPB * (b - 1))
                pool.tensor_scalar(vare[:, b % 2, :], mv[:, b % 2, :, 1], EPS, None, ALU.add).then_inc(s["ve"], 1)
                pool.wait_ge(s["ve"], b + 1)
                pool.tensor_tensor(rstd[:, b % 2, :], vare[:, b % 2, :], mhalf[:, :], ALU.pow).then_inc(s["rstd"], 1)

            def on_vector(dve, b):
                dve.wait_ge(s["rstd"], b + 1)
                for i in range(TPB):
                    t = TPB * b + i
                    dve.tensor_scalar(hn[:, t, :], X[:, t, :], mv[:, b % 2, i, 0:1], rstd[:, b % 2, i:i + 1],
                                      ALU.subtract, ALU.mult).then_inc(s["hn"], 1)

            def on_tensor(pe, b, bank):
                pe.wait_ge(s["hn"], TPB * (b + 1))
                for i in range(TPB):
                    last = pe.transpose(ps[:, bank, i * P:(i + 1) * P], hn[:, TPB * b + i, :], ident[:, :])
                last.then_inc(s["ps"], 1)

            def on_scalar(act, b, bank):
                act.wait_ge(s["ps"], b + 1)
                act.copy(hT[:, b * BLK:(b + 1) * BLK], ps[:, bank, :]).then_inc(s["hT"], 1)

            return s, on_vector_stats, on_gpsimd, on_vector, on_tensor, on_scalar

        s_uaT_ps, s_uaT, s_o_ps, s_x1 = sem("s_uaT_ps"), sem("s_uaT"), sem("s_o_ps"), sem("s_x1")
        s_c2, s_an_ps, s_an, s_wa_ps, s_wa2 = sem("s_c2"), sem("s_an_ps"), sem("s_an"), sem("s_wa_ps"), sem("s_wa2")
        s_wv_ps, s_wv, s_g0_ps, s_g0 = sem("s_wv_ps"), sem("s_wv"), sem("s_g0_ps"), sem("s_g0")
        ln0, ln0_stats, ln0_pool, ln0_norm, ln0_pe, ln0_act = layernorm("ln0", lambda dve, b: dve.wait_ge(s_x1, b + 1))
        with nc.Block() as block:
            @block.gpsimd
            def _(pool):
                pool.memset(anchors2[:, :], 0.0).then_inc(s_c2, 1)
                pool.wait_ge(s_c2, 1)
                pool.memset(mean_col[:, :], 1.0 / S).then_inc(s_c2, 1)
                pool.wait_ge(s_c2, 2)
                pool.iota(iota8[:, :], [[1, E]], base=0, channel_multiplier=0,
                          allow_small_or_imprecise_dtypes=True).then_inc(s_c2, 1)
                pool.wait_ge(s_c2, 3)
                for b in range(NB):
                    ln0_pool(pool, b)

            @block.tensor
            def _(pe):
                def out_block(b):
                    if b >= 1:
                        pe.wait_ge(s_uaT, 2 * b)
                    for m in range(2):
                        for i in range(TPB):
                            last = pe.transpose(ps[:, m, i * P:(i + 1) * P], ua[:, TPB * b + i, m * P:(m + 1) * P], ident[:, :])
                        last.then_inc(s_uaT_ps, 1)
                    pe.wait_ge(s_uaT, 2 * (b + 1))
                    if b >= 1:
                        pe.wait_ge(s_x1, b)
                    for i in range(TPB):
                        o = ps[:, 2, i * P:(i + 1) * P]
                        for m in range(2):
                            pe.matmul(o, uaT[:, m, i * P:(i + 1) * P], g_w[:, m, :], start=(m == 0), stop=False)
                        last = pe.matmul(o, ones_row[:, :], g_b[:, :], start=False, stop=True)
                    last.then_inc(s_o_ps, 1)

                out_block(0)
                out_block(1)
                pe.wait_ge(ld_l1a, 16 * 4)
                pe.wait_ge(ld_l0, 16 * 7)
                pe.transpose(ps[0:A, 4, 0:A], anchor[:, :], ident[0:A, 0:A])
                pe.transpose(ps[:, 4, P:P + E], gate0[:, :], ident[0:E, 0:E]).then_inc(s_an_ps, 1)
                for hp in range(HP):
                    last = pe.transpose(ps[:, 5 + hp // 4, (hp % 4) * P:(hp % 4 + 1) * P], w_out[:, hp * P:(hp + 1) * P], ident[:, :])
                last.then_inc(s_an_ps, 1)
                out_block(2)
                ln0_pe(pe, 0, 3)
                out_block(3)
                pe.wait_ge(s_an, 5)
                for half in range(2):
                    for q in range(4):
                        hp = 4 * half + q
                        last = pe.matmul(ps[:, 4 + half, q * P:(q + 1) * P], emb[:, hp, :], anchors2[:, :], start=True, stop=True)
                    last.then_inc(s_wa_ps, 1)
                pe.wait_ge(ln0["hT"], 1)
                ln0_pe(pe, 1, 3)
                for r in range(4):
                    bank = (6, 7, 4, 5)[r]
                    if r >= 2:
                        pe.wait_ge(s_wa2, r - 1)
                    for q in range(4):
                        h = 8 * (r // 2) + 2 * q + r % 2
                        rows = slice((h % 2) * A, (h % 2 + 1) * A)
                        last = pe.matmul(ps[:, bank, q * P:(q + 1) * P], emb[rows, HP + h // 2, :], w_oT[rows, h // 2, :],
                                         start=True, stop=True)
                    last.then_inc(s_wv_ps, 1)
                for b in (2, 3):
                    pe.wait_ge(ln0["hT"], b)
                    ln0_pe(pe, b, 3)

            @block.scalar
            def _(act):
                def out_block(b):
                    for m in range(2):
                        act.wait_ge(s_uaT_ps, 2 * b + m + 1)
                        if b >= 1:
                            act.wait_ge(s_o_ps, b)
                        act.copy(uaT[:, m, :], ps[:, m, :]).then_inc(s_uaT, 1)

                out_block(0)
                out_block(1)
                act.wait_ge(s_an_ps, 1)
                act.wait_ge(s_c2, 1)
                act.copy(anchors2[0:A, 0:A], ps[0:A, 4, 0:A]).then_inc(s_an, 1)
                act.copy(anchors2[A:P, A:P], ps[0:A, 4, 0:A]).then_inc(s_an, 1)
                act.copy(gate0T[:, :], ps[:, 4, P:P + E]).then_inc(s_an, 1)
                act.wait_ge(s_an_ps, 2)
                for m in range(2):
                    act.copy(w_oT[:, 4 * m:4 * (m + 1), :], ps[:, 5 + m, :].rearrange("p (h n) -> p h n", h=4)).then_inc(s_an, 1)
                out_block(2)
                ln0_act(act, 0, 3)
                out_block(3)
                for m in range(2):
                    act.wait_ge(s_wa_ps, m + 1)
                    act.copy(w_a[:, m * BLK:(m + 1) * BLK], ps[:, 4 + m, :]).then_inc(s_wa2, 1)
                ln0_act(act, 1, 3)
                for r in range(4):
                    act.wait_ge(s_wv_ps, r + 1)
                    act.copy(w_v[:, bass.ds(8 * (r // 2) + r % 2, 4, step=2), :], ps[:, (6, 7, 4, 5)[r], :].rearrange("p (h n) -> p h n", h=4)).then_inc(s_wv, 1)
                ln0_act(act, 2, 3)
                ln0_act(act, 3, 3)

            @block.vector
            def _(dve):
                for b in range(NB):
                    dve.wait_ge(s_o_ps, b + 1)
                    xb = X[:, TPB * b:TPB * (b + 1), :]
                    dve.tensor_tensor(xb, ps[:, 2, :].rearrange("p (i n) -> p i n", i=TPB), xb, ALU.add).then_inc(s_x1, 1)
                    ln0_stats(dve, b)
                    ln0_norm(dve, b)

        picks = ctx.enter_context(ExitStack())

        def sb(name, shape, dt=F32):
            return picks.enter_context(nc.sbuf_tensor(name, shape, dt))

        pooled = sb("pooled", [P, 1])
        g8 = sb("g8", [1, 12, E])
        gi = sb("gi", [1, E], U32)
        g1 = sb("g1", [1, 8])
        coef = sb("coef", [P, 4, E])
        pick = sb("pick", [P, E])
        gb = sb("gb", [E, P])
        tmp_d = sb("tmp_d", [P, D, E])
        tmp_u = sb("tmp_u", [P, 2, BN, E])
        tmp_b = sb("tmp_b", [P, E])
        sel_d = sb("sel_d", [P, D])
        sel_u = sb("sel_u", [P, P])
        sel_b = sb("sel_b", [P, 1])
        sel_dT = sb("sel_dT", [P, P])
        sel_uT = sb("sel_uT", [P, D])
        hid0 = sb("hid0", [P, 2, BLK])
        s_pool_ps, s_pooled, s_lg, s_gv, s_ge = sem("s_pool_ps"), sem("s_pooled"), sem("s_lg"), sem("s_gv"), sem("s_ge")
        s_cf_ps, s_cfd, s_sel, s_selT_ps, s_selT = sem("s_cf_ps"), sem("s_cfd"), sem("s_sel"), sem("s_selT_ps"), sem("s_selT")
        s_h0_ps, s_h0, s_y0_ps, s_x2 = sem("s_h0_ps"), sem("s_h0"), sem("s_y0_ps"), sem("s_x2")
        ln1, ln1_stats, ln1_pool, ln1_norm, ln1_pe, ln1_act = layernorm("ln1", lambda dve, b: dve.wait_ge(s_x2, b + 1))
        LOGIT, EXPD, PROB, TOP, IDX, OH0, OH1, CW0, CW1, GW = range(10)
        with nc.Block() as block:
            @block.tensor
            def _(pe):
                for t in range(NT):
                    last = pe.matmul(ps[:, 0, 0:1], hn[:, t, :], mean_col[:, :], start=(t == 0), stop=(t == NT - 1))
                last.then_inc(s_pool_ps, 1)
                pe.wait_ge(s_pooled, 1)
                pe.matmul(ps[0:1, 1, 0:E], pooled[:, :], gate0T[:, :], start=True, stop=True).then_inc(s_lg, 1)
                pe.wait_ge(s_gv, 14)
                pe.matmul(ps[:, 2, 0:4 * E], ones_row[:, :], g8[:, OH0:OH0 + 4, :].rearrange("p a e -> p (a e)"), start=True, stop=True).then_inc(s_cf_ps, 1)
                pe.matmul(ps[0:E, 3, 0:P], g8[:, GW, :], ones_row[:, :], start=True, stop=True).then_inc(s_cf_ps, 1)
                pe.wait_ge(s_sel, 2)
                pe.transpose(ps[:, 4, 0:P], sel_d[:, :], ident[:, :]).then_inc(s_selT_ps, 1)
                pe.wait_ge(s_sel, 4)
                pe.transpose(ps[:, 5, 0:P], sel_u[:, :], ident[:, :]).then_inc(s_selT_ps, 1)
                pe.wait_ge(s_selT, 2)
                for b in range(NB + 1):
                    if b < NB:
                        if b >= 2:
                            pe.wait_ge(s_h0, b - 1)
                        pe.matmul(ps[:, b % 2, :], sel_dT[:, :], hT[:, b * BLK:(b + 1) * BLK], start=True, stop=True).then_inc(s_h0_ps, 1)
                    if b >= 1:
                        pe.wait_ge(s_h0, b)
                        if b >= 2:
                            pe.wait_ge(s_x2, b - 1)
                        for i in range(TPB):
                            o = ps[:, 6, i * P:(i + 1) * P]
                            pe.matmul(o, hid0[:, (b - 1) % 2, i * P:(i + 1) * P], sel_uT[:, :], start=True, stop=False)
                            last = pe.matmul(o, gb[:, :], up0_b[:, :], start=False, stop=True)
                        last.then_inc(s_y0_ps, 1)
                for b in range(NB):
                    if b >= 1:
                        pe.wait_ge(ln1["hT"], b)
                    ln1_pe(pe, b, 7)

            @block.scalar
            def _(act):
                act.wait_ge(s_pool_ps, 1)
                act.copy(pooled[:, :], ps[:, 0, 0:1]).then_inc(s_pooled, 1)
                act.wait_ge(s_gv, 1)
                act.activation(g8[:, EXPD, :], ps[0:1, 1, 0:E], ACT.Exp, bias=g1[:, 0:1], accum_out=g1[:, 1:2]).then_inc(s_ge, 1)
                act.wait_ge(s_cf_ps, 1)
                act.copy(coef[:, :, :], ps[:, 2, 0:4 * E].rearrange("p (a e) -> p a e", a=4)).then_inc(s_cfd, 1)
                act.copy(pick[0:BN, :], ps[0:BN, 2, 0:E]).then_inc(s_cfd, 1)
                act.copy(pick[BN:P, :], ps[BN:P, 2, E:2 * E]).then_inc(s_cfd, 1)
                act.wait_ge(s_cf_ps, 2)
                act.copy(gb[:, :], ps[0:E, 3, 0:P]).then_inc(s_cfd, 1)
                act.wait_ge(s_selT_ps, 1)
                act.copy(sel_dT[:, :], ps[:, 4, 0:P]).then_inc(s_selT, 1)
                act.wait_ge(s_selT_ps, 2)
                act.copy(sel_uT[:, :], ps[:, 5, 0:P]).then_inc(s_selT, 1)
                act.wait_ge(s_sel, 6)
                for b in range(NB):
                    act.wait_ge(s_h0_ps, b + 1)
                    if b >= 2:
                        act.wait_ge(s_y0_ps, b - 1)
                    act.activation(hid0[:, b % 2, :], ps[:, b % 2, :], ACT.Gelu, bias=sel_b[:, :]).then_inc(s_h0, 1)
                for b in range(NB):
                    ln1_act(act, b, 7)

            @block.gpsimd
            def _(pool):
                for b in range(NB):
                    ln1_pool(pool, b)

            @block.vector
            def _(dve):
                done = [0]

                def step(ins):
                    ins.then_inc(s_gv, 1)
                    done[0] += 1
                    dve.wait_ge(s_gv, done[0])

                dve.wait_ge(s_lg, 1)
                step(dve.tensor_reduce(g1[:, 0:1], ps[0:1, 1, 0:E], AX.X, ALU.max, negate=True))
                dve.wait_ge(s_ge, 1)
                step(dve.reciprocal(g1[:, 2:3], g1[:, 1:2]))
                step(dve.tensor_scalar(g8[:, PROB, :], g8[:, EXPD, :], g1[:, 2:3], None, ALU.mult))
                step(dve.max(g8[:, TOP, :], g8[:, PROB, :]))
                step(dve.max_index(gi[:, :], g8[:, TOP, :], g8[:, PROB, :]))
                step(dve.tensor_copy(g8[:, IDX, :], gi[:, :]))
                step(dve.tensor_scalar(g8[:, OH0, :], iota8[0:1, :], g8[:, IDX, 0:1], None, ALU.is_equal))
                step(dve.tensor_scalar(g8[:, OH1, :], iota8[0:1, :], g8[:, IDX, 1:2], None, ALU.is_equal))
                step(dve.tensor_scalar(g1[:, 3:4], g8[:, TOP, 0:1], g8[:, TOP, 1:2], 1e-8, ALU.add, ALU.add))
                step(dve.reciprocal(g1[:, 4:5], g1[:, 3:4]))
                step(dve.tensor_scalar(g1[:, 5:7], g8[:, TOP, 0:2], g1[:, 4:5], None, ALU.mult))
                step(dve.tensor_scalar(g8[:, CW0, :], g8[:, OH0, :], g1[:, 5:6], None, ALU.mult))
                step(dve.tensor_scalar(g8[:, CW1, :], g8[:, OH1, :], g1[:, 6:7], None, ALU.mult))
                step(dve.tensor_tensor(g8[:, GW, :], g8[:, CW0, :], g8[:, CW1, :], ALU.add))
                dve.wait_ge(s_cfd, 3)
                dve.tensor_tensor(tmp_d[:, :, :], down0[:, :, :].rearrange("p e d -> p d e"),
                                  pick[:, :].unsqueeze(1).to_broadcast([P, D, E]), ALU.mult).then_inc(s_sel, 1)
                dve.wait_ge(s_sel, 1)
                dve.tensor_reduce(sel_d[:, :], tmp_d[:, :, :], AX.X, ALU.add).then_inc(s_sel, 1)
                dve.tensor_tensor(tmp_u[:, :, :, :], up0[:, :, :].rearrange("p e c -> p c e").unsqueeze(1).to_broadcast([P, 2, BN, E]),
                                  coef[:, 2:4, :].unsqueeze(2).to_broadcast([P, 2, BN, E]), ALU.mult).then_inc(s_sel, 1)
                dve.wait_ge(s_sel, 3)
                dve.tensor_reduce(sel_u[:, :].rearrange("p (k c) -> p k c", k=2), tmp_u[:, :, :, :], AX.X, ALU.add).then_inc(s_sel, 1)
                dve.tensor_tensor(tmp_b[:, :], down0_b[:, :], pick[:, :], ALU.mult).then_inc(s_sel, 1)
                dve.wait_ge(s_sel, 5)
                dve.tensor_reduce(sel_b[:, :], tmp_b[:, :], AX.X, ALU.add).then_inc(s_sel, 1)
                for b in range(NB):
                    dve.wait_ge(s_y0_ps, b + 1)
                    xb = X[:, TPB * b:TPB * (b + 1), :]
                    dve.tensor_tensor(xb, ps[:, 6, :].rearrange("p (i n) -> p i n", i=TPB), xb, ALU.add).then_inc(s_x2, 1)
                    ln1_stats(dve, b)
                    if b == 0:
                        dve.wait_ge(s_h0_ps, NB)
                    ln1_norm(dve, b)

        picks.close()
        late = ctx.enter_context(ExitStack())

        def sb(name, shape, dt=F32):
            return late.enter_context(nc.sbuf_tensor(name, shape, dt))

        pT = sb("pT", [P, HP, S])
        cen = sb("cen", [P, 2, H1, A])
        prb = sb("prb", [P, 2, H1, A])
        nrm = sb("nrm", [P, 3, H1, A])
        tmax = sb("tmax", [P, 2, H1])
        tsum = sb("tsum", [P, 2, H1])
        trec = sb("trec", [P, 2, H1])
        ones_col = sb("ones_col", [P, 1])
        yT = sb("yT", [P, H1 * A])
        zz = sb("zz", [P, HP, D])
        asum = sb("asum", [P, 4, HP])
        SCALE1 = float(A) ** -0.5
        FMAX = 3.4028234663852886e38
        s_ls, s_tm, s_cen, s_pr = sem("s_ls"), sem("s_tm"), sem("s_cen"), sem("s_pr")
        s_ts, s_tr, s_nr, s_y_ps, s_pT_ps, s_pT = sem("s_ts"), sem("s_tr"), sem("s_nr"), sem("s_y_ps"), sem("s_pT_ps"), sem("s_pT")
        s_yT, s_as, s_z_ps, s_z, s_o1_ps, s_x3, s_oc = sem("s_yT"), sem("s_as"), sem("s_z_ps"), sem("s_z"), sem("s_o1_ps"), sem("s_x3"), sem("s_oc")
        ln2, ln2_stats, ln2_pool, ln2_norm, ln2_pe, ln2_act = layernorm("ln2", lambda dve, b: dve.wait_ge(s_x3, b + 1))
        with nc.Block() as block:
            @block.tensor
            def _(pe):
                pe.wait_ge(s_oc, 1)
                for t in range(NT + 2):
                    if t < NT:
                        if t >= 2:
                            pe.wait_ge(s_cen, t - 1)
                        for m in range(2):
                            last = pe.matmul(ps[:, 2 * (t % 2) + m, :], hT[:, t * P:(t + 1) * P], w_a[:, m * BLK:(m + 1) * BLK],
                                             start=True, stop=True)
                        last.then_inc(s_ls, 1)
                    if t >= 2:
                        u = t - 2
                        pe.wait_ge(s_nr, u + 1)
                        pu = nrm[:, u % 3, :, :].rearrange("p h a -> p (h a)")
                        for m in range(2):
                            if 2 * u + m >= 1:
                                pe.wait_ge(s_pT, 2 * u + m)
                            for q in range(4):
                                c0 = (4 * m + q) * P
                                last = pe.transpose(ps[:, 6, q * P:(q + 1) * P], pu[:, c0:c0 + P], ident[:, :])
                            last.then_inc(s_pT_ps, 1)
                            pe.matmul(ps[:, 4 + m, :], hn[:, u, :], pu[:, m * BLK:(m + 1) * BLK], start=(u == 0),
                                      stop=(u == NT - 1))
                            for q in range(4):
                                hp = 4 * m + q
                                last = pe.matmul(ps[:, 7, hp:hp + 1], pu[:, hp * P:(hp + 1) * P], ones_col[:, :],
                                                 start=(u == 0 and hp == 0), stop=(u == NT - 1), skip_group_check=True)
                        last.then_inc(s_y_ps, 1)
                pe.wait_ge(s_yT, 2)
                for h in range(H1):
                    rows = slice((h % 2) * A, (h % 2 + 1) * A)
                    hp = h // 2
                    last = pe.matmul(ps[rows, hp // 4, (hp % 4) * P:(hp % 4 + 1) * P], yT[:, h * A:(h + 1) * A], w_v[:, h, :],
                                     start=True, stop=True)
                last.then_inc(s_z_ps, 1)
                pe.wait_ge(s_z, 2)
                for b in range(NB):
                    if b >= 2:
                        pe.wait_ge(s_x3, b - 1)
                    for i in range(TPB):
                        o = ps[:, 2 + b % 2, i * P:(i + 1) * P]
                        for hp in range(HP):
                            pe.matmul(o, pT[:, hp, b * BLK + i * P:b * BLK + (i + 1) * P], zz[:, hp, :], start=(hp == 0), stop=False)
                        last = pe.matmul(o, ones_row[:, :], b_out[:, :], start=False, stop=True)
                    last.then_inc(s_o1_ps, 1)
                    if b >= 1:
                        if b >= 2:
                            pe.wait_ge(ln2["hT"], b - 1)
                        ln2_pe(pe, b - 1, 5)
                pe.wait_ge(ln2["hT"], 3)
                ln2_pe(pe, 3, 5)

            @block.scalar
            def _(act):
                for t in range(NT + 2):
                    if t < NT:
                        act.wait_ge(s_cen, t + 1)
                        if t >= 2:
                            act.wait_ge(s_nr, t - 1)
                        act.activation(prb[:, t % 2, :, :], cen[:, t % 2, :, :], ACT.Exp, scale=SCALE1).then_inc(s_pr, 1)
                    if t >= 2:
                        u = t - 2
                        for m in range(2):
                            act.wait_ge(s_pT_ps, 2 * u + m + 1)
                            act.copy(pT[:, 4 * m:4 * (m + 1), u * P:(u + 1) * P],
                                     ps[:, 6, :].rearrange("p (h s) -> p h s", h=4)).then_inc(s_pT, 1)
                act.wait_ge(s_y_ps, NT)
                for m in range(2):
                    act.copy(yT[:, m * BLK:(m + 1) * BLK], ps[:, 4 + m, :]).then_inc(s_yT, 1)
                for b in range(NB):
                    ln2_act(act, b, 5)

            @block.gpsimd
            def _(pool):
                pool.memset(ones_col[:, :], 1.0).then_inc(s_oc, 1)
                pool.wait_ge(s_oc, 1)
                for t in range(NT):
                    pool.wait_ge(s_tr, t + 1)
                    if t >= 3:
                        pool.wait_ge(s_y_ps, t - 2)
                    pool.tensor_tensor(nrm[:, t % 3, :, :], prb[:, t % 2, :, :],
                                       trec[:, t % 2, :].unsqueeze(2).to_broadcast([P, H1, A]), ALU.mult).then_inc(s_nr, 1)
                for b in range(NB):
                    ln2_pool(pool, b)

            @block.vector
            def _(dve):
                for t in range(NT + 1):
                    if t < NT:
                        sc = ps[:, 2 * (t % 2):2 * (t % 2) + 2, :].rearrange("p m (h a) -> p (m h) a", a=A)
                        dve.wait_ge(s_ls, t + 1)
                        dve.tensor_reduce(tmax[:, t % 2, :], sc, AX.X, ALU.max).then_inc(s_tm, 1)
                        dve.wait_ge(s_tm, t + 1)
                        if t >= 2:
                            dve.wait_ge(s_pr, t - 1)
                        dve.tensor_tensor(cen[:, t % 2, :, :], sc, tmax[:, t % 2, :].unsqueeze(2).to_broadcast([P, H1, A]),
                                          ALU.subtract).then_inc(s_cen, 1)
                    if t >= 1:
                        u = t - 1
                        dve.wait_ge(s_pr, u + 1)
                        dve.tensor_reduce(tsum[:, u % 2, :], prb[:, u % 2, :, :], AX.X, ALU.add).then_inc(s_ts, 1)
                        dve.wait_ge(s_ts, u + 1)
                        if u >= 2:
                            dve.wait_ge(s_nr, u - 1)
                        dve.reciprocal(trec[:, u % 2, :], tsum[:, u % 2, :]).then_inc(s_tr, 1)
                dve.wait_ge(s_y_ps, NT)
                dve.tensor_copy(asum[:, 0, :], ps[:, 7, 0:HP]).then_inc(s_as, 1)
                dve.wait_ge(s_as, 1)
                dve.reciprocal(asum[:, 1, :], asum[:, 0, :]).then_inc(s_as, 1)
                dve.wait_ge(s_as, 2)
                dve.tensor_scalar(asum[:, 2, :], asum[:, 1, :], FMAX, None, ALU.is_le).then_inc(s_as, 1)
                dve.wait_ge(s_as, 3)
                dve.scalar_tensor_tensor(out=asum[:, 3, :], in0=asum[:, 1, :], scalar=FMAX, in1=asum[:, 2, :],
                                         op0=ALU.min, op1=ALU.mult).then_inc(s_as, 1)
                dve.wait_ge(s_as, 4)
                dve.wait_ge(s_z_ps, 1)
                for m in range(2):
                    dve.tensor_tensor(zz[:, 4 * m:4 * (m + 1), :], ps[:, m, :].rearrange("p (h n) -> p h n", h=4),
                                      asum[:, 3, 4 * m:4 * (m + 1)].unsqueeze(2).to_broadcast([P, 4, D]), ALU.mult).then_inc(s_z, 1)
                for b in range(NB):
                    dve.wait_ge(s_o1_ps, b + 1)
                    xb = X[:, TPB * b:TPB * (b + 1), :]
                    dve.tensor_tensor(xb, ps[:, 2 + b % 2, :].rearrange("p (i n) -> p i n", i=TPB), xb, ALU.add).then_inc(s_x3, 1)
                    ln2_stats(dve, b)
                    ln2_norm(dve, b)
        late.close()

        def sb(name, shape, dt=F32):
            return ctx.enter_context(nc.sbuf_tensor(name, shape, dt))

        sc1 = sb("sc1", [P, NT, E])
        top1 = sb("top1", [P, NT, E])
        idx1 = sb("idx1", [P, NT, E], U32)
        idf1 = sb("idf1", [P, NT, E])
        pd = sb("pd", [P, 4, NT])
        eq = sb("eq", [P, 4, NT, E])
        gw = sb("gw", [P, NT, E])
        gT = sb("gT", [40, S], F32R)
        gTf = sb("gTf", [E, S])
        spread_f = sb("spread_f", [40, E, M1])
        spread = sb("spread", [40, E, M1], F32R)
        act_g = sb("act_g", [P, 2, BLK])
        prod = sb("prod", [P, 2, BLK])
        hid = sb("hid", [P, 2, BLK])
        s_gtl, s_sc1, s_d1, s_e1, s_gt_ps, s_gt, s_sp = sem("s_gtl"), sem("s_sc1"), sem("s_d1"), sem("s_e1"), sem("s_gt_ps"), sem("s_gt"), sem("s_sp")
        s_gp, s_up, s_bp, s_sil, s_pr1, s_hid, s_dn, s_x4, s_out = (sem(n) for n in ("s_gp", "s_up", "s_bp", "s_sil", "s_pr1", "s_hid", "s_dn", "s_x4", "s_out"))
        w_gf, w_uf, sp_f = (w[:, :, :].rearrange("p e m -> p (e m)") for w in (w_g, w_u, spread))
        NS = NB * CH
        with nc.Block() as block:
            @block.gpsimd
            def _(pool):
                pool.memset(spread_f[:, :, :], 1.0).then_inc(s_sp, 1)
                pool.wait_ge(s_sp, 1)
                for n, r in enumerate((0, 32)):
                    v = spread_f[r:r + (32 if r == 0 else E), :, :]
                    pool.affine_select(out=v, in_=v, compare_op=ALU.is_equal, fill=0.0, base=0,
                                       pattern=[[-1, E], [0, M1]], channel_multiplier=1).then_inc(s_sp, 1)
                    pool.wait_ge(s_sp, 2 + n)
                pool.tensor_copy(spread[:, :, :], spread_f[:, :, :]).then_inc(s_sp, 1)
                pool.wait_ge(s_sp, 4)
                pool.memset(gT[:, :].bitcast(F32), 0.0).then_inc(s_sp, 1)

            @block.tensor
            def _(pe):
                pe.wait_ge(ld_l1f, 16 * 4)
                for t in range(NT):
                    last = pe.matmul(ps[:, 0, t * E:(t + 1) * E], hT[:, t * P:(t + 1) * P], gate1[:, :], start=True, stop=True)
                last.then_inc(s_sc1, 1)
                pe.wait_ge(s_d1, 12)
                for b in range(NB):
                    for i in range(TPB):
                        last = pe.transpose(ps[0:E, 1 + b, i * P:(i + 1) * P], gw[:, TPB * b + i, :], ident[:, :])
                    last.then_inc(s_gt_ps, 1)
                pe.wait_ge(s_sp, 5)
                pe.wait_ge(s_gtl, NB)
                for n in range(NS + 1):
                    if n < NS:
                        b, c = n // CH, n % CH
                        cols = slice(b * BLK, (b + 1) * BLK)
                        if n >= 2:
                            pe.wait_ge(s_sil, n - 1)
                        pe.matmul(ps[:, n % 2, :], w_gf[:, c * P:(c + 1) * P], hT[:, cols], start=True, stop=True).then_inc(s_gp, 1)
                        if n >= 2:
                            pe.wait_ge(s_pr1, n - 1)
                        pe.matmul(ps[:, 2 + n % 2, :], w_uf[:, c * P:(c + 1) * P], hT[:, cols], start=True, stop=True).then_inc(s_up, 1)
                        if n >= 2:
                            pe.wait_ge(s_hid, n - 1)
                        pe.matmul(ps[:, 4 + n % 2, :], sp_f[:, c * P:(c + 1) * P], gT[:, cols], start=True, stop=True).then_inc(s_bp, 1)
                    if n >= 1:
                        b, c = (n - 1) // CH, (n - 1) % CH
                        pe.wait_ge(s_hid, n)
                        if c == 0 and b >= 2:
                            pe.wait_ge(s_x4, b - 1)
                        for i in range(TPB):
                            last = pe.matmul(ps[:, 6 + b % 2, i * P:(i + 1) * P], hid[:, (n - 1) % 2, i * P:(i + 1) * P], w_d[:, c, :],
                                             start=(c == 0 and i == 0), stop=(c == CH - 1), skip_group_check=True)
                        last.then_inc(s_dn, 1)

            @block.scalar
            def _(act):
                act.wait_ge(s_sc1, 1)
                act.copy(sc1[:, :, :], ps[:, 0, 0:NT * E].rearrange("p (t e) -> p t e", t=NT)).then_inc(s_e1, 1)
                act.wait_ge(s_d1, 4)
                act.activation(pd[:, 1, :], pd[:, 0, :], ACT.Exp).then_inc(s_e1, 1)
                act.wait_ge(s_sp, 5)
                for b in range(NB):
                    cols = slice(b * BLK, (b + 1) * BLK)
                    act.wait_ge(s_gt_ps, b + 1)
                    act.copy(gTf[:, cols], ps[0:E, 1 + b, :]).then_inc(s_gt, 1)
                    act.copy(gT[0:E, cols], ps[0:E, 1 + b, :]).then_inc(s_gt, 1)
                for n in range(NS):
                    act.wait_ge(s_gp, n + 1)
                    if n >= 2:
                        act.wait_ge(s_pr1, n - 1)
                    act.activation(act_g[:, n % 2, :], ps[:, n % 2, :], ACT.Silu).then_inc(s_sil, 1)

            @block.vector
            def _(dve):
                done = [0]

                def step(ins):
                    ins.then_inc(s_d1, 1)
                    done[0] += 1
                    dve.wait_ge(s_d1, done[0])

                dve.wait_ge(s_e1, 1)
                for t in range(NT):
                    last = dve.max(top1[:, t, :], sc1[:, t, :])
                step(last)
                for t in range(NT):
                    last = dve.max_index(idx1[:, t, :], top1[:, t, :], sc1[:, t, :])
                step(last)
                step(dve.tensor_copy(idf1[:, :, :], idx1[:, :, :]))
                step(dve.tensor_tensor(pd[:, 0, :], top1[:, :, 1], top1[:, :, 0], ALU.subtract))
                dve.wait_ge(s_e1, 2)
                step(dve.tensor_scalar(pd[:, 2, :], pd[:, 1, :], 1.0, None, ALU.add))
                step(dve.reciprocal(pd[:, 3, :], pd[:, 2, :]))
                step(dve.tensor_tensor(pd[:, 2, :], pd[:, 1, :], pd[:, 3, :], ALU.mult))
                io = iota8[:, :].unsqueeze(1).to_broadcast([P, NT, E])
                for k, p in ((0, 3), (1, 2)):
                    step(dve.tensor_tensor(eq[:, k, :, :], io, idf1[:, :, k:k + 1].to_broadcast([P, NT, E]), ALU.is_equal))
                    step(dve.tensor_tensor(eq[:, 2 + k, :, :], eq[:, k, :, :], pd[:, p, :].unsqueeze(2).to_broadcast([P, NT, E]), ALU.mult))
                step(dve.tensor_tensor(gw[:, :, :], eq[:, 2, :, :], eq[:, 3, :, :], ALU.add))
                for b in range(NB):
                    cols = slice(b * BLK, (b + 1) * BLK)
                    dve.wait_ge(s_gt, 2 * (b + 1))
                    dve.tensor_tensor(gT[32:32 + E, cols], gTf[:, cols], gT[0:E, cols].bitcast(F32), ALU.subtract).then_inc(s_gtl, 1)
                for n in range(NS):
                    b, c = n // CH, n % CH
                    dve.wait_ge(s_up, n + 1)
                    dve.wait_ge(s_sil, n + 1)
                    if n >= 2:
                        dve.wait_ge(s_hid, n - 1)
                    dve.tensor_tensor(prod[:, n % 2, :], ps[:, 2 + n % 2, :], act_g[:, n % 2, :], ALU.mult).then_inc(s_pr1, 1)
                    dve.wait_ge(s_pr1, n + 1)
                    dve.wait_ge(s_bp, n + 1)
                    if n >= 2:
                        dve.wait_ge(s_dn, n - 1)
                    dve.tensor_tensor(hid[:, n % 2, :], ps[:, 4 + n % 2, :], prod[:, n % 2, :], ALU.mult).then_inc(s_hid, 1)
                    if c == 1 and b >= 1 or n == NS - 1:
                        o = b if n == NS - 1 else b - 1
                        dve.wait_ge(s_dn, CH * (o + 1))
                        xb = X[:, TPB * o:TPB * (o + 1), :]
                        dve.tensor_tensor(xb, ps[:, 6 + o % 2, :].rearrange("p (i n) -> p i n", i=TPB), xb, ALU.add).then_inc(s_x4, 1)

            @block.sync
            def _(sp):
                out_v = out.rearrange("a (t p) d -> p (a t) d", p=P)
                for b in range(NB):
                    sp.wait_ge(s_x4, b + 1)
                    sp.dma_start(out_v[:, TPB * b:TPB * (b + 1), :], X[:, TPB * b:TPB * (b + 1), :]).then_inc(s_out, 16)
                sp.wait_ge(s_out, 16 * NB)


_INS = ['L0_attn_h_t', 'L0_attn_W_DQ', 'L0_attn_b_DQ', 'L0_attn_W_UQ', 'L0_attn_b_UQ', 'L0_attn_W_DKV',
        'L0_attn_b_DKV', 'L0_attn_W_UK', 'L0_attn_b_UK', 'L0_attn_W_UV', 'L0_attn_b_UV', 'L0_attn_W_QR',
        'L0_attn_b_QR', 'L0_attn_W_KR', 'L0_attn_b_KR', 'L0_attn_W_O', 'L0_attn_b_O', 'L0_ffn_gate_w',
        'L0_ffn_down_w', 'L0_ffn_down_b', 'L0_ffn_up_w', 'L0_ffn_up_b', 'L1_attn_W_emb', 'L1_attn_W_anchor',
        'L1_attn_W_out', 'L1_attn_b_out', 'L1_ffn_w_gate', 'L1_ffn_w_g', 'L1_ffn_w_u', 'L1_ffn_w_d']
_OUTS = [((1, 2048, 128), 'float32')]


def kernel(**inputs):
    import numpy as _np
    import concourse.bacc as _bacc
    from concourse import mybir as _mybir
    from concourse.bass_utils import run_bass_kernel_spmd as _run

    nc = _bacc.Bacc("TRN2", target_bir_lowering=False, num_devices=1)
    arrays, tensors = {}, {}
    for name in _INS:
        a = _np.ascontiguousarray(inputs[name])
        arrays[f"in_{name}_dram"] = a
        tensors[name] = nc.dram_tensor(f"in_{name}_dram", a.shape, _mybir.dt.from_np(a.dtype), kind="ExternalInput").ap()
    outs = []
    for i, (shape, dtype) in enumerate(_OUTS):
        dt = _mybir.dt.from_np(_np.dtype(dtype))
        outs.append(nc.dram_tensor(f"out_{i}_dram", shape, dt, kind="ExternalOutput").ap())
    build_kernel(nc, tensors, outs[0])
    r = _run(nc, [arrays], core_ids=[0])
    got = tuple(r.results[0][f"out_{i}_dram"] for i in range(len(_OUTS)))
    return got[0]
```

```python
from contextlib import ExitStack

import concourse.bass as bass
from concourse import mybir

ALU = mybir.AluOpType
ACT = mybir.ActivationFunctionType
AX = mybir.AxisListType
F32 = mybir.dt.float32
F32R = mybir.dt.float32r
U32 = mybir.dt.uint32

P = 128
BLK = 512
TPB = BLK // P
EPS = 1e-5


def build_kernel(nc, d, out):
    S, D = d["L0_attn_h_t"].shape[1:]
    NT = S // P
    NB = S // BLK
    C = d["L0_attn_W_DQ"].shape[1]
    H = d["L0_attn_W_QR"].shape[1] // C
    DK = d["L0_attn_W_UQ"].shape[1] // H
    C1 = C + 1
    KW = 2 * C
    SCALE = float(DK + C) ** -0.5
    assert D == P and DK == P and NT == 16 and H == 8 and C == 32

    ctx = ExitStack()
    with ctx:
        def sb(name, shape, dt=F32):
            return ctx.enter_context(nc.sbuf_tensor(name, shape, dt))

        def sem(name):
            return ctx.enter_context(nc.semaphore(name))

        ps = ctx.enter_context(nc.psum_tensor("ps", [P, 8, BLK], F32))

        X = sb("X", [P, NT, D])
        ident = sb("ident", [P, P])
        ones_row = sb("ones_row", [1, P])
        mhalf = sb("mhalf", [P, TPB])

        E = d["L0_ffn_gate_w"].shape[0]
        BN = d["L0_ffn_down_w"].shape[1]
        A = d["L1_attn_W_anchor"].shape[0]
        H1 = d["L1_attn_W_out"].shape[1] // A
        HP = H1 // 2
        M1 = d["L1_ffn_w_g"].shape[2]
        CH = E * M1 // P
        assert E == 8 and 2 * BN == P and 2 * A == P and E * M1 == CH * P
        gate0 = sb("gate0", [E, D])
        down0 = sb("down0", [P, E, D])
        down0_b = sb("down0_b", [P, E])
        up0 = sb("up0", [P, E, BN])
        up0_b = sb("up0_b", [E, D])
        emb = sb("emb", [P, 2 * HP, D])
        anchor = sb("anchor", [A, A])
        w_out = sb("w_out", [P, H1 * A])
        b_out = sb("b_out", [1, D])
        gate1 = sb("gate1", [P, E])
        g_w = sb("g_w", [P, 2, D])
        g_b = sb("g_b", [1, D])
        stats = sb("stats", [P, 2, TPB, 6])
        mv = sb("mv", [P, 2, TPB, 2])
        rstd = sb("rstd", [P, 2, TPB])
        vare = sb("vare", [P, 2, TPB])
        ua = sb("ua", [P, NT, H * C])
        ld_l0, ld_l1a, ld_l1f = sem("ld_l0"), sem("ld_l1a"), sem("ld_l1f")

        attn = ctx.enter_context(ExitStack())

        def sb(name, shape, dt=F32, stack=attn):
            return stack.enter_context(nc.sbuf_tensor(name, shape, dt))

        wa_hi = sb("wa_hi", [P, H + 1, P], F32R)
        wa_lo = sb("wa_lo", [P, H + 1, P], F32R)
        fold = sb("fold", [2 * C + 1, C1])
        key1 = sb("key1", [P, S], F32R)
        key2 = sb("key2", [P, S], F32R)
        cq = sb("cq", [P, S], F32R)
        val = sb("val", [P, NT, 2 * C + 1], F32R)
        w_head = sb("w_head", [P, 2, P], F32R)
        q_hi = sb("q_hi", [P, NB, BLK], F32R)
        q_lo = sb("q_lo", [P, NB, BLK], F32R)

        folding = ctx.enter_context(ExitStack())

        def sb(name, shape, dt=F32, stack=folding):
            return stack.enter_context(nc.sbuf_tensor(name, shape, dt))

        w_dq = sb("w_dq", [P, C])
        w_kk = sb("w_kk", [P, KW])
        b_q = sb("b_q", [C, 1])
        b_kk = sb("b_kk", [KW, 1])
        b_v = sb("b_v", [P, C])
        uq = sb("uq", [C1, H * DK])
        uk = sb("uk", [C1, H * DK])
        uv = sb("uv", [C1, H * DK])
        qr = sb("qr", [C1, H, C])
        w_o = sb("w_o", [P, H, D])
        b_o = sb("b_o", [1, D])
        uqT = sb("uqT", [P, H, C1])
        ukT = sb("ukT", [P, H, C1])
        uvT = sb("uvT", [P, H, C1])
        wa = sb("wa", [P, H + 1, P])
        va = sb("va", [P, H + 1])
        va_hi = sb("va_hi", [P, H + 1], F32R)
        va_lo = sb("va_lo", [P, H + 1], F32R)
        hn = sb("hn", [P, 2, TPB, D])
        hT = sb("hT", [P, 2, BLK])
        k_f = sb("k_f", [KW, 2, BLK])
        c_f = sb("c_f", [C, 2, BLK])
        v_f = sb("v_f", [P, 2, TPB, C])
        sq = sb("sq", [H + 1, S], F32R)
        sq_dram = nc.dram_tensor("sq_dram", [(H + 1) * S], F32)
        sq_flat = sq_dram.ap().rearrange("(a n) -> a n", a=1)

        ld_x = [sem(f"ld_x{b}") for b in range(NB)]
        ld_w = sem("ld_w")
        s_const = sem("s_const")
        s_zero = sem("s_zero")

        s_wT_ps, s_wT = sem("s_wT_ps"), sem("s_wT")
        s_a_ps, s_a = sem("s_a_ps"), sem("s_a")
        s_wa, s_wah, s_wal = sem("s_wa"), sem("s_wah"), sem("s_wal")
        s_g_ps, s_g = sem("s_g_ps"), sem("s_g")
        s_st, s_mv, s_ve, s_rstd, s_hn = sem("s_st"), sem("s_mv"), sem("s_ve"), sem("s_rstd"), sem("s_hn")
        s_hT_ps, s_hT = sem("s_hT_ps"), sem("s_hT")
        s_proj, s_kf, s_cf, s_vf = sem("s_proj"), sem("s_kf"), sem("s_cf"), sem("s_vf")
        s_khi, s_chi, s_vhi, s_split, s_k2 = sem("s_khi"), sem("s_chi"), sem("s_vhi"), sem("s_split"), sem("s_k2")
        s_sq_ps, s_sqe, s_sqd = sem("s_sq_ps"), sem("s_sqe"), sem("s_sqd")

        HD = H * DK

        with nc.Block() as block:
            @block.sync
            def _(sp):
                x_v = d["L0_attn_h_t"].rearrange("a (t p) d -> p (a t) d", p=P)
                for b in range(NB):
                    sp.dma_start(X[:, b * TPB:(b + 1) * TPB, :], x_v[:, b * TPB:(b + 1) * TPB, :]).then_inc(ld_x[b], 16)
                for r in (0, BN):
                    sp.dma_start(down0[r:r + BN, :, :], d["L0_ffn_down_w"].rearrange("e c d -> c e d")).then_inc(ld_l0, 16)
                    with nc.allow_non_contiguous_dma("8 x 64 words"):
                        sp.dma_start(down0_b[r:r + BN, :], d["L0_ffn_down_b"].rearrange("e c -> c e")).then_inc(ld_l0, 16)
                sp.dma_start(gate0[:, :], d["L0_ffn_gate_w"]).then_inc(ld_l0, 16)
                sp.dma_start(up0[:, :, :], d["L0_ffn_up_w"].rearrange("e d c -> d e c")).then_inc(ld_l0, 16)
                sp.dma_start(up0_b[:, :], d["L0_ffn_up_b"]).then_inc(ld_l0, 16)
                sp.dma_start(emb[:, :, :], d["L1_attn_W_emb"].rearrange("(t p) d -> p t d", p=P)).then_inc(ld_l1a, 16)
                sp.dma_start(anchor[:, :], d["L1_attn_W_anchor"]).then_inc(ld_l1a, 16)
                sp.dma_start(w_out[:, :], d["L1_attn_W_out"]).then_inc(ld_l1a, 16)
                sp.dma_start(b_out[:, :], d["L1_attn_b_out"].rearrange("(a n) -> a n", a=1)).then_inc(ld_l1a, 16)
                sp.wait_ge(s_sqe, NB)
                sp.dma_start(sq_dram.ap().rearrange("(h s) -> h s", h=H + 1), sq[:, :].bitcast(F32)).then_inc(s_sqd, 16)
                sp.wait_ge(s_sqd, 16)

            @block.scalar
            def _(act):
                def load(dst, src):
                    act.dma_start(dst, src).then_inc(ld_w, 16)

                def row(name):
                    return d[name].rearrange("(a n) -> a n", a=1)

                def col(name):
                    return d[name].rearrange("(n a) -> n a", a=1)

                for t, name in ((uq, "UQ"), (uk, "UK"), (uv, "UV")):
                    load(t[0:C, :], d[f"L0_attn_W_{name}"])
                    load(t[C:C1, :], row(f"L0_attn_b_{name}"))
                load(qr[0:C, :, :], d["L0_attn_W_QR"].rearrange("c (h r) -> c h r", h=H))
                load(qr[C:C1, :, :], d["L0_attn_b_QR"].rearrange("(a h r) -> a h r", a=1, h=H))
                load(w_dq[:, :], d["L0_attn_W_DQ"])
                load(w_kk[:, 0:C], d["L0_attn_W_DKV"])
                load(w_kk[:, C:KW], d["L0_attn_W_KR"])
                load(b_q[:, :], col("L0_attn_b_DQ"))
                load(b_kk[0:C, :], col("L0_attn_b_DKV"))
                load(b_kk[C:KW, :], col("L0_attn_b_KR"))
                load(b_v[:, :], row("L0_attn_b_DKV").to_broadcast([P, C]))
                load(w_o[:, :, :], d["L0_attn_W_O"].rearrange("(h k) n -> k h n", h=H))
                load(b_o[:, :], row("L0_attn_b_O"))

                act.wait_ge(s_wT_ps, 3)
                act.copy(uqT[:, :, :], ps[:, 0, 0:H * C1].rearrange("p (h c) -> p h c", h=H)).then_inc(s_wT, 1)
                act.copy(ukT[:, :, :], ps[:, 1, 0:H * C1].rearrange("p (h c) -> p h c", h=H)).then_inc(s_wT, 1)
                act.copy(uvT[:, :, :], ps[:, 2, 0:H * C1].rearrange("p (h c) -> p h c", h=H)).then_inc(s_wT, 1)
                act.wait_ge(s_a_ps, 1)
                act.wait_ge(s_zero, 1)
                a_ps = ps[0:C1, 3, 0:H * C1].rearrange("p (h c) -> p h c", h=H)
                for r in (0, 64):
                    for c0 in (0, 64):
                        act.copy(wa[r:r + C1, 0:H, c0:c0 + C], a_ps[:, :, 0:C]).then_inc(s_a, 1)
                    act.copy(va[r:r + C1, 0:H], a_ps[:, :, C:C1].rearrange("p h c -> p (h c)")).then_inc(s_a, 1)
                act.wait_ge(s_wa, 4)
                act.wait_ge(s_a, 6)
                act.copy(wa_hi[:, :, :], wa[:, :, :]).then_inc(s_wah, 1)
                act.copy(va_hi[:, :], va[:, :]).then_inc(s_wah, 1)
                act.wait_ge(s_g_ps, 1)
                act.copy(g_w[:, :, :], ps[:, 4, 0:2 * D].rearrange("p (m n) -> p m n", m=2)).then_inc(s_g, 1)
                for b in range(NB):
                    act.wait_ge(s_hT_ps, b + 1)
                    if b >= 2:
                        act.wait_ge(s_proj, b - 1)
                    act.copy(hT[:, b % 2, :], ps[:, b % 2, :]).then_inc(s_hT, 1)
                    act.wait_ge(s_proj, b + 1)
                    if b >= 2:
                        act.wait_ge(s_split, 3 * (b - 1))
                    act.activation(k_f[:, b % 2, :], ps[0:KW, 2 + b % 2, :], ACT.Identity, bias=b_kk[:, :]).then_inc(s_kf, 1)
                    act.activation(c_f[:, b % 2, :], ps[0:C, 5 + b % 2, :], ACT.Identity, bias=b_q[:, :]).then_inc(s_cf, 1)
                    act.wait_ge(s_kf, b + 1)
                    act.copy(key1[0:KW, b * BLK:(b + 1) * BLK], k_f[:, b % 2, :]).then_inc(s_khi, 1)
                    act.wait_ge(s_cf, b + 1)
                    act.copy(cq[0:C, b * BLK:(b + 1) * BLK], c_f[:, b % 2, :]).then_inc(s_chi, 1)
                for b in range(NB):
                    act.wait_ge(s_sq_ps, b + 1)
                    act.copy(sq[:, b * BLK:(b + 1) * BLK], ps[0:H + 1, b % 2, :]).then_inc(s_sqe, 1)

            @block.gpsimd
            def _(pool):
                pool.memset(ident[:, :], 0.0).then_inc(s_const, 1)
                pool.wait_ge(s_const, 1)
                pool.affine_select(out=ident[:, :], in_=ident[:, :], compare_op=ALU.not_equal, fill=1.0, base=0,
                                   pattern=[[-1, P]], channel_multiplier=1).then_inc(s_const, 1)
                pool.wait_ge(s_const, 2)
                pool.memset(ones_row[:, :], 1.0).then_inc(s_const, 1)
                pool.wait_ge(s_const, 3)
                pool.memset(mhalf[:, :], -0.5).then_inc(s_const, 1)
                pool.wait_ge(s_const, 4)
                pool.memset(fold[:, :], 0.0).then_inc(s_const, 1)
                pool.wait_ge(s_const, 5)
                for n, base in enumerate((0, -C)):
                    pool.affine_select(out=fold[0:2 * C, 0:C], in_=fold[0:2 * C, 0:C], compare_op=ALU.not_equal,
                                       fill=1.0, base=base, pattern=[[-1, C]], channel_multiplier=1).then_inc(s_const, 1)
                    pool.wait_ge(s_const, 6 + n)
                pool.memset(fold[2 * C:2 * C + 1, C:C1], 1.0).then_inc(s_const, 1)
                pool.wait_ge(s_const, 8)
                for n, (t, value) in enumerate(((cq[:, :], 0.0), (key2[0:KW, :], 0.0), (q_lo[0:KW, :, :], 0.0),
                                                (cq[C:C1, :], 1.0), (key2[0:1, :], 1.0), (key2[32:33, :], 1.0),
                                                (val[:, :, 2 * C:2 * C + 1], 1.0))):
                    pool.memset(t.bitcast(F32), value).then_inc(s_k2, 1)
                    pool.wait_ge(s_k2, n + 1)
                for b in range(NB):
                    pool.wait_ge(s_mv, TPB * (b + 1))
                    if b >= 2:
                        pool.wait_ge(s_hn, TPB * (b - 1))
                    pool.tensor_scalar(vare[:, b % 2, :], mv[:, b % 2, :, 1], EPS, None, ALU.add).then_inc(s_ve, 1)
                    pool.wait_ge(s_ve, b + 1)
                    pool.tensor_tensor(rstd[:, b % 2, :], vare[:, b % 2, :], mhalf[:, :], ALU.pow).then_inc(s_rstd, 1)
                pool.wait_ge(s_rstd, NB)
                for b in range(NB):
                    pool.wait_ge(s_khi, b + 1)
                    pool.tensor_copy(key2[KW:P, b * BLK:(b + 1) * BLK], key1[0:KW, b * BLK:(b + 1) * BLK]).then_inc(s_k2, 1)

            @block.vector
            def _(dve):
                dve.memset(wa[:, :, :], 0.0)
                dve.memset(va[:, :], 0.0).then_inc(s_zero, 1)
                dve.wait_ge(s_zero, 1)
                dve.wait_ge(ld_w, 16 * 17)
                for r in (0, 64):
                    for c0 in (C, 64 + C):
                        dve.tensor_copy(wa[r:r + C1, 0:H, c0:c0 + C], qr[:, :, :]).then_inc(s_wa, 1)
                dve.wait_ge(s_wah, 2)
                dve.tensor_tensor(wa_lo[:, :, :], wa[:, :, :], wa_hi[:, :, :].bitcast(F32), ALU.subtract).then_inc(s_wal, 1)
                dve.tensor_tensor(va_lo[:, :], va[:, :], va_hi[:, :].bitcast(F32), ALU.subtract).then_inc(s_wal, 1)
                dve.wait_ge(s_g_ps, 2)
                dve.tensor_tensor(g_b[:, :], ps[0:1, 7, 0:D], b_o[:, :], ALU.add).then_inc(s_g, 1)

                def norm_stats(b):
                    dve.wait_ge(ld_x[b], 16)
                    for i in range(TPB):
                        dve.bn_stats(stats[:, b % 2, i, :], X[:, TPB * b + i, :]).then_inc(s_st, 1)
                    for i in range(TPB):
                        dve.wait_ge(s_st, TPB * b + i + 1)
                        dve.bn_aggr(mv[:, b % 2, i, :], stats[:, b % 2, i, :]).then_inc(s_mv, 1)

                def norm(b):
                    dve.wait_ge(s_rstd, b + 1)
                    if b >= 2:
                        dve.wait_ge(s_hT_ps, b - 1)
                    for i in range(TPB):
                        dve.tensor_scalar(hn[:, b % 2, i, :], X[:, TPB * b + i, :], mv[:, b % 2, i, 0:1],
                                          rstd[:, b % 2, i:i + 1], ALU.subtract, ALU.mult).then_inc(s_hn, 1)

                norm_stats(0)
                for b in range(NB):
                    if b + 1 < NB:
                        norm_stats(b + 1)
                    norm(b)
                    dve.wait_ge(s_proj, b + 1)
                    dve.tensor_tensor(v_f[:, b % 2, :, :], ps[:, 4, 0:TPB * C].rearrange("p (i c) -> p i c", i=TPB),
                                      b_v[:, :].unsqueeze(1).to_broadcast([P, TPB, C]), ALU.add).then_inc(s_vf, 1)
                    dve.wait_ge(s_vf, b + 1)
                    dve.tensor_copy(val[:, TPB * b:TPB * (b + 1), 0:C], v_f[:, b % 2, :, :]).then_inc(s_vhi, 1)
                    dve.wait_ge(s_vhi, b + 1)
                    dve.tensor_tensor(val[:, TPB * b:TPB * (b + 1), C:2 * C], v_f[:, b % 2, :, :],
                                      val[:, TPB * b:TPB * (b + 1), 0:C].bitcast(F32), ALU.subtract).then_inc(s_split, 1)
                    cols = slice(b * BLK, (b + 1) * BLK)
                    dve.wait_ge(s_khi, b + 1)
                    dve.tensor_tensor(key1[KW:P, cols], k_f[:, b % 2, :], key1[0:KW, cols].bitcast(F32),
                                      ALU.subtract).then_inc(s_split, 1)
                    dve.wait_ge(s_chi, b + 1)
                    dve.tensor_tensor(cq[64:64 + C, cols], c_f[:, b % 2, :], cq[0:C, cols].bitcast(F32),
                                      ALU.subtract).then_inc(s_split, 1)

            @block.tensor
            def _(pe):
                pe.wait_ge(s_const, 8)
                pe.wait_ge(ld_w, 16 * 17)
                for j, w in enumerate((uq, uk, uv)):
                    for h in range(H):
                        last = pe.transpose(ps[:, j, h * C1:(h + 1) * C1], w[:, h * DK:(h + 1) * DK], ident[0:C1, 0:C1])
                    last.then_inc(s_wT_ps, 1)
                pe.wait_ge(s_wT, 3)
                for h in range(H):
                    last = pe.matmul(ps[0:C1, 3, h * C1:(h + 1) * C1], uqT[:, h, :], ukT[:, h, :], start=True, stop=True)
                last.then_inc(s_a_ps, 1)
                for h in range(H):
                    j, m = h % 4, h // 4
                    last = pe.matmul(ps[C * j:C * (j + 1), 4, m * D:(m + 1) * D], uvT[:, h, 0:C], w_o[:, h, :],
                                     start=True, stop=True)
                last.then_inc(s_g_ps, 1)
                for h in range(H):
                    last = pe.matmul(ps[0:1, 7, 0:D], uvT[:, h, C:C1], w_o[:, h, :], start=(h == 0), stop=(h == H - 1))
                last.then_inc(s_g_ps, 1)
                for b in range(NB):
                    pe.wait_ge(s_hn, TPB * (b + 1))
                    if b < 2:
                        pe.wait_ge(s_wT, 3)
                    else:
                        pe.wait_ge(s_hT, b - 1)
                    for i in range(TPB):
                        last = pe.transpose(ps[:, b % 2, i * P:(i + 1) * P], hn[:, b % 2, i, :], ident[:, :])
                    last.then_inc(s_hT_ps, 1)
                    pe.wait_ge(s_hT, b + 1)
                    if b == 0:
                        pe.wait_ge(s_a, 6)
                        pe.wait_ge(s_g, 1)
                    else:
                        pe.wait_ge(s_vf, b)
                    if b >= 2:
                        pe.wait_ge(s_cf, b - 1)
                    pe.matmul(ps[0:KW, 2 + b % 2, :], w_kk[:, :], hT[:, b % 2, :], start=True, stop=True)
                    pe.matmul(ps[0:C, 5 + b % 2, :], w_dq[:, :], hT[:, b % 2, :], start=True, stop=True)
                    for i in range(TPB):
                        last = pe.matmul(ps[:, 4, i * C:(i + 1) * C], hT[:, b % 2, i * P:(i + 1) * P], w_kk[:, 0:C],
                                         start=True, stop=True)
                    last.then_inc(s_proj, 1)
                pe.wait_ge(s_wal, 2)
                pe.wait_ge(s_k2, 7)
                for b in range(NB):
                    pe.wait_ge(s_split, 3 * (b + 1))
                    pe.wait_ge(s_hT, NB)
                    if b >= 2:
                        pe.wait_ge(s_sqe, b - 1)
                    pe.matmul(ps[0:H + 1, b % 2, :], va_hi[:, :], cq[:, b * BLK:(b + 1) * BLK], start=True, stop=False)
                    pe.matmul(ps[0:H + 1, b % 2, :], va_lo[:, :], cq[:, b * BLK:(b + 1) * BLK], start=False,
                              stop=True).then_inc(s_sq_ps, 1)

        folding.close()

        def sb(name, shape, dt=F32):
            return attn.enter_context(nc.sbuf_tensor(name, shape, dt))

        p32 = sb("p32", [P, 2, 2 * BLK])
        p_hi = sb("p_hi", [P, 4, 2 * BLK], F32R)
        p_lo = sb("p_lo", [P, 4, 2 * BLK], F32R)
        mx = sb("mx", [P, 2, TPB, 2])
        nmx = sb("nmx", [P, 2, TPB], F32R)
        ident_r = sb("ident_r", [P, P], F32R)
        u_sb = sb("u_sb", [2 * C + 1, BLK])
        rden = sb("rden", [P, TPB])

        PAIRS = NT // 2
        LAG = 3
        NBLK = H * NB
        ON_POOL = (0, 4)
        s_idr = sem("s_idr")
        s_wh = sem("s_wh")
        s_qps, s_qhi, s_qlo, s_qc = sem("s_qps"), sem("s_qhi"), sem("s_qlo"), sem("s_qc")
        s_mps, s_mrd, s_nmx, s_shps, s_shift = sem("s_mps"), sem("s_mrd"), sem("s_nmx"), sem("s_shps"), sem("s_shift")
        s_sc, s_exp, s_phi, s_pv = sem("s_sc"), sem("s_exp"), sem("s_phi"), sem("s_pv")
        s_plo, s_plo_pool = sem("s_plo"), sem("s_plo_pool")
        s_usb, s_utps, s_rden, s_ut = sem("s_usb"), sem("s_utps"), sem("s_rden"), sem("s_ut")
        sc_ps = [ps[:, 0:2, :], ps[:, 2:4, :]]

        def chunk_of(h, k, slot):
            c = (slot + 2) % PAIRS
            ahead = 1 if slot + 2 < PAIRS else 2
            return 4 * h + k + ahead, (k + ahead) % NB, c

        def wait_low(eng, n, p):
            if p in ON_POOL:
                eng.wait_ge(s_plo_pool, len(ON_POOL) * n + sum(x <= p for x in ON_POOL))
            else:
                eng.wait_ge(s_plo, (PAIRS - len(ON_POOL)) * n + p + 1 - sum(x <= p for x in ON_POOL))

        with nc.Block() as block:
            @block.gpsimd
            def _(pool):
                def weights(h):
                    for part, w in enumerate((wa_hi, wa_lo)):
                        pool.tensor_copy(w_head[:, part, :], w[:, bass.ds(h, 1), :].rearrange("p a c -> p (a c)")).then_inc(s_wh, 1)

                def low(g, b4):
                    pool.wait_ge(s_phi, g + 1)
                    pool.tensor_tensor(p_lo[:, b4, :], p32[:, b4 % 2, :], p_hi[:, b4, :].bitcast(F32),
                                       ALU.subtract).then_inc(s_plo_pool, 1)

                def head(h):
                    for k in range(NB):
                        for p in ON_POOL:
                            low(PAIRS * (4 * h + k) + p, p % 4)
                        if k == 1:
                            pool.wait_ge(s_qps, 4 * h + 4)
                            weights(h + 1)

                weights(0)
                head(0)
                with pool.Fori(1, H) as h:
                    head(h)

            @block.tensor
            def _(pe):
                def query(n, k, head):
                    bank = 7 - k % 2
                    pe.wait_ge(s_wh, 2 * (head + 1))
                    cols = cq[:, k * BLK:(k + 1) * BLK]
                    pe.matmul(ps[:, bank, :], w_head[:, 0, :], cols, start=True, stop=False)
                    pe.matmul(ps[:, bank, :], w_head[:, 1, :], cols, start=False, stop=True).then_inc(s_qps, 1)

                def rows(n, k, c, first=False):
                    if c == 0:
                        pe.wait_ge(s_qhi, n + 1)
                    if not first:
                        pe.wait_ge(s_mrd, PAIRS * n + c)
                    i, half = c // 2, c % 2
                    for j, (r, key) in enumerate(((0, key1), (KW, key2))):
                        t0 = (2 * half + j) * BLK
                        last = pe.matmul(ps[:, 4 + j, :], q_hi[r:r + KW, k, i * P:(i + 1) * P], key[r:r + KW, t0:t0 + BLK],
                                         start=True, stop=True)
                    last.then_inc(s_mps, 1)

                def shift(n, k):
                    bank = 6 + k % 2
                    pe.wait_ge(s_nmx, n + 1)
                    pe.wait_ge(s_qlo, n + 2)
                    pe.wait_ge(s_qhi, n + 2)
                    for i in range(TPB):
                        last = pe.matmul(ps[0:1, bank, i * P:(i + 1) * P], nmx[:, k % 2, i:i + 1], ident_r[:, :],
                                         start=True, stop=True)
                    last.then_inc(s_shps, 1)

                def pv(n, k, p, h0):
                    g = PAIRS * n + p
                    pe.wait_ge(s_phi, g + 1)
                    wait_low(pe, n, p)
                    if p == 0:
                        pe.wait_ge(s_shift, n + 1)
                        pe.wait_ge(s_qlo, n + 2)
                        pe.wait_ge(s_qhi, n + 2)
                        if h0 is None or k >= 2:
                            pe.wait_ge(s_ut, n - 1)
                    for part in (p_hi, p_lo):
                        for j in range(2):
                            t = 2 * p + j
                            last = pe.matmul(ps[0:2 * C + 1, 6 + k % 2, :], val[:, t, :],
                                             part[:, p % 4, j * BLK:(j + 1) * BLK],
                                             start=(p == 0 and part is p_hi and j == 0),
                                             stop=(p == PAIRS - 1 and part is p_lo and j == 1))
                    last.then_inc(s_pv, 1)

                def turn(n, k):
                    pe.wait_ge(s_usb, n + 1)
                    for i in range(TPB):
                        last = pe.matmul(ps[:, 6 + k % 2, i * C1:(i + 1) * C1], u_sb[:, i * P:(i + 1) * P], fold[:, :],
                                         start=True, stop=True)
                    last.then_inc(s_utps, 1)

                def head(h, h0):
                    for k in range(NB):
                        n = 4 * h + k
                        for slot in range(PAIRS):
                            g = PAIRS * n + slot
                            if slot == 7:
                                shift(n + 1, (k + 1) % NB)
                            rows(*chunk_of(h, k, slot))
                            if slot == 0:
                                pe.wait_ge(s_shift, n + 1)
                                pe.wait_ge(s_qlo, n + 1)
                                pe.wait_ge(s_qc, 16 * (n + 1))
                            if h0 is None or k > 0 or slot >= 2:
                                pe.wait_ge(s_exp, g - 1)
                            for j in range(2):
                                cols = slice((2 * slot + j) * P, (2 * slot + j + 1) * P)
                                pe.matmul(sc_ps[slot % 2][:, j, :], key1[:, cols], q_hi[:, k, :], start=True, stop=False)
                                last = pe.matmul(sc_ps[slot % 2][:, j, :], key2[:, cols], q_lo[:, k, :], start=False,
                                                 stop=True)
                            last.then_inc(s_sc, 1)
                            if slot == 0 and (h0 is None or k >= 2):
                                turn(n - 2, k)
                            if slot == 4:
                                if h0 is None or k > 0:
                                    pe.wait_ge(s_usb, n)
                                query(n + 2, (k + 2) % NB, h if k < 2 else h + 1)
                            if slot >= LAG:
                                pv(n, k, slot - LAG, h0)
                            elif h0 is None or k > 0:
                                pv(n - 1, (k - 1) % NB, slot - LAG + PAIRS, h0)

                query(0, 0, 0)
                query(1, 1, 0)
                for c in range(PAIRS):
                    rows(0, 0, c, first=(c == 0))
                rows(1, 1, 0)
                rows(1, 1, 1)
                pe.wait_ge(s_idr, 1)
                shift(0, 0)
                head(0, 0)
                with pe.Fori(1, H) as h:
                    head(h, None)
                for p in range(PAIRS - LAG, PAIRS):
                    pv(NBLK - 1, NB - 1, p, None)
                turn(NBLK - 2, 2)
                pe.wait_ge(s_ut, NBLK - 1)
                turn(NBLK - 1, 3)

            @block.scalar
            def _(act):
                def query_hi(n, k):
                    act.wait_ge(s_qps, n + 1)
                    act.copy(q_hi[:, k, :], ps[:, 7 - k % 2, :]).then_inc(s_qhi, 1)

                def constants(n, k):
                    act.dma_start(q_lo[0:1, k, :].bitcast(F32), sq_flat[:, bass.ds(n * BLK, BLK)]).then_inc(s_qc, 16)

                def shift_row(n, k):
                    act.wait_ge(s_shps, n + 1)
                    act.copy(q_lo[32:33, k, :], ps[0:1, 6 + k % 2, :]).then_inc(s_shift, 1)

                def sums(n, k):
                    act.wait_ge(s_pv, PAIRS * (n + 1))
                    act.copy(u_sb[:, :], ps[0:2 * C + 1, 6 + k % 2, :]).then_inc(s_usb, 1)

                def high(g, b4):
                    act.wait_ge(s_exp, g + 1)
                    act.copy(p_hi[:, b4, :], p32[:, b4 % 2, :]).then_inc(s_phi, 1)

                def head(h, h0):
                    for k in range(NB):
                        n = 4 * h + k
                        for slot in range(PAIRS):
                            g = PAIRS * n + slot
                            if slot == 4 and (h0 is None or k > 0):
                                if h0 is None or k > 1:
                                    act.wait_ge(s_utps, n - 1)
                                sums(n - 1, (k - 1) % NB)
                            if slot == 5:
                                query_hi(n + 2, (k + 2) % NB)
                            if slot == 6:
                                act.wait_ge(s_qc, 16 * (n + 2))
                                constants(n + 2, (k + 2) % NB)
                            if h0 is None or k > 0 or slot >= 1:
                                if h0 is None or k > 0 or slot >= 5:
                                    act.wait_ge(s_pv, g - 4)
                                high(g - 1, (slot - 1) % 4)
                            if slot == 7:
                                shift_row(n + 1, (k + 1) % NB)
                            act.wait_ge(s_sc, g + 1)
                            if h0 is None or k > 0 or slot >= 2:
                                wait_low(act, n if slot >= 2 else n - 1, (slot - 2) % PAIRS)
                            act.activation(p32[:, slot % 2, :], sc_ps[slot % 2].rearrange("p a n -> p (a n)"), ACT.Exp,
                                           scale=SCALE).then_inc(s_exp, 1)

                constants(0, 0)
                query_hi(0, 0)
                query_hi(1, 1)
                act.wait_ge(s_qc, 16)
                constants(1, 1)
                shift_row(0, 0)
                head(0, 0)
                with act.Fori(1, H) as h:
                    head(h, None)
                high(PAIRS * NBLK - 1, 3)
                act.wait_ge(s_utps, NBLK - 1)
                sums(NBLK - 1, 3)
                act.wait_ge(s_qc, 16 * (NBLK + 2))

            @block.vector
            def _(dve):
                def query_lo(n, k):
                    dve.wait_ge(s_qhi, n + 1)
                    dve.tensor_tensor(q_lo[KW:P, k, :], ps[KW:P, 7 - k % 2, :], q_hi[KW:P, k, :].bitcast(F32),
                                      ALU.subtract).then_inc(s_qlo, 1)

                def chunk_max(n, k, c):
                    dve.wait_ge(s_mps, PAIRS * n + c + 1)
                    dve.tensor_reduce(mx[:, k % 2, c // 2, c % 2:c % 2 + 1], ps[:, 4:6, :], AX.XY, ALU.max).then_inc(s_mrd, 1)

                def minus_max(n, k):
                    dve.wait_ge(s_mrd, PAIRS * (n + 1))
                    dve.tensor_reduce(nmx[:, k % 2, :], mx[:, k % 2, :, :], AX.X, ALU.max, negate=True).then_inc(s_nmx, 1)

                def low(g, b4, first=False):
                    dve.wait_ge(s_phi, g + 1)
                    dve.tensor_tensor(p_lo[:, b4, :], p32[:, b4 % 2, :], p_hi[:, b4, :].bitcast(F32),
                                      ALU.subtract).then_inc(s_plo, 1)

                def normalise(n, k, h):
                    dve.wait_ge(s_utps, n + 1)
                    u = ps[:, 6 + k % 2, 0:TPB * C1].rearrange("p (i c) -> p i c", i=TPB)
                    dve.reciprocal(rden[:, :], u[:, :, C]).then_inc(s_rden, 1)
                    dve.wait_ge(s_rden, n + 1)
                    dve.tensor_tensor(ua[:, TPB * k:TPB * (k + 1), bass.ds(h * C, C)], u[:, :, 0:C],
                                      rden[:, :].unsqueeze(2).to_broadcast([P, TPB, C]), ALU.mult).then_inc(s_ut, 1)

                def head(h, h0):
                    for k in range(NB):
                        n = 4 * h + k
                        for slot in range(PAIRS):
                            g = PAIRS * n + slot
                            if slot == 1 and (h0 is None or k >= 2):
                                normalise(n - 2, (k - 2) % NB, h if k >= 2 else h - 1)
                            if slot == 5:
                                query_lo(n + 2, (k + 2) % NB)
                            if slot == 6:
                                minus_max(n + 1, (k + 1) % NB)
                            chunk_max(*chunk_of(h, k, slot))
                            if (h0 is None or k > 0 or slot >= 1) and (slot - 1) % PAIRS not in ON_POOL:
                                low(g - 1, (slot - 1) % 4)

                dve.tensor_copy(ident_r[:, :], ident[:, :]).then_inc(s_idr, 1)
                query_lo(0, 0)
                query_lo(1, 1)
                for c in range(PAIRS):
                    chunk_max(0, 0, c)
                minus_max(0, 0)
                chunk_max(1, 1, 0)
                chunk_max(1, 1, 1)
                head(0, 0)
                with dve.Fori(1, H) as h:
                    head(h, None)
                low(PAIRS * NBLK - 1, 3)
                normalise(NBLK - 2, 2, H - 1)
                normalise(NBLK - 1, 3, H - 1)

        attn.close()

        def sb(name, shape, dt=F32):
            return ctx.enter_context(nc.sbuf_tensor(name, shape, dt))

        hn = sb("hn_rows", [P, NT, D])
        hT_hi = sb("hT_hi", [P, S], F32R)
        hT_lo = sb("hT_lo", [P, S], F32R)
        uaT = sb("uaT", [P, 2, BLK])
        anchors2 = sb("anchors2", [P, P])
        w_a_hi = sb("w_a_hi", [P, H1 * A], F32R)
        w_a_lo = sb("w_a_lo", [P, H1 * A], F32R)
        w_hi = [sb(f"w_hi{n}", [P, E * M1], F32R) for n in range(3)]
        w_lo = [sb(f"w_lo{n}", [P, E * M1], F32R) for n in range(3)]
        gate1_hi = sb("gate1_hi", [P, E], F32R)
        gate1_lo = sb("gate1_lo", [P, E], F32R)
        w_oT = sb("w_oT", [P, HP, D])
        w_v = sb("w_v", [P, H1, D])
        gate0T = sb("gate0T", [P, E])
        mean_col = sb("mean_col", [P, 1])
        iota8 = sb("iota8", [P, E])

        early = ctx.enter_context(ExitStack())

        def sb(name, shape, dt=F32):
            return early.enter_context(nc.sbuf_tensor(name, shape, dt))

        hT = sb("hT_whole", [P, S])
        w_raw = [sb(f"w_raw{n}", [P, E * M1]) for n in range(3)]

        def layernorm(tag, wait_x, whole):
            names = ("st", "mv", "ve", "rstd", "hn", "ps", "hT", "lo")
            s = {n: sem(f"s_{tag}_{n}") for n in names}

            def on_vector_stats(dve, b):
                wait_x(dve, b)
                for i in range(TPB):
                    dve.bn_stats(stats[:, b % 2, i, :], X[:, TPB * b + i, :]).then_inc(s["st"], 1)
                for i in range(TPB):
                    dve.wait_ge(s["st"], TPB * b + i + 1)
                    dve.bn_aggr(mv[:, b % 2, i, :], stats[:, b % 2, i, :]).then_inc(s["mv"], 1)

            def on_gpsimd(pool, b):
                pool.wait_ge(s["mv"], TPB * (b + 1))
                if b >= 2:
                    pool.wait_ge(s["hn"], TPB * (b - 1))
                pool.tensor_scalar(vare[:, b % 2, :], mv[:, b % 2, :, 1], EPS, None, ALU.add).then_inc(s["ve"], 1)
                pool.wait_ge(s["ve"], b + 1)
                pool.tensor_tensor(rstd[:, b % 2, :], vare[:, b % 2, :], mhalf[:, :], ALU.pow).then_inc(s["rstd"], 1)

            def on_vector(dve, b):
                dve.wait_ge(s["rstd"], b + 1)
                for i in range(TPB):
                    t = TPB * b + i
                    dve.tensor_scalar(hn[:, t, :], X[:, t, :], mv[:, b % 2, i, 0:1], rstd[:, b % 2, i:i + 1],
                                      ALU.subtract, ALU.mult).then_inc(s["hn"], 1)

            def on_tensor(pe, b, bank):
                pe.wait_ge(s["hn"], TPB * (b + 1))
                for i in range(TPB):
                    last = pe.transpose(ps[:, bank, i * P:(i + 1) * P], hn[:, TPB * b + i, :], ident[:, :])
                last.then_inc(s["ps"], 1)

            def on_scalar(act, b, bank):
                act.wait_ge(s["ps"], b + 1)
                act.copy((hT if whole else hT_hi)[:, b * BLK:(b + 1) * BLK], ps[:, bank, :]).then_inc(s["hT"], 1)

            def on_vector_lo(dve, b, bank):
                cols = slice(b * BLK, (b + 1) * BLK)
                dve.wait_ge(s["hT"], b + 1)
                dve.tensor_tensor(hT_lo[:, cols], ps[:, bank, :], hT_hi[:, cols].bitcast(F32), ALU.subtract).then_inc(s["lo"], 1)

            return s, on_vector_stats, on_gpsimd, on_vector, on_tensor, on_scalar, on_vector_lo

        s_uaT_ps, s_uaT, s_o_ps, s_x1 = sem("s_uaT_ps"), sem("s_uaT"), sem("s_o_ps"), sem("s_x1")
        s_c2, s_an_ps, s_an, s_wa_ps, s_wa2 = sem("s_c2"), sem("s_an_ps"), sem("s_an"), sem("s_wa_ps"), sem("s_wa2")
        s_wv_ps, s_wv, s_g0_ps, s_g0 = sem("s_wv_ps"), sem("s_wv"), sem("s_g0_ps"), sem("s_g0")
        ln0, ln0_stats, ln0_pool, ln0_norm, ln0_pe, ln0_act, _ = layernorm("ln0", lambda dve, b: dve.wait_ge(s_x1, b + 1), True)
        s_wsp, s_wa_lo = sem("s_wsp"), sem("s_wa_lo")
        with nc.Block() as block:
            @block.gpsimd
            def _(pool):
                pool.memset(anchors2[:, :], 0.0).then_inc(s_c2, 1)
                pool.wait_ge(s_c2, 1)
                pool.memset(mean_col[:, :], 1.0 / S).then_inc(s_c2, 1)
                pool.wait_ge(s_c2, 2)
                pool.iota(iota8[:, :], [[1, E]], base=0, channel_multiplier=0,
                          allow_small_or_imprecise_dtypes=True).then_inc(s_c2, 1)
                pool.wait_ge(s_c2, 3)
                for b in range(NB):
                    ln0_pool(pool, b)

            @block.sync
            def _(sp):
                for n, name in enumerate(("w_g", "w_u")):
                    sp.dma_start(w_raw[n][:, :].rearrange("p (e m) -> p e m", e=E),
                                 d[f"L1_ffn_{name}"].rearrange("e d m -> d e m")).then_inc(ld_l1f, 16)
                sp.dma_start(w_raw[2][:, :].rearrange("p (c n) -> p c n", c=CH),
                             d["L1_ffn_w_d"].rearrange("e m d -> (e m) d").rearrange("(c p) d -> p c d", p=P)).then_inc(ld_l1f, 16)
                sp.dma_start(gate1[:, :], d["L1_ffn_w_gate"]).then_inc(ld_l1f, 16)

            @block.tensor
            def _(pe):
                def out_block(b):
                    if b >= 1:
                        pe.wait_ge(s_uaT, 2 * b)
                    for m in range(2):
                        for i in range(TPB):
                            last = pe.transpose(ps[:, m, i * P:(i + 1) * P], ua[:, TPB * b + i, m * P:(m + 1) * P], ident[:, :])
                        last.then_inc(s_uaT_ps, 1)
                    pe.wait_ge(s_uaT, 2 * (b + 1))
                    if b >= 1:
                        pe.wait_ge(s_x1, b)
                    for i in range(TPB):
                        o = ps[:, 2, i * P:(i + 1) * P]
                        for m in range(2):
                            pe.matmul(o, uaT[:, m, i * P:(i + 1) * P], g_w[:, m, :], start=(m == 0), stop=False)
                        last = pe.matmul(o, ones_row[:, :], g_b[:, :], start=False, stop=True)
                    last.then_inc(s_o_ps, 1)

                out_block(0)
                out_block(1)
                pe.wait_ge(ld_l1a, 16 * 4)
                pe.wait_ge(ld_l0, 16 * 7)
                pe.transpose(ps[0:A, 4, 0:A], anchor[:, :], ident[0:A, 0:A])
                pe.transpose(ps[:, 4, P:P + E], gate0[:, :], ident[0:E, 0:E]).then_inc(s_an_ps, 1)
                for hp in range(HP):
                    last = pe.transpose(ps[:, 5 + hp // 4, (hp % 4) * P:(hp % 4 + 1) * P], w_out[:, hp * P:(hp + 1) * P], ident[:, :])
                last.then_inc(s_an_ps, 1)
                out_block(2)
                ln0_pe(pe, 0, 3)
                out_block(3)
                pe.wait_ge(s_an, 5)
                for half in range(2):
                    for q in range(4):
                        hp = 4 * half + q
                        last = pe.matmul(ps[:, 4 + half, q * P:(q + 1) * P], emb[:, hp, :], anchors2[:, :], start=True, stop=True)
                    last.then_inc(s_wa_ps, 1)
                pe.wait_ge(ln0["hT"], 1)
                ln0_pe(pe, 1, 3)
                for r in range(4):
                    bank = (6, 7, 4, 5)[r]
                    if r >= 2:
                        pe.wait_ge(s_wa_lo, r - 1)
                    for q in range(4):
                        h = 8 * (r // 2) + 2 * q + r % 2
                        rows = slice((h % 2) * A, (h % 2 + 1) * A)
                        last = pe.matmul(ps[:, bank, q * P:(q + 1) * P], emb[rows, HP + h // 2, :], w_oT[rows, h // 2, :],
                                         start=True, stop=True)
                    last.then_inc(s_wv_ps, 1)
                for b in (2, 3):
                    pe.wait_ge(ln0["hT"], b)
                    ln0_pe(pe, b, 3)

            @block.scalar
            def _(act):
                def out_block(b):
                    for m in range(2):
                        act.wait_ge(s_uaT_ps, 2 * b + m + 1)
                        if b >= 1:
                            act.wait_ge(s_o_ps, b)
                        act.copy(uaT[:, m, :], ps[:, m, :]).then_inc(s_uaT, 1)

                out_block(0)
                out_block(1)
                act.wait_ge(s_an_ps, 1)
                act.wait_ge(s_c2, 1)
                act.copy(anchors2[0:A, 0:A], ps[0:A, 4, 0:A]).then_inc(s_an, 1)
                act.copy(anchors2[A:P, A:P], ps[0:A, 4, 0:A]).then_inc(s_an, 1)
                act.copy(gate0T[:, :], ps[:, 4, P:P + E]).then_inc(s_an, 1)
                act.wait_ge(s_an_ps, 2)
                for m in range(2):
                    act.copy(w_oT[:, 4 * m:4 * (m + 1), :], ps[:, 5 + m, :].rearrange("p (h n) -> p h n", h=4)).then_inc(s_an, 1)
                out_block(2)
                ln0_act(act, 0, 3)
                out_block(3)
                for m in range(2):
                    act.wait_ge(s_wa_ps, m + 1)
                    act.copy(w_a_hi[:, m * BLK:(m + 1) * BLK], ps[:, 4 + m, :]).then_inc(s_wa2, 1)
                ln0_act(act, 1, 3)
                for r in range(4):
                    act.wait_ge(s_wv_ps, r + 1)
                    act.copy(w_v[:, bass.ds(8 * (r // 2) + r % 2, 4, step=2), :], ps[:, (6, 7, 4, 5)[r], :].rearrange("p (h n) -> p h n", h=4)).then_inc(s_wv, 1)
                ln0_act(act, 2, 3)
                ln0_act(act, 3, 3)

            @block.vector
            def _(dve):
                for b in range(NB):
                    dve.wait_ge(s_o_ps, b + 1)
                    xb = X[:, TPB * b:TPB * (b + 1), :]
                    dve.tensor_tensor(xb, ps[:, 2, :].rearrange("p (i n) -> p i n", i=TPB), xb, ALU.add).then_inc(s_x1, 1)
                    ln0_stats(dve, b)
                    ln0_norm(dve, b)
                for m in range(2):
                    cols = slice(m * BLK, (m + 1) * BLK)
                    dve.wait_ge(s_wa2, m + 1)
                    dve.tensor_tensor(w_a_lo[:, cols], ps[:, 4 + m, :], w_a_hi[:, cols].bitcast(F32), ALU.subtract).then_inc(s_wa_lo, 1)

        pooled = sb("pooled", [P, 1])
        g8 = sb("g8", [1, 12, E])
        gi = sb("gi", [1, E], U32)
        g1 = sb("g1", [1, 8])
        coef = sb("coef", [P, 4, E])
        pick = sb("pick", [P, E])
        gb = sb("gb", [E, P])
        tmp_d = sb("tmp_d", [P, D, E])
        tmp_u = sb("tmp_u", [P, 2, BN, E])
        tmp_b = sb("tmp_b", [P, E])
        sel_d = sb("sel_d", [P, D])
        sel_u = sb("sel_u", [P, P])
        sel_b = sb("sel_b", [P, 1])
        sel_dT = sb("sel_dT", [P, P])
        sel_uT = sb("sel_uT", [P, D])
        hid0 = sb("hid0", [P, 2, BLK])
        s_pool_ps, s_pooled, s_lg, s_gv, s_ge = sem("s_pool_ps"), sem("s_pooled"), sem("s_lg"), sem("s_gv"), sem("s_ge")
        s_cf_ps, s_cfd, s_sel, s_selT_ps, s_selT = sem("s_cf_ps"), sem("s_cfd"), sem("s_sel"), sem("s_selT_ps"), sem("s_selT")
        s_h0_ps, s_h0, s_y0_ps, s_x2 = sem("s_h0_ps"), sem("s_h0"), sem("s_y0_ps"), sem("s_x2")
        ln1, ln1_stats, ln1_pool, ln1_norm, ln1_pe, ln1_act, ln1_lo = layernorm("ln1", lambda dve, b: dve.wait_ge(s_x2, b + 1), False)
        LOGIT, EXPD, PROB, TOP, IDX, OH0, OH1, CW0, CW1, GW = range(10)
        with nc.Block() as block:
            @block.tensor
            def _(pe):
                for t in range(NT):
                    last = pe.matmul(ps[:, 0, 0:1], hn[:, t, :], mean_col[:, :], start=(t == 0), stop=(t == NT - 1))
                last.then_inc(s_pool_ps, 1)
                pe.wait_ge(s_pooled, 1)
                pe.matmul(ps[0:1, 1, 0:E], pooled[:, :], gate0T[:, :], start=True, stop=True).then_inc(s_lg, 1)
                pe.wait_ge(s_gv, 14)
                pe.matmul(ps[:, 2, 0:4 * E], ones_row[:, :], g8[:, OH0:OH0 + 4, :].rearrange("p a e -> p (a e)"), start=True, stop=True).then_inc(s_cf_ps, 1)
                pe.matmul(ps[0:E, 3, 0:P], g8[:, GW, :], ones_row[:, :], start=True, stop=True).then_inc(s_cf_ps, 1)
                pe.wait_ge(s_sel, 2)
                pe.transpose(ps[:, 4, 0:P], sel_d[:, :], ident[:, :]).then_inc(s_selT_ps, 1)
                pe.wait_ge(s_sel, 4)
                pe.transpose(ps[:, 5, 0:P], sel_u[:, :], ident[:, :]).then_inc(s_selT_ps, 1)
                pe.wait_ge(s_selT, 2)

                def ln1_block(b):
                    if b >= 2:
                        pe.wait_ge(ln1["lo"], b - 1)
                    ln1_pe(pe, b, 4 + b % 2)

                for b in range(NB + 1):
                    if b < NB:
                        if b >= 2:
                            pe.wait_ge(s_h0, b - 1)
                        pe.matmul(ps[:, b % 2, :], sel_dT[:, :], hT[:, b * BLK:(b + 1) * BLK], start=True, stop=True).then_inc(s_h0_ps, 1)
                    if b >= 1:
                        pe.wait_ge(s_h0, b)
                        if b >= 2:
                            pe.wait_ge(s_x2, b - 1)
                        for i in range(TPB):
                            o = ps[:, 6, i * P:(i + 1) * P]
                            pe.matmul(o, hid0[:, (b - 1) % 2, i * P:(i + 1) * P], sel_uT[:, :], start=True, stop=False)
                            last = pe.matmul(o, gb[:, :], up0_b[:, :], start=False, stop=True)
                        last.then_inc(s_y0_ps, 1)
                    if b >= 2:
                        ln1_block(b - 2)
                ln1_block(NB - 1)

            @block.scalar
            def _(act):
                act.wait_ge(s_pool_ps, 1)
                act.copy(pooled[:, :], ps[:, 0, 0:1]).then_inc(s_pooled, 1)
                act.wait_ge(s_gv, 1)
                act.activation(g8[:, EXPD, :], ps[0:1, 1, 0:E], ACT.Exp, bias=g1[:, 0:1], accum_out=g1[:, 1:2]).then_inc(s_ge, 1)
                act.wait_ge(s_cf_ps, 1)
                act.copy(coef[:, :, :], ps[:, 2, 0:4 * E].rearrange("p (a e) -> p a e", a=4)).then_inc(s_cfd, 1)
                act.copy(pick[0:BN, :], ps[0:BN, 2, 0:E]).then_inc(s_cfd, 1)
                act.copy(pick[BN:P, :], ps[BN:P, 2, E:2 * E]).then_inc(s_cfd, 1)
                act.wait_ge(s_cf_ps, 2)
                act.copy(gb[:, :], ps[0:E, 3, 0:P]).then_inc(s_cfd, 1)
                act.wait_ge(s_selT_ps, 1)
                act.copy(sel_dT[:, :], ps[:, 4, 0:P]).then_inc(s_selT, 1)
                act.wait_ge(s_selT_ps, 2)
                act.copy(sel_uT[:, :], ps[:, 5, 0:P]).then_inc(s_selT, 1)
                act.wait_ge(s_sel, 6)
                for b in range(NB):
                    act.wait_ge(s_h0_ps, b + 1)
                    if b >= 2:
                        act.wait_ge(s_y0_ps, b - 1)
                    act.activation(hid0[:, b % 2, :], ps[:, b % 2, :], ACT.Gelu, bias=sel_b[:, :]).then_inc(s_h0, 1)
                for b in range(NB):
                    ln1_act(act, b, 4 + b % 2)

            @block.gpsimd
            def _(pool):
                pool.wait_ge(ld_l1f, 16 * 4)
                for n, (hi, lo, raw) in enumerate(((gate1_hi, gate1_lo, gate1), *zip(w_hi, w_lo, w_raw))):
                    pool.tensor_copy(hi[:, :], raw[:, :]).then_inc(s_wsp, 1)
                    pool.wait_ge(s_wsp, 2 * n + 1)
                    pool.tensor_tensor(lo[:, :], raw[:, :], hi[:, :].bitcast(F32), ALU.subtract).then_inc(s_wsp, 1)
                    pool.wait_ge(s_wsp, 2 * n + 2)
                for b in range(NB):
                    ln1_pool(pool, b)

            @block.vector
            def _(dve):
                done = [0]

                def step(ins):
                    ins.then_inc(s_gv, 1)
                    done[0] += 1
                    dve.wait_ge(s_gv, done[0])

                dve.wait_ge(s_lg, 1)
                step(dve.tensor_reduce(g1[:, 0:1], ps[0:1, 1, 0:E], AX.X, ALU.max, negate=True))
                dve.wait_ge(s_ge, 1)
                step(dve.reciprocal(g1[:, 2:3], g1[:, 1:2]))
                step(dve.tensor_scalar(g8[:, PROB, :], g8[:, EXPD, :], g1[:, 2:3], None, ALU.mult))
                step(dve.max(g8[:, TOP, :], g8[:, PROB, :]))
                step(dve.max_index(gi[:, :], g8[:, TOP, :], g8[:, PROB, :]))
                step(dve.tensor_copy(g8[:, IDX, :], gi[:, :]))
                step(dve.tensor_scalar(g8[:, OH0, :], iota8[0:1, :], g8[:, IDX, 0:1], None, ALU.is_equal))
                step(dve.tensor_scalar(g8[:, OH1, :], iota8[0:1, :], g8[:, IDX, 1:2], None, ALU.is_equal))
                step(dve.tensor_scalar(g1[:, 3:4], g8[:, TOP, 0:1], g8[:, TOP, 1:2], 1e-8, ALU.add, ALU.add))
                step(dve.reciprocal(g1[:, 4:5], g1[:, 3:4]))
                step(dve.tensor_scalar(g1[:, 5:7], g8[:, TOP, 0:2], g1[:, 4:5], None, ALU.mult))
                step(dve.tensor_scalar(g8[:, CW0, :], g8[:, OH0, :], g1[:, 5:6], None, ALU.mult))
                step(dve.tensor_scalar(g8[:, CW1, :], g8[:, OH1, :], g1[:, 6:7], None, ALU.mult))
                step(dve.tensor_tensor(g8[:, GW, :], g8[:, CW0, :], g8[:, CW1, :], ALU.add))
                dve.wait_ge(s_cfd, 3)
                dve.tensor_tensor(tmp_d[:, :, :], down0[:, :, :].rearrange("p e d -> p d e"),
                                  pick[:, :].unsqueeze(1).to_broadcast([P, D, E]), ALU.mult).then_inc(s_sel, 1)
                dve.wait_ge(s_sel, 1)
                dve.tensor_reduce(sel_d[:, :], tmp_d[:, :, :], AX.X, ALU.add).then_inc(s_sel, 1)
                dve.tensor_tensor(tmp_u[:, :, :, :], up0[:, :, :].rearrange("p e c -> p c e").unsqueeze(1).to_broadcast([P, 2, BN, E]),
                                  coef[:, 2:4, :].unsqueeze(2).to_broadcast([P, 2, BN, E]), ALU.mult).then_inc(s_sel, 1)
                dve.wait_ge(s_sel, 3)
                dve.tensor_reduce(sel_u[:, :].rearrange("p (k c) -> p k c", k=2), tmp_u[:, :, :, :], AX.X, ALU.add).then_inc(s_sel, 1)
                dve.tensor_tensor(tmp_b[:, :], down0_b[:, :], pick[:, :], ALU.mult).then_inc(s_sel, 1)
                dve.wait_ge(s_sel, 5)
                dve.tensor_reduce(sel_b[:, :], tmp_b[:, :], AX.X, ALU.add).then_inc(s_sel, 1)
                for b in range(NB):
                    dve.wait_ge(s_y0_ps, b + 1)
                    xb = X[:, TPB * b:TPB * (b + 1), :]
                    dve.tensor_tensor(xb, ps[:, 6, :].rearrange("p (i n) -> p i n", i=TPB), xb, ALU.add).then_inc(s_x2, 1)
                    ln1_stats(dve, b)
                    ln1_norm(dve, b)
                    if b >= 1:
                        ln1_lo(dve, b - 1, 4 + (b - 1) % 2)
                ln1_lo(dve, NB - 1, 4 + (NB - 1) % 2)

        early.close()
        late = ctx.enter_context(ExitStack())

        def sb(name, shape, dt=F32):
            return late.enter_context(nc.sbuf_tensor(name, shape, dt))

        pT = sb("pT", [P, HP, S])
        cen = emb[:, :, :].rearrange("p (b t) d -> p b (t d)", b=2).rearrange("p b (h a) -> p b h a", a=A)
        prb = ua[:, 0:NT // 2, :].rearrange("p (b t) d -> p b (t d)", b=2).rearrange("p b (h a) -> p b h a", a=A)
        nrm = sb("nrm", [P, 3, H1, A])
        tmax = sb("tmax", [P, 2, H1])
        tsum = sb("tsum", [P, 2, H1])
        trec = sb("trec", [P, 2, H1])
        yT, zz = w_out, w_oT
        asum = sb("asum", [P, 4, HP])
        apart = sb("apart", [P, HP, NT])
        SCALE1 = float(A) ** -0.5
        FMAX = 3.4028234663852886e38
        s_ls, s_tm, s_cen, s_pr = sem("s_ls"), sem("s_tm"), sem("s_cen"), sem("s_pr")
        s_ts, s_tr, s_nr, s_y_ps, s_pT_ps, s_pT = sem("s_ts"), sem("s_tr"), sem("s_nr"), sem("s_y_ps"), sem("s_pT_ps"), sem("s_pT")
        s_yT, s_as, s_z_ps, s_z, s_o1_ps, s_x3, s_oc = sem("s_yT"), sem("s_as"), sem("s_z_ps"), sem("s_z"), sem("s_o1_ps"), sem("s_x3"), sem("s_oc")
        ln2, ln2_stats, ln2_pool, ln2_norm, ln2_pe, ln2_act, ln2_lo = layernorm("ln2", lambda dve, b: dve.wait_ge(s_x3, b + 1), False)
        with nc.Block() as block:
            @block.tensor
            def _(pe):
                for t in range(NT + 2):
                    if t < NT:
                        if t >= 2:
                            pe.wait_ge(s_cen, t - 1)
                        for x, (h_part, w_part) in enumerate(((hT_hi, w_a_hi), (hT_hi, w_a_lo), (hT_lo, w_a_hi))):
                            for m in range(2):
                                last = pe.matmul(ps[:, 2 * (t % 2) + m, :], h_part[:, t * P:(t + 1) * P],
                                                 w_part[:, m * BLK:(m + 1) * BLK], start=(x == 0), stop=(x == 2))
                        last.then_inc(s_ls, 1)
                    if t >= 2:
                        u = t - 2
                        pe.wait_ge(s_nr, u + 1)
                        pu = nrm[:, u % 3, :, :].rearrange("p h a -> p (h a)")
                        for m in range(2):
                            if u >= 1:
                                pe.wait_ge(s_pT, HP * (u - 1) + 4 * (m + 1))
                            for q in range(4):
                                c0 = (4 * m + q) * P
                                last = pe.transpose(ps[:, 6 + m, q * P:(q + 1) * P], pu[:, c0:c0 + P], ident[:, :])
                            last.then_inc(s_pT_ps, 1)
                            last = pe.matmul(ps[:, 4 + m, :], hn[:, u, :], pu[:, m * BLK:(m + 1) * BLK], start=(u == 0),
                                             stop=(u == NT - 1))
                        last.then_inc(s_y_ps, 1)
                pe.wait_ge(s_yT, 2)
                for h in range(H1):
                    rows = slice((h % 2) * A, (h % 2 + 1) * A)
                    hp = h // 2
                    last = pe.matmul(ps[rows, hp // 4, (hp % 4) * P:(hp % 4 + 1) * P], yT[:, h * A:(h + 1) * A], w_v[:, h, :],
                                     start=True, stop=True)
                last.then_inc(s_z_ps, 1)
                pe.wait_ge(s_z, 2)
                for b in range(NB):
                    if b >= 2:
                        pe.wait_ge(s_x3, b - 1)
                    for i in range(TPB):
                        o = ps[:, 2 + b % 2, i * P:(i + 1) * P]
                        for hp in range(HP):
                            pe.matmul(o, pT[:, hp, b * BLK + i * P:b * BLK + (i + 1) * P], zz[:, hp, :], start=(hp == 0), stop=False)
                        last = pe.matmul(o, ones_row[:, :], b_out[:, :], start=False, stop=True)
                    last.then_inc(s_o1_ps, 1)
                    if b >= 1:
                        if b >= 3:
                            pe.wait_ge(ln2["lo"], b - 2)
                        ln2_pe(pe, b - 1, 4 + (b - 1) % 2)
                pe.wait_ge(ln2["lo"], 2)
                ln2_pe(pe, 3, 5)

            @block.scalar
            def _(act):
                for t in range(NT + 2):
                    if t < NT:
                        act.wait_ge(s_cen, t + 1)
                        if t >= 2:
                            act.wait_ge(s_nr, t - 1)
                        act.activation(prb[:, t % 2], cen[:, t % 2], ACT.Exp, scale=SCALE1).then_inc(s_pr, 1)
                    if t >= 2:
                        u = t - 2
                        for m in range(2):
                            act.wait_ge(s_pT_ps, 2 * u + m + 1)
                            for q in range(4):
                                act.activation(pT[:, 4 * m + q, u * P:(u + 1) * P], ps[:, 6 + m, q * P:(q + 1) * P],
                                               ACT.Copy, accum_out=apart[:, 4 * m + q, u:u + 1]).then_inc(s_pT, 1)
                act.wait_ge(s_y_ps, NT)
                for m in range(2):
                    act.copy(yT[:, m * BLK:(m + 1) * BLK], ps[:, 4 + m, :]).then_inc(s_yT, 1)
                for b in range(NB):
                    ln2_act(act, b, 4 + b % 2)

            @block.gpsimd
            def _(pool):
                for t in range(NT):
                    pool.wait_ge(s_tr, t + 1)
                    if t >= 3:
                        pool.wait_ge(s_y_ps, t - 2)
                    pool.tensor_tensor(nrm[:, t % 3, :, :], prb[:, t % 2],
                                       trec[:, t % 2, :].unsqueeze(2).to_broadcast([P, H1, A]), ALU.mult).then_inc(s_nr, 1)
                for b in range(NB):
                    ln2_pool(pool, b)

            @block.vector
            def _(dve):
                for t in range(NT + 1):
                    if t < NT:
                        sc = ps[:, 2 * (t % 2):2 * (t % 2) + 2, :].rearrange("p m (h a) -> p (m h) a", a=A)
                        dve.wait_ge(s_ls, t + 1)
                        dve.tensor_reduce(tmax[:, t % 2, :], sc, AX.X, ALU.max).then_inc(s_tm, 1)
                        dve.wait_ge(s_tm, t + 1)
                        if t >= 2:
                            dve.wait_ge(s_pr, t - 1)
                        dve.tensor_tensor(cen[:, t % 2], sc, tmax[:, t % 2, :].unsqueeze(2).to_broadcast([P, H1, A]),
                                          ALU.subtract).then_inc(s_cen, 1)
                    if t >= 1:
                        u = t - 1
                        dve.wait_ge(s_pr, u + 1)
                        dve.tensor_reduce(tsum[:, u % 2, :], prb[:, u % 2], AX.X, ALU.add).then_inc(s_ts, 1)
                        dve.wait_ge(s_ts, u + 1)
                        if u >= 2:
                            dve.wait_ge(s_nr, u - 1)
                        dve.reciprocal(trec[:, u % 2, :], tsum[:, u % 2, :]).then_inc(s_tr, 1)
                dve.wait_ge(s_pT, HP * NT)
                dve.tensor_reduce(asum[:, 0, :], apart[:, :, :], AX.X, ALU.add).then_inc(s_as, 1)
                dve.wait_ge(s_as, 1)
                dve.reciprocal(asum[:, 1, :], asum[:, 0, :]).then_inc(s_as, 1)
                dve.wait_ge(s_as, 2)
                dve.tensor_scalar(asum[:, 2, :], asum[:, 1, :], FMAX, None, ALU.is_le).then_inc(s_as, 1)
                dve.wait_ge(s_as, 3)
                dve.scalar_tensor_tensor(out=asum[:, 3, :], in0=asum[:, 1, :], scalar=FMAX, in1=asum[:, 2, :],
                                         op0=ALU.min, op1=ALU.mult).then_inc(s_as, 1)
                dve.wait_ge(s_as, 4)
                dve.wait_ge(s_z_ps, 1)
                for m in range(2):
                    dve.tensor_tensor(zz[:, 4 * m:4 * (m + 1), :], ps[:, m, :].rearrange("p (h n) -> p h n", h=4),
                                      asum[:, 3, 4 * m:4 * (m + 1)].unsqueeze(2).to_broadcast([P, 4, D]), ALU.mult).then_inc(s_z, 1)
                for b in range(NB):
                    dve.wait_ge(s_o1_ps, b + 1)
                    xb = X[:, TPB * b:TPB * (b + 1), :]
                    dve.tensor_tensor(xb, ps[:, 2 + b % 2, :].rearrange("p (i n) -> p i n", i=TPB), xb, ALU.add).then_inc(s_x3, 1)
                    ln2_stats(dve, b)
                    ln2_norm(dve, b)
                    if b >= 1:
                        ln2_lo(dve, b - 1, 4 + (b - 1) % 2)
                ln2_lo(dve, NB - 1, 5)
        late.close()

        def sb(name, shape, dt=F32):
            return ctx.enter_context(nc.sbuf_tensor(name, shape, dt))

        sc1 = sb("sc1", [P, NT, E])
        top1 = sb("top1", [P, NT, E])
        idx1 = sb("idx1", [P, NT, E], U32)
        idf1 = sb("idf1", [P, NT, E])
        pd = sb("pd", [P, 4, NT])
        eq = sb("eq", [P, 4, NT, E])
        gw = sb("gw", [P, NT, E])
        gT = sb("gT", [40, S], F32R)
        gTf = sb("gTf", [E, S])
        spread_f = sb("spread_f", [40, E, M1])
        spread = sb("spread", [40, E, M1], F32R)
        act_g = sb("act_g", [P, 2, BLK])
        prod = sb("prod", [P, 2, BLK])
        hid = sb("hid", [P, 2, BLK])
        hid_hi = sb("hid_hi", [P, 4, BLK], F32R)
        hid_lo = sb("hid_lo", [P, 4, BLK], F32R)
        y_T = sb("y_T", [P, BLK])
        s_sc1, s_d1, s_e1, s_gt_ps, s_gt, s_gtl, s_sp = (sem(n) for n in ("s_sc1", "s_d1", "s_e1", "s_gt_ps", "s_gt", "s_gtl", "s_sp"))
        s_gp, s_up, s_bp, s_sil, s_pr1, s_hid, s_hhi, s_hlo = (sem(n) for n in ("s_gp", "s_up", "s_bp", "s_sil", "s_pr1", "s_hid", "s_hhi", "s_hlo"))
        s_dn, s_yT1, s_yt_ps, s_x4, s_out = (sem(n) for n in ("s_dn", "s_yT1", "s_yt_ps", "s_x4", "s_out"))
        sp_f = spread[:, :, :].rearrange("p e m -> p (e m)")
        NS = NB * CH
        DLAG = 3
        GLAG = 2
        with nc.Block() as block:
            @block.gpsimd
            def _(pool):
                pool.memset(spread_f[:, :, :], 1.0).then_inc(s_sp, 1)
                pool.wait_ge(s_sp, 1)
                for n, r in enumerate((0, 32)):
                    v = spread_f[r:r + (32 if r == 0 else E), :, :]
                    pool.affine_select(out=v, in_=v, compare_op=ALU.is_equal, fill=0.0, base=0,
                                       pattern=[[-1, E], [0, M1]], channel_multiplier=1).then_inc(s_sp, 1)
                    pool.wait_ge(s_sp, 2 + n)
                pool.tensor_copy(spread[:, :, :], spread_f[:, :, :]).then_inc(s_sp, 1)
                pool.wait_ge(s_sp, 4)
                pool.memset(gT[:, :].bitcast(F32), 0.0).then_inc(s_sp, 1)
                pool.wait_ge(s_sp, 5)
                for n in range(NS):
                    pool.wait_ge(s_hhi, n + 1)
                    if n >= 4:
                        pool.wait_ge(s_dn, n - 3)
                    pool.tensor_tensor(hid_lo[:, n % 4, :], hid[:, n % 2, :], hid_hi[:, n % 4, :].bitcast(F32),
                                       ALU.subtract).then_inc(s_hlo, 1)

            @block.tensor
            def _(pe):
                def split(out_ps, w, x_hi, x_lo, start=True, stop=True):
                    pe.matmul(out_ps, w[0], x_hi, start=start, stop=False)
                    pe.matmul(out_ps, w[1], x_hi, start=False, stop=False)
                    return pe.matmul(out_ps, w[0], x_lo, start=False, stop=stop)

                def gates(n):
                    b, c = n // CH, n % CH
                    if n >= 2:
                        pe.wait_ge(s_hid, n - 1)
                    pe.matmul(ps[:, 4 + n % 2, :], sp_f[:, c * P:(c + 1) * P], gT[:, b * BLK:(b + 1) * BLK],
                              start=True, stop=True).then_inc(s_bp, 1)

                for t in range(NT):
                    cols = slice(t * P, (t + 1) * P)
                    o = ps[:, 6, t * E:(t + 1) * E]
                    pe.matmul(o, hT_hi[:, cols], gate1_hi[:, :], start=True, stop=False)
                    pe.matmul(o, hT_hi[:, cols], gate1_lo[:, :], start=False, stop=False)
                    last = pe.matmul(o, hT_lo[:, cols], gate1_hi[:, :], start=False, stop=True)
                last.then_inc(s_sc1, 1)
                for n in range(NS + DLAG):
                    if n < NS:
                        b, c = n // CH, n % CH
                        cols, part = slice(b * BLK, (b + 1) * BLK), slice(c * P, (c + 1) * P)
                        if n >= 2:
                            pe.wait_ge(s_sil, n - 1)
                        split(ps[:, n % 2, :], (w_hi[0][:, part], w_lo[0][:, part]), hT_hi[:, cols], hT_lo[:, cols]).then_inc(s_gp, 1)
                        if n >= 2:
                            pe.wait_ge(s_pr1, n - 1)
                        split(ps[:, 2 + n % 2, :], (w_hi[1][:, part], w_lo[1][:, part]), hT_hi[:, cols], hT_lo[:, cols]).then_inc(s_up, 1)
                        if n == GLAG - 1:
                            pe.wait_ge(s_d1, 12)
                            for q in range(NB):
                                if q >= 1:
                                    pe.wait_ge(s_gtl, q)
                                for i in range(TPB):
                                    last = pe.transpose(ps[0:E, 7, i * P:(i + 1) * P], gw[:, TPB * q + i, :], ident[:, :])
                                last.then_inc(s_gt_ps, 1)
                            pe.wait_ge(s_gtl, NB)
                            for q in range(GLAG):
                                gates(q)
                        if n >= GLAG:
                            gates(n)
                    if n >= DLAG:
                        u = n - DLAG
                        b, c = u // CH, u % CH
                        part = slice(c * P, (c + 1) * P)
                        pe.wait_ge(s_hlo, u + 1)
                        if c == 0 and b >= 1:
                            pe.wait_ge(s_yT1, b)
                        split(ps[:, 6, :], (w_hi[2][:, part], w_lo[2][:, part]), hid_hi[:, u % 4, :], hid_lo[:, u % 4, :],
                              start=(c == 0), stop=(c == CH - 1)).then_inc(s_dn, 1)
                        if c == 1 and b >= 1 or u == NS - 1:
                            o = b if u == NS - 1 else b - 1
                            pe.wait_ge(s_yT1, o + 1)
                            if o >= 1:
                                pe.wait_ge(s_x4, o)
                            for i in range(TPB):
                                last = pe.transpose(ps[:, 7, i * P:(i + 1) * P], y_T[:, i * P:(i + 1) * P], ident[:, :])
                            last.then_inc(s_yt_ps, 1)

            @block.scalar
            def _(act):
                act.wait_ge(s_sc1, 1)
                act.copy(sc1[:, :, :], ps[:, 6, 0:NT * E].rearrange("p (t e) -> p t e", t=NT)).then_inc(s_e1, 1)
                act.wait_ge(s_d1, 4)
                act.activation(pd[:, 1, :], pd[:, 0, :], ACT.Exp).then_inc(s_e1, 1)

                def silu(n):
                    act.wait_ge(s_gp, n + 1)
                    if n >= 2:
                        act.wait_ge(s_pr1, n - 1)
                    act.activation(act_g[:, n % 2, :], ps[:, n % 2, :], ACT.Silu).then_inc(s_sil, 1)

                for n in range(GLAG):
                    silu(n)
                act.wait_ge(s_sp, 5)
                for b in range(NB):
                    cols = slice(b * BLK, (b + 1) * BLK)
                    act.wait_ge(s_gt_ps, b + 1)
                    act.copy(gTf[:, cols], ps[0:E, 7, :]).then_inc(s_gt, 1)
                    act.copy(gT[0:E, cols], ps[0:E, 7, :]).then_inc(s_gt, 1)
                for n in range(GLAG, NS + 2):
                    u = n - 2
                    act.wait_ge(s_hid, u + 1)
                    if u >= 4:
                        act.wait_ge(s_dn, u - 3)
                    act.copy(hid_hi[:, u % 4, :], hid[:, u % 2, :]).then_inc(s_hhi, 1)
                    if n < NS:
                        silu(n)
                    if u % CH == 0 and u >= CH or u == NS - 1:
                        o = u // CH if u == NS - 1 else u // CH - 1
                        act.wait_ge(s_dn, CH * (o + 1))
                        if o >= 1:
                            act.wait_ge(s_yt_ps, o)
                        act.copy(y_T[:, :], ps[:, 6, :]).then_inc(s_yT1, 1)

            @block.vector
            def _(dve):
                done = [0]

                def step(ins):
                    ins.then_inc(s_d1, 1)
                    done[0] += 1
                    dve.wait_ge(s_d1, done[0])

                dve.wait_ge(s_e1, 1)
                for t in range(NT):
                    last = dve.max(top1[:, t, :], sc1[:, t, :])
                step(last)
                for t in range(NT):
                    last = dve.max_index(idx1[:, t, :], top1[:, t, :], sc1[:, t, :])
                step(last)
                step(dve.tensor_copy(idf1[:, :, :], idx1[:, :, :]))
                step(dve.tensor_tensor(pd[:, 0, :], top1[:, :, 1], top1[:, :, 0], ALU.subtract))
                dve.wait_ge(s_e1, 2)
                step(dve.tensor_scalar(pd[:, 2, :], pd[:, 1, :], 1.0, None, ALU.add))
                step(dve.reciprocal(pd[:, 3, :], pd[:, 2, :]))
                step(dve.tensor_tensor(pd[:, 2, :], pd[:, 1, :], pd[:, 3, :], ALU.mult))
                io = iota8[:, :].unsqueeze(1).to_broadcast([P, NT, E])
                for k, p in ((0, 3), (1, 2)):
                    step(dve.tensor_tensor(eq[:, k, :, :], io, idf1[:, :, k:k + 1].to_broadcast([P, NT, E]), ALU.is_equal))
                    step(dve.tensor_tensor(eq[:, 2 + k, :, :], eq[:, k, :, :], pd[:, p, :].unsqueeze(2).to_broadcast([P, NT, E]), ALU.mult))
                step(dve.tensor_tensor(gw[:, :, :], eq[:, 2, :, :], eq[:, 3, :, :], ALU.add))
                for b in range(NB):
                    cols = slice(b * BLK, (b + 1) * BLK)
                    dve.wait_ge(s_gt, 2 * (b + 1))
                    dve.tensor_tensor(gT[32:32 + E, cols], gTf[:, cols], gT[0:E, cols].bitcast(F32), ALU.subtract).then_inc(s_gtl, 1)
                for n in range(NS):
                    dve.wait_ge(s_up, n + 1)
                    dve.wait_ge(s_sil, n + 1)
                    if n >= 2:
                        dve.wait_ge(s_hid, n - 1)
                    dve.tensor_tensor(prod[:, n % 2, :], ps[:, 2 + n % 2, :], act_g[:, n % 2, :], ALU.mult).then_inc(s_pr1, 1)
                    dve.wait_ge(s_pr1, n + 1)
                    dve.wait_ge(s_bp, n + 1)
                    if n >= 2:
                        dve.wait_ge(s_hlo, n - 1)
                    dve.tensor_tensor(hid[:, n % 2, :], ps[:, 4 + n % 2, :], prod[:, n % 2, :], ALU.mult).then_inc(s_hid, 1)
                    if n % CH == 8 and n > CH or n == NS - 1:
                        o = n // CH if n == NS - 1 else n // CH - 1
                        dve.wait_ge(s_yt_ps, o + 1)
                        xb = X[:, TPB * o:TPB * (o + 1), :]
                        dve.tensor_tensor(xb, ps[:, 7, :].rearrange("p (i n) -> p i n", i=TPB), xb, ALU.add).then_inc(s_x4, 1)

            @block.sync
            def _(sp):
                out_v = out.rearrange("a (t p) d -> p (a t) d", p=P)
                for b in range(NB):
                    sp.wait_ge(s_x4, b + 1)
                    sp.dma_start(out_v[:, TPB * b:TPB * (b + 1), :], X[:, TPB * b:TPB * (b + 1), :]).then_inc(s_out, 16)
                sp.wait_ge(s_out, 16 * NB)


_INS = ['L0_attn_h_t', 'L0_attn_W_DQ', 'L0_attn_b_DQ', 'L0_attn_W_UQ', 'L0_attn_b_UQ', 'L0_attn_W_DKV',
        'L0_attn_b_DKV', 'L0_attn_W_UK', 'L0_attn_b_UK', 'L0_attn_W_UV', 'L0_attn_b_UV', 'L0_attn_W_QR',
        'L0_attn_b_QR', 'L0_attn_W_KR', 'L0_attn_b_KR', 'L0_attn_W_O', 'L0_attn_b_O', 'L0_ffn_gate_w',
        'L0_ffn_down_w', 'L0_ffn_down_b', 'L0_ffn_up_w', 'L0_ffn_up_b', 'L1_attn_W_emb', 'L1_attn_W_anchor',
        'L1_attn_W_out', 'L1_attn_b_out', 'L1_ffn_w_gate', 'L1_ffn_w_g', 'L1_ffn_w_u', 'L1_ffn_w_d']
_OUTS = [((1, 2048, 128), 'float32')]


def kernel(**inputs):
    import numpy as _np
    import concourse.bacc as _bacc
    from concourse import mybir as _mybir
    from concourse.bass_utils import run_bass_kernel_spmd as _run

    nc = _bacc.Bacc("TRN2", target_bir_lowering=False, num_devices=1)
    arrays, tensors = {}, {}
    for name in _INS:
        a = _np.ascontiguousarray(inputs[name])
        arrays[f"in_{name}_dram"] = a
        tensors[name] = nc.dram_tensor(f"in_{name}_dram", a.shape, _mybir.dt.from_np(a.dtype), kind="ExternalInput").ap()
    outs = []
    for i, (shape, dtype) in enumerate(_OUTS):
        dt = _mybir.dt.from_np(_np.dtype(dtype))
        outs.append(nc.dram_tensor(f"out_{i}_dram", shape, dt, kind="ExternalOutput").ap())
    build_kernel(nc, tensors, outs[0])
    r = _run(nc, [arrays], core_ids=[0])
    got = tuple(r.results[0][f"out_{i}_dram"] for i in range(len(_OUTS)))
    return got[0]
```

```python
from contextlib import ExitStack

import concourse.bass as bass
from concourse import mybir

ALU = mybir.AluOpType
ACT = mybir.ActivationFunctionType
AX = mybir.AxisListType
F32 = mybir.dt.float32
F32R = mybir.dt.float32r
U32 = mybir.dt.uint32

P = 128
BLK = 512
TPB = BLK // P
EPS = 1e-5


def build_kernel(nc, d, out):
    S, D = d["L0_attn_h_t"].shape[1:]
    NT = S // P
    NB = S // BLK
    C = d["L0_attn_W_DQ"].shape[1]
    H = d["L0_attn_W_QR"].shape[1] // C
    DK = d["L0_attn_W_UQ"].shape[1] // H
    C1 = C + 1
    KW = 2 * C
    SCALE = float(DK + C) ** -0.5
    assert D == P and DK == P and NT == 16 and H == 8 and C == 32

    ctx = ExitStack()
    with ctx:
        def sb(name, shape, dt=F32):
            return ctx.enter_context(nc.sbuf_tensor(name, shape, dt))

        def sem(name):
            return ctx.enter_context(nc.semaphore(name))

        ps = ctx.enter_context(nc.psum_tensor("ps", [P, 8, BLK], F32))

        X = sb("X", [P, NT, D])
        ident = sb("ident", [P, P])
        ones_row = sb("ones_row", [1, P])
        mhalf = sb("mhalf", [P, TPB])

        E = d["L0_ffn_gate_w"].shape[0]
        BN = d["L0_ffn_down_w"].shape[1]
        A = d["L1_attn_W_anchor"].shape[0]
        H1 = d["L1_attn_W_out"].shape[1] // A
        HP = H1 // 2
        M1 = d["L1_ffn_w_g"].shape[2]
        CH = E * M1 // P
        assert E == 8 and 2 * BN == P and 2 * A == P and E * M1 == CH * P
        gate0 = sb("gate0", [E, D])
        down0 = sb("down0", [P, E, D])
        down0_b = sb("down0_b", [P, E])
        up0 = sb("up0", [P, E, BN])
        up0_b = sb("up0_b", [E, D])
        emb = sb("emb", [P, 2 * HP, D])
        anchor = sb("anchor", [A, A])
        w_out = sb("w_out", [P, H1 * A])
        b_out = sb("b_out", [P, D])
        gate1 = sb("gate1", [P, E])
        g_w = sb("g_w", [P, 2, D])
        g_b = sb("g_b", [1, D])
        g_bias = sb("g_bias", [P, D])
        spread = sb("spread", [40, E, M1], F32R)
        warm = sb("warm", [1, 1])
        stats = sb("stats", [P, 2, TPB, 6])
        mv = sb("mv", [P, 2, TPB, 2])
        rstd = sb("rstd", [P, 2, TPB])
        vare = sb("vare", [P, 2, TPB])
        ua = sb("ua", [P, NT, H * C])
        ld_l0, ld_l1a, ld_l1f = sem("ld_l0"), sem("ld_l1a"), sem("ld_l1f")

        attn = ctx.enter_context(ExitStack())

        def sb(name, shape, dt=F32, stack=attn):
            return stack.enter_context(nc.sbuf_tensor(name, shape, dt))

        wa_hi = sb("wa_hi", [P, H + 1, P], F32R)
        wa_lo = sb("wa_lo", [P, H + 1, P], F32R)
        key1 = sb("key1", [P, S], F32R)
        key2 = sb("key2", [P, S], F32R)
        cq = sb("cq", [P, S], F32R)
        sq = sb("sq", [H + 1, S])
        val = sb("val", [P, NT, 2 * C + 1], F32R)
        w_head = sb("w_head", [P, 2, P], F32R)
        q_hi = sb("q_hi", [P, NB, BLK], F32R)
        q_lo = sb("q_lo", [P, NB, BLK], F32R)

        spread_f = sb("spread_f", [40, E, M1])

        folding = ctx.enter_context(ExitStack())

        def sb(name, shape, dt=F32, stack=folding):
            return stack.enter_context(nc.sbuf_tensor(name, shape, dt))

        w_kc = sb("w_kc", [P, KW + C])
        b_kc = sb("b_kc", [KW + C, 1])
        b_v = sb("b_v", [P, C])
        uq = sb("uq", [C1, H * DK])
        uk = sb("uk", [C1, H * DK])
        uv = sb("uv", [C1, H * DK])
        qr = sb("qr", [C1, H, C])
        w_o = sb("w_o", [P, H, D])
        b_o = sb("b_o", [1, D])
        uqT = sb("uqT", [P, H, C1])
        ukT = sb("ukT", [P, H, C1])
        uvT = sb("uvT", [P, H, C1])
        wa = sb("wa", [P, H + 1, P])
        va = sb("va", [P, H + 1])
        va_hi = sb("va_hi", [P, H + 1], F32R)
        va_lo = sb("va_lo", [P, H + 1], F32R)
        hn = sb("hn", [P, NT, D])
        hT = sb("hT", [P, NB, BLK])
        v_f = sb("v_f", [P, 2, TPB, C])
        sq_dram = nc.dram_tensor("sq_dram", [(H + 1) * S], F32)
        sq_flat = sq_dram.ap().rearrange("(a n) -> a n", a=1)

        ld_x = [sem(f"ld_x{b}") for b in range(NB)]
        ld_p = sem("ld_p")
        ld_w = sem("ld_w")
        s_const = sem("s_const")
        s_zero = sem("s_zero")

        s_wT_ps, s_wT = sem("s_wT_ps"), sem("s_wT")
        s_a_ps, s_a = sem("s_a_ps"), sem("s_a")
        s_wa, s_wah, s_wal = sem("s_wa"), sem("s_wah"), sem("s_wal")
        s_g_ps, s_g, s_gb = sem("s_g_ps"), sem("s_g"), sem("s_gb")
        s_st, s_mv, s_ve, s_rstd, s_hn = sem("s_st"), sem("s_mv"), sem("s_ve"), sem("s_rstd"), sem("s_hn")
        s_hT_ps, s_hT = sem("s_hT_ps"), sem("s_hT")
        s_proj, s_vf, s_vhi, s_val = sem("s_proj"), sem("s_vf"), sem("s_vhi"), sem("s_val")
        s_khi, s_chi, s_klo, s_clo, s_k2 = sem("s_khi"), sem("s_chi"), sem("s_klo"), sem("s_clo"), sem("s_k2")
        s_sq_ps, s_sqe, s_sqd = sem("s_sq_ps"), sem("s_sqe"), sem("s_sqd")

        HD = H * DK

        with nc.Block() as block:
            @block.sync
            def _(sp):
                x_v = d["L0_attn_h_t"].rearrange("a (t p) d -> p (a t) d", p=P)
                for b in range(NB):
                    sp.dma_start(X[:, b * TPB:(b + 1) * TPB, :], x_v[:, b * TPB:(b + 1) * TPB, :]).then_inc(ld_x[b], 16)
                sp.wait_ge(ld_p, 16 * 7)
                sp.wait_ge(ld_w, 16 * 10)
                for r in (0, BN):
                    sp.dma_start(down0[r:r + BN, :, :], d["L0_ffn_down_w"].rearrange("e c d -> c e d")).then_inc(ld_l0, 16)
                    with nc.allow_non_contiguous_dma("8 x 64 words"):
                        sp.dma_start(down0_b[r:r + BN, :], d["L0_ffn_down_b"].rearrange("e c -> c e")).then_inc(ld_l0, 16)
                sp.dma_start(gate0[:, :], d["L0_ffn_gate_w"]).then_inc(ld_l0, 16)
                sp.dma_start(up0[:, :, :], d["L0_ffn_up_w"].rearrange("e d c -> d e c")).then_inc(ld_l0, 16)
                sp.dma_start(up0_b[:, :], d["L0_ffn_up_b"]).then_inc(ld_l0, 16)
                sp.dma_start(emb[:, :, :], d["L1_attn_W_emb"].rearrange("(t p) d -> p t d", p=P)).then_inc(ld_l1a, 16)
                sp.dma_start(anchor[:, :], d["L1_attn_W_anchor"]).then_inc(ld_l1a, 16)
                sp.dma_start(w_out[:, :], d["L1_attn_W_out"]).then_inc(ld_l1a, 16)
                sp.dma_start(b_out[:, :], d["L1_attn_b_out"].rearrange("(a n) -> a n", a=1).to_broadcast([P, D])).then_inc(ld_l1a, 16)
                sp.wait_ge(s_sqe, NB)
                sp.dma_start(sq_dram.ap().rearrange("(h s) -> h s", h=H + 1), sq[:, :]).then_inc(s_sqd, 16)

            @block.scalar
            def _(act):
                def load(dst, src, signal):
                    act.dma_start(dst, src).then_inc(signal, 16)

                def row(name):
                    return d[name].rearrange("(a n) -> a n", a=1)

                def col(name):
                    return d[name].rearrange("(n a) -> n a", a=1)

                for n, name in enumerate(("DKV", "KR", "DQ")):
                    load(w_kc[:, n * C:(n + 1) * C], d[f"L0_attn_W_{name}"], ld_p)
                    load(b_kc[n * C:(n + 1) * C, :], col(f"L0_attn_b_{name}"), ld_p)
                load(b_v[:, :], row("L0_attn_b_DKV").to_broadcast([P, C]), ld_p)
                for t, name in ((uq, "UQ"), (uk, "UK"), (uv, "UV")):
                    load(t[0:C, :], d[f"L0_attn_W_{name}"], ld_w)
                    load(t[C:C1, :], row(f"L0_attn_b_{name}"), ld_w)
                load(qr[0:C, :, :], d["L0_attn_W_QR"].rearrange("c (h r) -> c h r", h=H), ld_w)
                load(qr[C:C1, :, :], d["L0_attn_b_QR"].rearrange("(a h r) -> a h r", a=1, h=H), ld_w)
                load(w_o[:, :, :], d["L0_attn_W_O"].rearrange("(h k) n -> k h n", h=H), ld_w)
                load(b_o[:, :], row("L0_attn_b_O"), ld_w)

                def keys(b):
                    cols = slice(b * BLK, (b + 1) * BLK)
                    act.wait_ge(s_proj, b + 1)
                    act.activation(key1[0:KW, cols], ps[0:KW, 4 + b % 2, :], ACT.Identity, bias=b_kc[0:KW, :]).then_inc(s_khi, 1)
                    act.activation(cq[KW:KW + C, cols], ps[KW:KW + C, 4 + b % 2, :], ACT.Identity,
                                   bias=b_kc[KW:KW + C, :]).then_inc(s_chi, 1)

                for b in range(NB):
                    act.wait_ge(s_hT_ps, b + 1)
                    act.copy(hT[:, b, :], ps[:, b, :]).then_inc(s_hT, 1)
                act.wait_ge(s_zero, 2)
                keys(0)
                keys(1)
                for j, t in enumerate((uqT, ukT, uvT)):
                    act.wait_ge(s_wT_ps, j + 1)
                    act.copy(t[:, :, :], ps[:, j, 0:H * C1].rearrange("p (h c) -> p h c", h=H)).then_inc(s_wT, 1)
                keys(2)
                act.wait_ge(s_a_ps, 1)
                a_ps = ps[0:C1, 3, 0:H * C1].rearrange("p (h c) -> p h c", h=H)
                for r, n in ((0, C1), (64, C)):
                    for c0 in (0, 64):
                        act.copy(wa[r:r + n, 0:H, c0:c0 + C], a_ps[0:n, :, 0:C]).then_inc(s_a, 1)
                    act.copy(va[r:r + n, 0:H], a_ps[0:n, :, C:C1].rearrange("p h c -> p (h c)")).then_inc(s_a, 1)
                act.wait_ge(s_wa, 4)
                act.wait_ge(s_a, 6)
                act.copy(va_hi[:, :], va[:, :]).then_inc(s_wah, 1)
                act.copy(wa_hi[:, :, :], wa[:, :, :]).then_inc(s_wah, 1)
                keys(3)
                act.wait_ge(s_g_ps, 1)
                act.copy(g_w[:, :, :], ps[:, 0, 0:2 * D].rearrange("p (m n) -> p m n", m=2)).then_inc(s_g, 1)
                for b in range(NB):
                    act.wait_ge(s_sq_ps, b + 1)
                    act.copy(sq[:, b * BLK:(b + 1) * BLK], ps[0:H + 1, 4 + b % 2, :]).then_inc(s_sqe, 1)
                act.wait_ge(s_g_ps, 3)
                act.copy(g_bias[:, :], ps[:, 2, 0:D]).then_inc(s_g, 1)

            @block.gpsimd
            def _(pool):
                done = [0]

                def step(ins):
                    ins.then_inc(s_const, 1)
                    done[0] += 1
                    pool.wait_ge(s_const, done[0])

                def rstd_of(b):
                    pool.wait_ge(s_mv, TPB * (b + 1))
                    if b >= 2:
                        pool.wait_ge(s_hn, TPB * (b - 1))
                    pool.tensor_scalar(vare[:, b % 2, :], mv[:, b % 2, :, 1], EPS, None, ALU.add).then_inc(s_ve, 1)
                    pool.wait_ge(s_ve, b + 1)
                    pool.tensor_tensor(rstd[:, b % 2, :], vare[:, b % 2, :], mhalf[:, :], ALU.pow).then_inc(s_rstd, 1)
                    pool.wait_ge(s_rstd, b + 1)

                step(pool.memset(ident[:, :], 0.0))
                step(pool.affine_select(out=ident[:, :], in_=ident[:, :], compare_op=ALU.not_equal, fill=1.0, base=0,
                                        pattern=[[-1, P]], channel_multiplier=1))
                step(pool.memset(mhalf[:, :], -0.5))
                step(pool.memset(key2[0:KW, :].bitcast(F32), 1.0))
                rstd_of(0)
                rstd_of(1)
                step(pool.memset(ones_row[:, :], 1.0))
                rstd_of(2)
                rstd_of(3)
                step(pool.memset(val[:, :, 2 * C:2 * C + 1].bitcast(F32), 1.0))
                step(pool.memset(q_lo[0:KW, :, :].bitcast(F32), 0.0))
                for b in range(NB):
                    pool.wait_ge(s_khi, b + 1)
                    pool.tensor_copy(key2[KW:P, b * BLK:(b + 1) * BLK], key1[0:KW, b * BLK:(b + 1) * BLK]).then_inc(s_k2, 1)

            @block.vector
            def _(dve):
                def norm_stats(b):
                    dve.wait_ge(ld_x[b], 16)
                    for i in range(TPB):
                        dve.bn_stats(stats[:, b % 2, i, :], X[:, TPB * b + i, :]).then_inc(s_st, 1)
                    for i in range(TPB):
                        dve.wait_ge(s_st, TPB * b + i + 1)
                        dve.bn_aggr(mv[:, b % 2, i, :], stats[:, b % 2, i, :]).then_inc(s_mv, 1)

                def norm(b):
                    dve.wait_ge(s_rstd, b + 1)
                    for i in range(TPB):
                        dve.tensor_scalar(hn[:, TPB * b + i, :], X[:, TPB * b + i, :], mv[:, b % 2, i, 0:1],
                                          rstd[:, b % 2, i:i + 1], ALU.subtract, ALU.mult).then_inc(s_hn, 1)

                def values(b):
                    tiles = slice(TPB * b, TPB * (b + 1))
                    dve.wait_ge(s_proj, b + 1)
                    dve.tensor_tensor(v_f[:, b % 2, :, :], ps[:, 6 + b % 2, 0:TPB * C].rearrange("p (i c) -> p i c", i=TPB),
                                      b_v[:, :].unsqueeze(1).to_broadcast([P, TPB, C]), ALU.add).then_inc(s_vf, 1)
                    dve.wait_ge(s_vf, b + 1)
                    dve.tensor_copy(val[:, tiles, 0:C], v_f[:, b % 2, :, :]).then_inc(s_vhi, 1)
                    dve.wait_ge(s_vhi, b + 1)
                    dve.tensor_tensor(val[:, tiles, C:2 * C], v_f[:, b % 2, :, :], val[:, tiles, 0:C].bitcast(F32),
                                      ALU.subtract).then_inc(s_val, 1)

                def keys_lo(b):
                    cols = slice(b * BLK, (b + 1) * BLK)
                    dve.wait_ge(s_khi, b + 1)
                    dve.scalar_tensor_tensor(out=key1[KW:P, cols], in0=ps[0:KW, 4 + b % 2, :], scalar=b_kc[0:KW, :],
                                             in1=key1[0:KW, cols].bitcast(F32), op0=ALU.add, op1=ALU.subtract).then_inc(s_klo, 1)
                    dve.wait_ge(s_chi, b + 1)
                    dve.scalar_tensor_tensor(out=cq[0:C, cols], in0=ps[KW:KW + C, 4 + b % 2, :], scalar=b_kc[KW:KW + C, :],
                                             in1=cq[KW:KW + C, cols].bitcast(F32), op0=ALU.add, op1=ALU.subtract).then_inc(s_clo, 1)

                dve.memset(cq[:, :].bitcast(F32), 1.0).then_inc(s_zero, 1)
                dve.memset(wa[:, :, :], 0.0)
                dve.memset(va[:, :], 0.0).then_inc(s_zero, 1)
                norm_stats(0)
                for b in range(NB):
                    if b + 1 < NB:
                        norm_stats(b + 1)
                    norm(b)
                values(0)
                keys_lo(0)
                dve.wait_ge(s_zero, 2)
                dve.wait_ge(ld_w, 16 * 10)
                for r, n in ((0, C1), (64, C)):
                    for c0 in (C, 64 + C):
                        dve.tensor_copy(wa[r:r + n, 0:H, c0:c0 + C], qr[0:n, :, :]).then_inc(s_wa, 1)
                values(1)
                keys_lo(1)
                values(2)
                keys_lo(2)
                dve.wait_ge(s_wah, 1)
                dve.tensor_tensor(va_lo[:, :], va[:, :], va_hi[:, :].bitcast(F32), ALU.subtract).then_inc(s_wal, 1)
                dve.wait_ge(s_wah, 2)
                dve.tensor_tensor(wa_lo[:, :, :], wa[:, :, :], wa_hi[:, :, :].bitcast(F32), ALU.subtract).then_inc(s_wal, 1)
                values(3)
                keys_lo(3)
                dve.wait_ge(s_g_ps, 2)
                dve.tensor_tensor(g_b[:, :], ps[0:1, 1, 0:D], b_o[:, :], ALU.add).then_inc(s_gb, 1)

            @block.tensor
            def _(pe):
                def project(b):
                    pe.wait_ge(s_hT, b + 1)
                    pe.wait_ge(ld_p, 16 * 7)
                    if b >= 2:
                        pe.wait_ge(s_klo, b - 1)
                        pe.wait_ge(s_clo, b - 1)
                        pe.wait_ge(s_vf, b - 1)
                    pe.matmul(ps[0:KW + C, 4 + b % 2, :], w_kc[:, :], hT[:, b, :], start=True, stop=True)
                    for i in range(TPB):
                        last = pe.matmul(ps[:, 6 + b % 2, i * C:(i + 1) * C], hT[:, b, i * P:(i + 1) * P], w_kc[:, 0:C],
                                         start=True, stop=True)
                    last.then_inc(s_proj, 1)

                pe.wait_ge(s_const, 2)
                for b in range(NB):
                    pe.wait_ge(s_hn, TPB * (b + 1))
                    for i in range(TPB):
                        last = pe.transpose(ps[:, b, i * P:(i + 1) * P], hn[:, TPB * b + i, :], ident[:, :])
                    last.then_inc(s_hT_ps, 1)
                project(0)
                project(1)
                pe.wait_ge(s_hT, NB)
                pe.wait_ge(ld_w, 16 * 10)
                for j, w in enumerate((uq, uk, uv)):
                    for h in range(H):
                        last = pe.transpose(ps[:, j, h * C1:(h + 1) * C1], w[:, h * DK:(h + 1) * DK], ident[0:C1, 0:C1])
                    last.then_inc(s_wT_ps, 1)
                project(2)
                pe.wait_ge(s_wT, 3)
                for h in range(H):
                    last = pe.matmul(ps[0:C1, 3, h * C1:(h + 1) * C1], uqT[:, h, :], ukT[:, h, :], start=True, stop=True)
                last.then_inc(s_a_ps, 1)
                project(3)
                for h in range(H):
                    j, m = h % 4, h // 4
                    last = pe.matmul(ps[C * j:C * (j + 1), 0, m * D:(m + 1) * D], uvT[:, h, 0:C], w_o[:, h, :],
                                     start=True, stop=True)
                last.then_inc(s_g_ps, 1)
                for h in range(H):
                    last = pe.matmul(ps[0:1, 1, 0:D], uvT[:, h, C:C1], w_o[:, h, :], start=(h == 0), stop=(h == H - 1))
                last.then_inc(s_g_ps, 1)
                pe.wait_ge(s_wal, 1)
                for b in range(NB):
                    pe.wait_ge(s_clo, b + 1)
                    if b < 2:
                        pe.wait_ge(s_klo, b + 3)
                        pe.wait_ge(s_clo, b + 3)
                    else:
                        pe.wait_ge(s_sqe, b - 1)
                    pe.matmul(ps[0:H + 1, 4 + b % 2, :], va_hi[:, :], cq[:, b * BLK:(b + 1) * BLK], start=True, stop=False)
                    pe.matmul(ps[0:H + 1, 4 + b % 2, :], va_lo[:, :], cq[:, b * BLK:(b + 1) * BLK], start=False,
                              stop=True).then_inc(s_sq_ps, 1)
                pe.wait_ge(s_gb, 1)
                pe.wait_ge(s_const, 5)
                pe.matmul(ps[:, 2, 0:D], ones_row[:, :], g_b[:, :], start=True, stop=True).then_inc(s_g_ps, 1)

        folding.close()

        def sb(name, shape, dt=F32):
            return attn.enter_context(nc.sbuf_tensor(name, shape, dt))

        p32 = sb("p32", [P, 2, 2 * BLK])
        p_hi = sb("p_hi", [P, 4, 2 * BLK], F32R)
        p_lo = sb("p_lo", [P, 4, 2 * BLK], F32R)
        mx = sb("mx", [P, 2, TPB, 2])
        nmx = sb("nmx", [P, 2, TPB], F32R)
        ident_r = sb("ident_r", [P, P], F32R)
        u_sb = sb("u_sb", [2 * C + 1, BLK])
        rden = sb("rden", [P, TPB])
        u_hi = sb("u_hi", [P, TPB, C])
        u_sum = sb("u_sum", [P, TPB, C])
        UW = 2 * C + 1

        PAIRS = NT // 2
        LAG = 3
        NBLK = H * NB
        ON_POOL = (0, 4)
        s_idr, s_aside = sem("s_idr"), sem("s_aside")
        s_wh = sem("s_wh")
        s_qps, s_qhi, s_qlo, s_qc = sem("s_qps"), sem("s_qhi"), sem("s_qlo"), sem("s_qc")
        s_mps, s_mrd, s_nmx, s_shps, s_shift = sem("s_mps"), sem("s_mrd"), sem("s_nmx"), sem("s_shps"), sem("s_shift")
        s_sc, s_exp, s_phi, s_pv = sem("s_sc"), sem("s_exp"), sem("s_phi"), sem("s_pv")
        s_plo, s_plo_pool = sem("s_plo"), sem("s_plo_pool")
        s_usb, s_utps, s_rden, s_ut = sem("s_usb"), sem("s_utps"), sem("s_rden"), sem("s_ut")
        sc_ps = [ps[:, 0:2, :], ps[:, 2:4, :]]

        def chunk_of(h, k, slot):
            c = (slot + 2) % PAIRS
            ahead = 1 if slot + 2 < PAIRS else 2
            return 4 * h + k + ahead, (k + ahead) % NB, c

        def wait_low(eng, n, p):
            if p in ON_POOL:
                eng.wait_ge(s_plo_pool, len(ON_POOL) * n + sum(x <= p for x in ON_POOL))
            else:
                eng.wait_ge(s_plo, (PAIRS - len(ON_POOL)) * n + p + 1 - sum(x <= p for x in ON_POOL))

        with nc.Block() as block:
            @block.gpsimd
            def _(pool):
                def weights(h):
                    for part, w in enumerate((wa_hi, wa_lo)):
                        pool.tensor_copy(w_head[:, part, :], w[:, bass.ds(h, 1), :].rearrange("p a c -> p (a c)")).then_inc(s_wh, 1)

                def low(g, b4):
                    pool.wait_ge(s_phi, g + 1)
                    pool.tensor_tensor(p_lo[:, b4, :], p32[:, b4 % 2, :], p_hi[:, b4, :].bitcast(F32),
                                       ALU.subtract).then_inc(s_plo_pool, 1)

                def add_bias(b):
                    xb = X[:, TPB * b:TPB * (b + 1), :]
                    return pool.tensor_tensor(xb, xb, g_bias[:, :].unsqueeze(1).to_broadcast([P, TPB, D]), ALU.add)

                def spread_row(r, rows):
                    v = spread_f[r:r + rows, :, :]
                    return pool.affine_select(out=v, in_=v, compare_op=ALU.is_equal, fill=0.0, base=0,
                                              pattern=[[-1, E], [0, M1]], channel_multiplier=1)

                def aside(n):
                    if n < NB:
                        ins = add_bias(n)
                    elif n == NB:
                        ins = pool.memset(spread_f[:, :, :], 1.0)
                    elif n == NB + 1:
                        ins = spread_row(0, 32)
                    elif n == NB + 2:
                        ins = spread_row(32, E)
                    else:
                        ins = pool.tensor_copy(spread[:, :, :], spread_f[:, :, :])
                    ins.then_inc(s_aside, 1)
                    pool.wait_ge(s_aside, n + 1)

                def head(h, h0):
                    for k in range(NB):
                        for x, p in enumerate(ON_POOL):
                            low(PAIRS * (4 * h + k) + p, p % 4)
                            if h0 is not None:
                                pool.wait_ge(s_plo_pool, len(ON_POOL) * k + x + 1)
                                aside(len(ON_POOL) * k + x)
                        if k == 1:
                            pool.wait_ge(s_qps, 4 * h + 4)
                            weights(h + 1)

                weights(0)
                head(0, 0)
                with pool.Fori(1, H) as h:
                    head(h, None)

            @block.tensor
            def _(pe):
                def query(n, k, head):
                    bank = 7 - k % 2
                    pe.wait_ge(s_wh, 2 * (head + 1))
                    cols = cq[:, k * BLK:(k + 1) * BLK]
                    pe.matmul(ps[:, bank, :], w_head[:, 0, :], cols, start=True, stop=False)
                    pe.matmul(ps[:, bank, :], w_head[:, 1, :], cols, start=False, stop=True).then_inc(s_qps, 1)

                def rows(n, k, c, bank=4, read=None):
                    if c == 0:
                        pe.wait_ge(s_qhi, n + 1)
                    if read is None:
                        pe.wait_ge(s_mrd, PAIRS * n + c)
                    elif read > 0:
                        pe.wait_ge(s_mrd, read)
                    i, half = c // 2, c % 2
                    for j, (r, key) in enumerate(((0, key1), (KW, key2))):
                        t0 = (2 * half + j) * BLK
                        last = pe.matmul(ps[:, bank + j, :], q_hi[r:r + KW, k, i * P:(i + 1) * P], key[r:r + KW, t0:t0 + BLK],
                                         start=True, stop=True)
                    last.then_inc(s_mps, 1)

                def shift(n, k):
                    bank = 6 + k % 2
                    pe.wait_ge(s_nmx, n + 1)
                    pe.wait_ge(s_qlo, n + 2)
                    pe.wait_ge(s_qhi, n + 2)
                    for i in range(TPB):
                        last = pe.matmul(ps[0:1, bank, i * P:(i + 1) * P], nmx[:, k % 2, i:i + 1], ident_r[:, :],
                                         start=True, stop=True)
                    last.then_inc(s_shps, 1)

                def pv(n, k, p, h0):
                    g = PAIRS * n + p
                    pe.wait_ge(s_phi, g + 1)
                    wait_low(pe, n, p)
                    if p == 0:
                        pe.wait_ge(s_shift, n + 1)
                        pe.wait_ge(s_qlo, n + 2)
                        pe.wait_ge(s_qhi, n + 2)
                        if h0 is None or k >= 2:
                            pe.wait_ge(s_ut, n - 1)
                    for part in (p_hi, p_lo):
                        for j in range(2):
                            t = 2 * p + j
                            last = pe.matmul(ps[0:2 * C + 1, 6 + k % 2, :], val[:, t, :],
                                             part[:, p % 4, j * BLK:(j + 1) * BLK],
                                             start=(p == 0 and part is p_hi and j == 0),
                                             stop=(p == PAIRS - 1 and part is p_lo and j == 1))
                    last.then_inc(s_pv, 1)

                def turn(n, k):
                    pe.wait_ge(s_usb, n + 1)
                    for i in range(TPB):
                        last = pe.transpose(ps[:, 6 + k % 2, i * UW:(i + 1) * UW], u_sb[:, i * P:(i + 1) * P], ident[0:UW, 0:UW])
                    last.then_inc(s_utps, 1)

                def head(h, h0):
                    for k in range(NB):
                        n = 4 * h + k
                        for slot in range(PAIRS):
                            g = PAIRS * n + slot
                            if slot == 7:
                                shift(n + 1, (k + 1) % NB)
                            rows(*chunk_of(h, k, slot))
                            if slot == 0:
                                pe.wait_ge(s_shift, n + 1)
                                pe.wait_ge(s_qlo, n + 1)
                                pe.wait_ge(s_qc, 16 * (n + 1))
                            if h0 is None or k > 0 or slot >= 2:
                                pe.wait_ge(s_exp, g - 1)
                            for j in range(2):
                                cols = slice((2 * slot + j) * P, (2 * slot + j + 1) * P)
                                pe.matmul(sc_ps[slot % 2][:, j, :], key1[:, cols], q_hi[:, k, :], start=True, stop=False)
                                last = pe.matmul(sc_ps[slot % 2][:, j, :], key2[:, cols], q_lo[:, k, :], start=False,
                                                 stop=True)
                            last.then_inc(s_sc, 1)
                            if slot == 0 and (h0 is None or k >= 2):
                                turn(n - 2, k)
                            if slot == 4:
                                if h0 is None or k > 0:
                                    pe.wait_ge(s_usb, n)
                                query(n + 2, (k + 2) % NB, h if k < 2 else h + 1)
                            if slot >= LAG:
                                pv(n, k, slot - LAG, h0)
                            elif h0 is None or k > 0:
                                pv(n - 1, (k - 1) % NB, slot - LAG + PAIRS, h0)

                query(0, 0, 0)
                query(1, 1, 0)
                for c in range(PAIRS):
                    rows(0, 0, c, bank=2 * (c % 2), read=max(c - 1, 0))
                rows(1, 1, 0, read=PAIRS)
                rows(1, 1, 1)
                pe.wait_ge(s_idr, 1)
                shift(0, 0)
                head(0, 0)
                with pe.Fori(1, H) as h:
                    head(h, None)
                for p in range(PAIRS - LAG, PAIRS):
                    pv(NBLK - 1, NB - 1, p, None)
                turn(NBLK - 2, 2)
                pe.wait_ge(s_ut, NBLK - 1)
                turn(NBLK - 1, 3)

            @block.scalar
            def _(act):
                def query_hi(n, k):
                    act.wait_ge(s_qps, n + 1)
                    act.copy(q_hi[:, k, :], ps[:, 7 - k % 2, :]).then_inc(s_qhi, 1)

                def constants(n, k):
                    act.dma_start(q_lo[0:1, k, :].bitcast(F32), sq_flat[:, bass.ds(n * BLK, BLK)]).then_inc(s_qc, 16)

                def shift_row(n, k):
                    act.wait_ge(s_shps, n + 1)
                    act.copy(q_lo[32:33, k, :], ps[0:1, 6 + k % 2, :]).then_inc(s_shift, 1)

                def sums(n, k):
                    act.wait_ge(s_pv, PAIRS * (n + 1))
                    act.copy(u_sb[:, :], ps[0:2 * C + 1, 6 + k % 2, :]).then_inc(s_usb, 1)

                def high(g, b4):
                    act.wait_ge(s_exp, g + 1)
                    act.copy(p_hi[:, b4, :], p32[:, b4 % 2, :]).then_inc(s_phi, 1)

                def head(h, h0):
                    for k in range(NB):
                        n = 4 * h + k
                        for slot in range(PAIRS):
                            g = PAIRS * n + slot
                            if slot == 4 and (h0 is None or k > 0):
                                if h0 is None or k > 1:
                                    act.wait_ge(s_utps, n - 1)
                                sums(n - 1, (k - 1) % NB)
                            if slot == 5:
                                query_hi(n + 2, (k + 2) % NB)
                            if slot == 6:
                                act.wait_ge(s_qc, 16 * (n + 2))
                                constants(n + 2, (k + 2) % NB)
                            if h0 is None or k > 0 or slot >= 1:
                                if h0 is None or k > 0 or slot >= 5:
                                    act.wait_ge(s_pv, g - 4)
                                high(g - 1, (slot - 1) % 4)
                            if slot == 7:
                                shift_row(n + 1, (k + 1) % NB)
                            act.wait_ge(s_sc, g + 1)
                            if h0 is None or k > 0 or slot >= 2:
                                wait_low(act, n if slot >= 2 else n - 1, (slot - 2) % PAIRS)
                            act.activation(p32[:, slot % 2, :], sc_ps[slot % 2].rearrange("p a n -> p (a n)"), ACT.Exp,
                                           scale=SCALE).then_inc(s_exp, 1)

                act.wait_ge(s_sqd, 16)
                constants(0, 0)
                query_hi(0, 0)
                query_hi(1, 1)
                act.wait_ge(s_qc, 16)
                constants(1, 1)
                shift_row(0, 0)
                head(0, 0)
                with act.Fori(1, H) as h:
                    head(h, None)
                high(PAIRS * NBLK - 1, 3)
                act.wait_ge(s_utps, NBLK - 1)
                sums(NBLK - 1, 3)
                act.wait_ge(s_qc, 16 * (NBLK + 2))

            @block.vector
            def _(dve):
                def query_lo(n, k):
                    dve.wait_ge(s_qhi, n + 1)
                    dve.tensor_tensor(q_lo[KW:P, k, :], ps[KW:P, 7 - k % 2, :], q_hi[KW:P, k, :].bitcast(F32),
                                      ALU.subtract).then_inc(s_qlo, 1)

                def chunk_max(n, k, c, bank=4):
                    dve.wait_ge(s_mps, PAIRS * n + c + 1)
                    dve.tensor_reduce(mx[:, k % 2, c // 2, c % 2:c % 2 + 1], ps[:, bank:bank + 2, :], AX.XY, ALU.max).then_inc(s_mrd, 1)

                def minus_max(n, k):
                    dve.wait_ge(s_mrd, PAIRS * (n + 1))
                    dve.tensor_reduce(nmx[:, k % 2, :], mx[:, k % 2, :, :], AX.X, ALU.max, negate=True).then_inc(s_nmx, 1)

                def low(g, b4, first=False):
                    dve.wait_ge(s_phi, g + 1)
                    dve.tensor_tensor(p_lo[:, b4, :], p32[:, b4 % 2, :], p_hi[:, b4, :].bitcast(F32),
                                      ALU.subtract).then_inc(s_plo, 1)

                def normalise(n, k, h):
                    dve.wait_ge(s_utps, n + 1)
                    u = ps[:, 6 + k % 2, 0:TPB * UW].rearrange("p (i c) -> p i c", i=TPB)
                    dve.reciprocal(rden[:, :], u[:, :, 2 * C]).then_inc(s_rden, 1)
                    dve.tensor_copy(u_hi[:, :, :], u[:, :, 0:C]).then_inc(s_rden, 1)
                    dve.wait_ge(s_rden, 3 * n + 2)
                    dve.tensor_tensor(u_sum[:, :, :], u[:, :, C:2 * C], u_hi[:, :, :], ALU.add).then_inc(s_rden, 1)
                    dve.wait_ge(s_rden, 3 * (n + 1))
                    dve.tensor_tensor(ua[:, TPB * k:TPB * (k + 1), bass.ds(h * C, C)], u_sum[:, :, :],
                                      rden[:, :].unsqueeze(2).to_broadcast([P, TPB, C]), ALU.mult).then_inc(s_ut, 1)

                def head(h, h0):
                    for k in range(NB):
                        n = 4 * h + k
                        for slot in range(PAIRS):
                            g = PAIRS * n + slot
                            if slot == 6:
                                minus_max(n + 1, (k + 1) % NB)
                            chunk_max(*chunk_of(h, k, slot))
                            if slot == 1 and (h0 is None or k >= 2):
                                normalise(n - 2, (k - 2) % NB, h if k >= 2 else h - 1)
                            if slot == 5:
                                query_lo(n + 2, (k + 2) % NB)
                            if (h0 is None or k > 0 or slot >= 1) and (slot - 1) % PAIRS not in ON_POOL:
                                low(g - 1, (slot - 1) % 4)

                dve.tensor_copy(ident_r[:, :], ident[:, :]).then_inc(s_idr, 1)
                query_lo(0, 0)
                query_lo(1, 1)
                for c in range(PAIRS):
                    chunk_max(0, 0, c, bank=2 * (c % 2))
                minus_max(0, 0)
                chunk_max(1, 1, 0)
                chunk_max(1, 1, 1)
                head(0, 0)
                with dve.Fori(1, H) as h:
                    head(h, None)
                low(PAIRS * NBLK - 1, 3)
                normalise(NBLK - 2, 2, H - 1)
                normalise(NBLK - 1, 3, H - 1)

        attn.close()

        def sb(name, shape, dt=F32):
            return ctx.enter_context(nc.sbuf_tensor(name, shape, dt))

        hn = sb("hn_rows", [P, NT, D])
        hT_hi = sb("hT_hi", [P, S], F32R)
        hT_lo = sb("hT_lo", [P, S], F32R)
        anchors2 = sb("anchors2", [P, P])
        w_a_hi = sb("w_a_hi", [P, H1 * A], F32R)
        w_a_lo = sb("w_a_lo", [P, H1 * A], F32R)
        w_hi = [sb(f"w_hi{n}", [P, E * M1], F32R) for n in range(3)]
        w_lo = [sb(f"w_lo{n}", [P, E * M1], F32R) for n in range(3)]
        gate1_hi = sb("gate1_hi", [P, E], F32R)
        gate1_lo = sb("gate1_lo", [P, E], F32R)
        w_oT = sb("w_oT", [P, HP, D])
        w_v = sb("w_v", [P, H1, D])
        gate0T = sb("gate0T", [P, E])
        hsum = sb("hsum", [P, NB])
        iota8 = sb("iota8", [P, E])

        early = ctx.enter_context(ExitStack())

        def sb(name, shape, dt=F32):
            return early.enter_context(nc.sbuf_tensor(name, shape, dt))

        hT = sb("hT_whole", [P, S])
        uaT = sb("uaT", [P, 2, 2, BLK])
        w_raw = [sb(f"w_raw{n}", [P, E * M1]) for n in range(3)]

        def layernorm(tag, wait_x, whole):
            names = ("st", "mv", "ve", "rstd", "hn", "ps", "hT", "lo")
            s = {n: sem(f"s_{tag}_{n}") for n in names}

            def on_vector_stats(dve, b):
                wait_x(dve, b)
                for i in range(TPB):
                    dve.bn_stats(stats[:, b % 2, i, :], X[:, TPB * b + i, :]).then_inc(s["st"], 1)
                for i in range(TPB):
                    dve.wait_ge(s["st"], TPB * b + i + 1)
                    dve.bn_aggr(mv[:, b % 2, i, :], stats[:, b % 2, i, :]).then_inc(s["mv"], 1)

            def on_gpsimd(pool, b):
                pool.wait_ge(s["mv"], TPB * (b + 1))
                if b >= 2:
                    pool.wait_ge(s["hn"], TPB * (b - 1))
                pool.tensor_scalar(vare[:, b % 2, :], mv[:, b % 2, :, 1], EPS, None, ALU.add).then_inc(s["ve"], 1)
                pool.wait_ge(s["ve"], b + 1)
                pool.tensor_tensor(rstd[:, b % 2, :], vare[:, b % 2, :], mhalf[:, :], ALU.pow).then_inc(s["rstd"], 1)

            def on_vector(dve, b):
                dve.wait_ge(s["rstd"], b + 1)
                for i in range(TPB):
                    t = TPB * b + i
                    dve.tensor_scalar(hn[:, t, :], X[:, t, :], mv[:, b % 2, i, 0:1], rstd[:, b % 2, i:i + 1],
                                      ALU.subtract, ALU.mult).then_inc(s["hn"], 1)

            def on_tensor(pe, b, bank):
                pe.wait_ge(s["hn"], TPB * (b + 1))
                for i in range(TPB):
                    last = pe.transpose(ps[:, bank, i * P:(i + 1) * P], hn[:, TPB * b + i, :], ident[:, :])
                last.then_inc(s["ps"], 1)

            def on_scalar(act, b, bank):
                act.wait_ge(s["ps"], b + 1)
                cols = slice(b * BLK, (b + 1) * BLK)
                if whole:
                    act.activation(hT[:, cols], ps[:, bank, :], ACT.Copy, accum_out=hsum[:, b:b + 1]).then_inc(s["hT"], 1)
                else:
                    act.copy(hT_hi[:, cols], ps[:, bank, :]).then_inc(s["hT"], 1)

            def on_vector_lo(dve, b, bank):
                cols = slice(b * BLK, (b + 1) * BLK)
                dve.wait_ge(s["hT"], b + 1)
                dve.tensor_tensor(hT_lo[:, cols], ps[:, bank, :], hT_hi[:, cols].bitcast(F32), ALU.subtract).then_inc(s["lo"], 1)

            return s, on_vector_stats, on_gpsimd, on_vector, on_tensor, on_scalar, on_vector_lo

        s_uaT_ps, s_uaT, s_o_ps, s_x1 = sem("s_uaT_ps"), sem("s_uaT"), sem("s_o_ps"), sem("s_x1")
        s_c2, s_an_ps, s_an, s_wo_ps, s_wo = sem("s_c2"), sem("s_an_ps"), sem("s_an"), sem("s_wo_ps"), sem("s_wo")
        s_wa_ps, s_wa2, s_wa_lo, s_wv_ps, s_wv = sem("s_wa_ps"), sem("s_wa2"), sem("s_wa_lo"), sem("s_wv_ps"), sem("s_wv")
        ln0, ln0_stats, ln0_pool, ln0_norm, ln0_pe, ln0_act, _ = layernorm("ln0", lambda dve, b: dve.wait_ge(s_x1, b + 1), True)
        s_wsp, s_whi, s_wd = sem("s_wsp"), sem("s_whi"), sem("s_wd")
        with nc.Block() as block:
            @block.gpsimd
            def _(pool):
                pool.memset(anchors2[:, :], 0.0).then_inc(s_c2, 1)
                pool.wait_ge(s_c2, 1)
                pool.iota(iota8[:, :], [[1, E]], base=0, channel_multiplier=0,
                          allow_small_or_imprecise_dtypes=True).then_inc(s_c2, 1)
                pool.wait_ge(s_c2, 2)
                for b in range(NB):
                    ln0_pool(pool, b)

            @block.sync
            def _(sp):
                for n, name in enumerate(("w_g", "w_u")):
                    sp.dma_start(w_raw[n][:, :].rearrange("p (e m) -> p e m", e=E),
                                 d[f"L1_ffn_{name}"].rearrange("e d m -> d e m")).then_inc(ld_l1f, 16)
                sp.dma_start(w_raw[2][:, :].rearrange("p (c n) -> p c n", c=CH),
                             d["L1_ffn_w_d"].rearrange("e m d -> (e m) d").rearrange("(c p) d -> p c d", p=P)).then_inc(ld_l1f, 16)
                sp.dma_start(gate1[:, :], d["L1_ffn_w_gate"]).then_inc(ld_l1f, 16)

            @block.tensor
            def _(pe):
                def turn_sums(b):
                    if b >= 2:
                        pe.wait_ge(s_uaT, 2 * (b - 1))
                    for m in range(2):
                        for i in range(TPB):
                            last = pe.transpose(ps[:, 4 * (b % 2) + m, i * P:(i + 1) * P],
                                                ua[:, TPB * b + i, m * P:(m + 1) * P], ident[:, :])
                        last.then_inc(s_uaT_ps, 1)

                def output(b):
                    pe.wait_ge(s_uaT, 2 * (b + 1))
                    if b >= 2:
                        pe.wait_ge(s_x1, b - 1)
                    for i in range(TPB):
                        for m in range(2):
                            last = pe.matmul(ps[:, 2 + b % 2, i * P:(i + 1) * P], uaT[:, b % 2, m, i * P:(i + 1) * P],
                                             g_w[:, m, :], start=(m == 0), stop=(m == 1))
                    last.then_inc(s_o_ps, 1)

                def norm_T(b):
                    if b >= 2:
                        pe.wait_ge(ln0["hT"], b - 1)
                    ln0_pe(pe, b, 6 + b % 2)

                turn_sums(0)
                turn_sums(1)
                output(0)
                turn_sums(2)
                output(1)
                turn_sums(3)
                output(2)
                norm_T(0)
                output(3)
                norm_T(1)
                pe.wait_ge(ld_l1a, 16 * 4)
                pe.wait_ge(ld_l0, 16 * 7)
                pe.wait_ge(s_uaT, 8)
                pe.transpose(ps[0:A, 0, 0:A], anchor[:, :], ident[0:A, 0:A])
                pe.transpose(ps[:, 0, P:P + E], gate0[:, :], ident[0:E, 0:E]).then_inc(s_an_ps, 1)
                norm_T(2)
                for hp in range(HP):
                    last = pe.transpose(ps[:, 4 + hp // 4, (hp % 4) * P:(hp % 4 + 1) * P], w_out[:, hp * P:(hp + 1) * P], ident[:, :])
                last.then_inc(s_wo_ps, 1)
                norm_T(3)

            @block.scalar
            def _(act):
                for b in range(NB):
                    for m in range(2):
                        act.wait_ge(s_uaT_ps, 2 * b + m + 1)
                        if b >= 2:
                            act.wait_ge(s_o_ps, b - 1)
                        act.copy(uaT[:, b % 2, m, :], ps[:, 4 * (b % 2) + m, :]).then_inc(s_uaT, 1)
                ln0_act(act, 0, 6)
                ln0_act(act, 1, 7)
                act.wait_ge(s_an_ps, 1)
                act.wait_ge(s_c2, 1)
                act.copy(anchors2[0:A, 0:A], ps[0:A, 0, 0:A]).then_inc(s_an, 1)
                act.copy(anchors2[A:P, A:P], ps[0:A, 0, 0:A]).then_inc(s_an, 1)
                act.activation(gate0T[:, :], ps[:, 0, P:P + E], ACT.Copy, scale=1.0 / S).then_inc(s_an, 1)
                ln0_act(act, 2, 6)
                act.wait_ge(s_wo_ps, 1)
                for m in range(2):
                    act.copy(w_oT[:, 4 * m:4 * (m + 1), :], ps[:, 4 + m, :].rearrange("p (h n) -> p h n", h=4)).then_inc(s_wo, 1)
                ln0_act(act, 3, 7)

            @block.vector
            def _(dve):
                for b in range(NB + 1):
                    if b < NB:
                        dve.wait_ge(s_o_ps, b + 1)
                        xb = X[:, TPB * b:TPB * (b + 1), :]
                        dve.tensor_tensor(xb, ps[:, 2 + b % 2, :].rearrange("p (i n) -> p i n", i=TPB), xb, ALU.add).then_inc(s_x1, 1)
                        ln0_stats(dve, b)
                    if b >= 1:
                        ln0_norm(dve, b - 1)

        pooled = sb("pooled", [P, 1])
        g8 = sb("g8", [1, 12, E])
        gi = sb("gi", [1, E], U32)
        g1 = sb("g1", [1, 8])
        coef = sb("coef", [P, 4, E])
        pick = sb("pick", [P, E])
        gb = sb("gb", [E, P])
        tmp_d = sb("tmp_d", [P, D, E])
        tmp_u = sb("tmp_u", [P, 2, BN, E])
        tmp_b = sb("tmp_b", [P, E])
        sel_d = sb("sel_d", [P, D])
        sel_u = sb("sel_u", [P, P])
        sel_b = sb("sel_b", [P, 1])
        sel_dT = sb("sel_dT", [P, P])
        sel_uT = sb("sel_uT", [P, D])
        hid0 = sb("hid0", [P, 2, BLK])
        bias0 = sb("bias0", [P, D])
        s_pooled, s_lg, s_gv, s_ge = sem("s_pooled"), sem("s_lg"), sem("s_gv"), sem("s_ge")
        s_b0_ps, s_b0, s_xb = sem("s_b0_ps"), sem("s_b0"), sem("s_xb")
        s_cf_ps, s_cfd, s_sel, s_selT_ps, s_selT = sem("s_cf_ps"), sem("s_cfd"), sem("s_sel"), sem("s_selT_ps"), sem("s_selT")
        s_h0_ps, s_h0, s_y0_ps, s_x2 = sem("s_h0_ps"), sem("s_h0"), sem("s_y0_ps"), sem("s_x2")
        ln1, ln1_stats, ln1_pool, ln1_norm, ln1_pe, ln1_act, ln1_lo = layernorm("ln1", lambda dve, b: dve.wait_ge(s_x2, b + 1), False)
        LOGIT, EXPD, PROB, TOP, IDX, OH0, OH1, CW0, CW1, GW = range(10)
        with nc.Block() as block:
            @block.tensor
            def _(pe):
                pe.wait_ge(s_pooled, 1)
                pe.matmul(ps[0:1, 7, 0:E], pooled[:, :], gate0T[:, :], start=True, stop=True).then_inc(s_lg, 1)

                def values(r):
                    for q in range(4):
                        h = 8 * (r // 2) + 2 * q + r % 2
                        rows = slice((h % 2) * A, (h % 2 + 1) * A)
                        last = pe.matmul(ps[:, r, q * P:(q + 1) * P], emb[rows, HP + h // 2, :], w_oT[rows, h // 2, :],
                                         start=True, stop=True)
                    last.then_inc(s_wv_ps, 1)

                def hidden(b):
                    if b < 2:
                        pe.wait_ge(s_wv, b + 1)
                    else:
                        pe.wait_ge(s_h0, b - 1)
                    pe.matmul(ps[:, b % 2, :], sel_dT[:, :], hT[:, b * BLK:(b + 1) * BLK], start=True, stop=True).then_inc(s_h0_ps, 1)

                values(0)
                values(1)
                pe.wait_ge(s_gv, 14)
                pe.matmul(ps[:, 7, 64:64 + 4 * E], ones_row[:, :], g8[:, OH0:OH0 + 4, :].rearrange("p a e -> p (a e)"), start=True, stop=True).then_inc(s_cf_ps, 1)
                pe.matmul(ps[0:E, 7, P:2 * P], g8[:, GW, :], ones_row[:, :], start=True, stop=True).then_inc(s_cf_ps, 1)
                values(2)
                pe.wait_ge(s_cfd, 4)
                pe.matmul(ps[:, 7, 2 * P:2 * P + D], gb[:, :], up0_b[:, :], start=True, stop=True).then_inc(s_b0_ps, 1)
                pe.wait_ge(s_sel, 2)
                pe.transpose(ps[:, 6, 0:P], sel_d[:, :], ident[:, :]).then_inc(s_selT_ps, 1)
                pe.wait_ge(s_selT, 1)
                hidden(0)
                values(3)
                hidden(1)
                for half in range(2):
                    for q in range(4):
                        hp = 4 * half + q
                        last = pe.matmul(ps[:, 4 + half, q * P:(q + 1) * P], emb[:, hp, :], anchors2[:, :], start=True, stop=True)
                    last.then_inc(s_wa_ps, 1)
                pe.wait_ge(s_sel, 6)
                pe.wait_ge(s_b0, 1)
                pe.transpose(ps[:, 7, 0:P], sel_u[:, :], ident[:, :]).then_inc(s_selT_ps, 1)
                pe.wait_ge(s_selT, 2)

                def ln1_block(b):
                    if b < 2:
                        pe.wait_ge(s_wa_lo, b + 1)
                    else:
                        pe.wait_ge(ln1["lo"], b - 1)
                    ln1_pe(pe, b, 4 + b % 2)

                for b in range(1, NB + 1):
                    if 2 <= b < NB:
                        hidden(b)
                    pe.wait_ge(s_h0, b)
                    if b >= 2:
                        pe.wait_ge(s_x2, b - 1)
                    for i in range(TPB):
                        last = pe.matmul(ps[:, 6, i * P:(i + 1) * P], hid0[:, (b - 1) % 2, i * P:(i + 1) * P], sel_uT[:, :],
                                         start=True, stop=True)
                    last.then_inc(s_y0_ps, 1)
                    if b >= 3:
                        ln1_block(b - 3)
                ln1_block(NB - 2)
                ln1_block(NB - 1)

            @block.scalar
            def _(act):
                act.wait_ge(s_gv, 1)
                act.activation(g8[:, EXPD, :], ps[0:1, 7, 0:E], ACT.Exp, bias=g1[:, 0:1], accum_out=g1[:, 1:2]).then_inc(s_ge, 1)
                act.wait_ge(s_ge, 1)
                act.activation(warm[:, :], g1[:, 1:2], ACT.Gelu).then_inc(s_ge, 1)

                def weights_hi(n):
                    act.wait_ge(ld_l1f, 16 * 4)
                    act.copy(w_hi[n][:, :], w_raw[n][:, :]).then_inc(s_whi, 1)

                def values(r):
                    act.wait_ge(s_wv_ps, r + 1)
                    act.copy(w_v[:, bass.ds(8 * (r // 2) + r % 2, 4, step=2), :], ps[:, r, :].rearrange("p (h n) -> p h n", h=4)).then_inc(s_wv, 1)

                def hidden(b):
                    act.wait_ge(s_h0_ps, b + 1)
                    if b >= 2:
                        act.wait_ge(s_y0_ps, b - 1)
                    act.activation(hid0[:, b % 2, :], ps[:, b % 2, :], ACT.Gelu, bias=sel_b[:, :]).then_inc(s_h0, 1)

                weights_hi(0)
                values(0)
                values(1)
                act.wait_ge(s_cf_ps, 2)
                act.copy(coef[:, :, :], ps[:, 7, 64:64 + 4 * E].rearrange("p (a e) -> p a e", a=4)).then_inc(s_cfd, 1)
                act.copy(pick[0:BN, :], ps[0:BN, 7, 64:64 + E]).then_inc(s_cfd, 1)
                act.copy(pick[BN:P, :], ps[BN:P, 7, 64 + E:64 + 2 * E]).then_inc(s_cfd, 1)
                act.copy(gb[:, :], ps[0:E, 7, P:2 * P]).then_inc(s_cfd, 1)
                values(2)
                act.wait_ge(s_b0_ps, 1)
                act.copy(bias0[:, :], ps[:, 7, 2 * P:2 * P + D]).then_inc(s_b0, 1)
                act.wait_ge(s_selT_ps, 1)
                act.copy(sel_dT[:, :], ps[:, 6, 0:P]).then_inc(s_selT, 1)
                act.wait_ge(s_sel, 4)
                hidden(0)
                values(3)
                hidden(1)
                weights_hi(1)
                for m in range(2):
                    act.wait_ge(s_wa_ps, m + 1)
                    act.copy(w_a_hi[:, m * BLK:(m + 1) * BLK], ps[:, 4 + m, :]).then_inc(s_wa2, 1)
                act.wait_ge(s_selT_ps, 2)
                act.copy(sel_uT[:, :], ps[:, 7, 0:P]).then_inc(s_selT, 1)
                hidden(2)
                hidden(3)
                weights_hi(2)
                for b in range(NB):
                    ln1_act(act, b, 4 + b % 2)

            @block.gpsimd
            def _(pool):
                pool.wait_ge(ld_l1f, 16 * 4)
                pool.tensor_copy(gate1_hi[:, :], gate1[:, :]).then_inc(s_wsp, 1)
                pool.wait_ge(s_wsp, 1)
                pool.tensor_tensor(gate1_lo[:, :], gate1[:, :], gate1_hi[:, :].bitcast(F32), ALU.subtract).then_inc(s_wsp, 1)
                pool.wait_ge(s_wsp, 2)

                def weights_lo(n):
                    pool.wait_ge(s_whi, n + 1)
                    pool.tensor_tensor(w_lo[n][:, :], w_raw[n][:, :], w_hi[n][:, :].bitcast(F32), ALU.subtract).then_inc(s_wsp, 1)
                    pool.wait_ge(s_wsp, 3 + n)

                weights_lo(0)
                pool.wait_ge(s_b0, 1)
                for b in range(NB):
                    xb = X[:, TPB * b:TPB * (b + 1), :]
                    pool.tensor_tensor(xb, xb, bias0[:, :].unsqueeze(1).to_broadcast([P, TPB, D]), ALU.add).then_inc(s_xb, 1)
                    pool.wait_ge(s_xb, b + 1)
                weights_lo(1)
                for b in range(NB):
                    ln1_pool(pool, b)

            @block.vector
            def _(dve):
                done = [0]

                def step(ins):
                    ins.then_inc(s_gv, 1)
                    done[0] += 1
                    dve.wait_ge(s_gv, done[0])

                dve.tensor_reduce(pooled[:, :], hsum[:, :], AX.X, ALU.add).then_inc(s_pooled, 1)
                dve.wait_ge(s_lg, 1)
                step(dve.tensor_reduce(g1[:, 0:1], ps[0:1, 7, 0:E], AX.X, ALU.max, negate=True))
                dve.wait_ge(s_ge, 1)
                step(dve.reciprocal(g1[:, 2:3], g1[:, 1:2]))
                step(dve.tensor_scalar(g8[:, PROB, :], g8[:, EXPD, :], g1[:, 2:3], None, ALU.mult))
                step(dve.max(g8[:, TOP, :], g8[:, PROB, :]))
                step(dve.max_index(gi[:, :], g8[:, TOP, :], g8[:, PROB, :]))
                step(dve.tensor_copy(g8[:, IDX, :], gi[:, :]))
                step(dve.tensor_scalar(g8[:, OH0, :], iota8[0:1, :], g8[:, IDX, 0:1], None, ALU.is_equal))
                step(dve.tensor_scalar(g8[:, OH1, :], iota8[0:1, :], g8[:, IDX, 1:2], None, ALU.is_equal))
                step(dve.tensor_scalar(g1[:, 3:4], g8[:, TOP, 0:1], g8[:, TOP, 1:2], 1e-8, ALU.add, ALU.add))
                step(dve.reciprocal(g1[:, 4:5], g1[:, 3:4]))
                step(dve.tensor_scalar(g1[:, 5:7], g8[:, TOP, 0:2], g1[:, 4:5], None, ALU.mult))
                step(dve.tensor_scalar(g8[:, CW0, :], g8[:, OH0, :], g1[:, 5:6], None, ALU.mult))
                step(dve.tensor_scalar(g8[:, CW1, :], g8[:, OH1, :], g1[:, 6:7], None, ALU.mult))
                step(dve.tensor_tensor(g8[:, GW, :], g8[:, CW0, :], g8[:, CW1, :], ALU.add))
                dve.wait_ge(s_cfd, 3)
                dve.tensor_tensor(tmp_d[:, :, :], down0[:, :, :].rearrange("p e d -> p d e"),
                                  pick[:, :].unsqueeze(1).to_broadcast([P, D, E]), ALU.mult).then_inc(s_sel, 1)
                dve.wait_ge(s_sel, 1)
                dve.tensor_reduce(sel_d[:, :], tmp_d[:, :, :], AX.X, ALU.add).then_inc(s_sel, 1)
                dve.tensor_tensor(tmp_b[:, :], down0_b[:, :], pick[:, :], ALU.mult).then_inc(s_sel, 1)
                dve.wait_ge(s_sel, 3)
                dve.tensor_reduce(sel_b[:, :], tmp_b[:, :], AX.X, ALU.add).then_inc(s_sel, 1)
                dve.tensor_tensor(tmp_u[:, :, :, :], up0[:, :, :].rearrange("p e c -> p c e").unsqueeze(1).to_broadcast([P, 2, BN, E]),
                                  coef[:, 2:4, :].unsqueeze(2).to_broadcast([P, 2, BN, E]), ALU.mult).then_inc(s_sel, 1)
                dve.wait_ge(s_sel, 5)
                dve.tensor_reduce(sel_u[:, :].rearrange("p (k c) -> p k c", k=2), tmp_u[:, :, :, :], AX.X, ALU.add).then_inc(s_sel, 1)
                for m in range(2):
                    cols = slice(m * BLK, (m + 1) * BLK)
                    dve.wait_ge(s_wa2, m + 1)
                    dve.tensor_tensor(w_a_lo[:, cols], ps[:, 4 + m, :], w_a_hi[:, cols].bitcast(F32), ALU.subtract).then_inc(s_wa_lo, 1)
                for b in range(NB + 1):
                    if b < NB:
                        dve.wait_ge(s_y0_ps, b + 1)
                        dve.wait_ge(s_xb, b + 1)
                        xb = X[:, TPB * b:TPB * (b + 1), :]
                        dve.tensor_tensor(xb, ps[:, 6, :].rearrange("p (i n) -> p i n", i=TPB), xb, ALU.add).then_inc(s_x2, 1)
                        ln1_stats(dve, b)
                    if b >= 1:
                        ln1_norm(dve, b - 1)
                    if b >= 2:
                        ln1_lo(dve, b - 2, 4 + b % 2)
                dve.wait_ge(s_whi, 3)
                dve.tensor_tensor(w_lo[2][:, :], w_raw[2][:, :], w_hi[2][:, :].bitcast(F32), ALU.subtract).then_inc(s_wd, 1)
                ln1_lo(dve, NB - 1, 4 + (NB - 1) % 2)

        early.close()
        gT = ctx.enter_context(nc.sbuf_tensor("gT", [40, S], F32R))
        late = ctx.enter_context(ExitStack())

        def sb(name, shape, dt=F32):
            return late.enter_context(nc.sbuf_tensor(name, shape, dt))

        pT = sb("pT", [P, HP, S])
        cen = emb[:, :, :].rearrange("p (b t) d -> p b (t d)", b=2).rearrange("p b (h a) -> p b h a", a=A)
        prb = ua[:, 0:NT // 2, :].rearrange("p (b t) d -> p b (t d)", b=2).rearrange("p b (h a) -> p b h a", a=A)
        nrm = [t.rearrange("p t d -> p (t d)").rearrange("p (h a) -> p h a", a=A)
               for t in (ua[:, NT // 2:3 * NT // 4, :], ua[:, 3 * NT // 4:NT, :], down0[:, :, :])]
        tmax = sb("tmax", [P, 2, H1])
        tsum = sb("tsum", [P, 2, H1])
        trec = sb("trec", [P, 2, H1])
        yT, zz = w_out, w_oT
        asum = sb("asum", [P, 4, HP])
        apart = sb("apart", [P, HP, NT])
        top1 = sb("top1", [P, TPB, E])
        idx1 = sb("idx1", [P, TPB, E], U32)
        idf1 = sb("idf1", [P, TPB, E])
        pd = sb("pd", [P, 4, TPB])
        eq = sb("eq", [P, 4, TPB, E])
        gw = sb("gw", [P, 2, TPB, E])
        s_sc1, s_d1, s_e1, s_gt_ps, s_gt, s_gtl, s_z0 = (sem(n) for n in ("s_sc1", "s_d1", "s_e1", "s_gt_ps", "s_gt", "s_gtl", "s_z0"))
        STEPS = 12
        SCALE1 = float(A) ** -0.5
        LAG1 = 3
        FMAX = 3.4028234663852886e38
        s_ls, s_tm, s_cen, s_pr = sem("s_ls"), sem("s_tm"), sem("s_cen"), sem("s_pr")
        s_ts, s_tr, s_nr, s_y_ps, s_pT_ps, s_pT = sem("s_ts"), sem("s_tr"), sem("s_nr"), sem("s_y_ps"), sem("s_pT_ps"), sem("s_pT")
        s_yT, s_as, s_z_ps, s_z, s_o1_ps, s_x3 = sem("s_yT"), sem("s_as"), sem("s_z_ps"), sem("s_z"), sem("s_o1_ps"), sem("s_x3")
        ln2, ln2_stats, ln2_pool, ln2_norm, ln2_pe, ln2_act, ln2_lo = layernorm("ln2", lambda dve, b: dve.wait_ge(s_x3, b + 1), False)
        with nc.Block() as block:
            @block.tensor
            def _(pe):
                for t in range(NT + LAG1):
                    if t < NT:
                        if t >= 2:
                            pe.wait_ge(s_cen, t - 1)
                        for x, (h_part, w_part) in enumerate(((hT_hi, w_a_hi), (hT_hi, w_a_lo), (hT_lo, w_a_hi))):
                            for m in range(2):
                                last = pe.matmul(ps[:, 2 * (t % 2) + m, :], h_part[:, t * P:(t + 1) * P],
                                                 w_part[:, m * BLK:(m + 1) * BLK], start=(x == 0), stop=(x == 2))
                        last.then_inc(s_ls, 1)
                    if t >= LAG1:
                        u = t - LAG1
                        pe.wait_ge(s_nr, u + 1)
                        pu = nrm[u % 3][:, :, :].rearrange("p h a -> p (h a)")
                        for m in range(2):
                            if u >= 1:
                                pe.wait_ge(s_pT, HP * (u - 1) + 4 * (m + 1))
                            for q in range(4):
                                c0 = (4 * m + q) * P
                                last = pe.transpose(ps[:, 6 + m, q * P:(q + 1) * P], pu[:, c0:c0 + P], ident[:, :])
                            last.then_inc(s_pT_ps, 1)
                            last = pe.matmul(ps[:, 4 + m, :], hn[:, u, :], pu[:, m * BLK:(m + 1) * BLK], start=(u == 0),
                                             stop=(u == NT - 1))
                        last.then_inc(s_y_ps, 1)
                pe.wait_ge(s_yT, 2)
                for h in range(H1):
                    rows = slice((h % 2) * A, (h % 2 + 1) * A)
                    hp = h // 2
                    last = pe.matmul(ps[rows, hp // 4, (hp % 4) * P:(hp % 4 + 1) * P], yT[:, h * A:(h + 1) * A], w_v[:, h, :],
                                     start=True, stop=True)
                last.then_inc(s_z_ps, 1)
                pe.wait_ge(s_z, 2)

                def output(b):
                    if b >= 2:
                        pe.wait_ge(s_x3, b - 1)
                    for i in range(TPB):
                        for hp in range(HP):
                            last = pe.matmul(ps[:, 2 + b % 2, i * P:(i + 1) * P], pT[:, hp, b * BLK + i * P:b * BLK + (i + 1) * P],
                                             zz[:, hp, :], start=(hp == 0), stop=(hp == HP - 1))
                    last.then_inc(s_o1_ps, 1)

                def norm_T(b):
                    if b >= 2:
                        pe.wait_ge(ln2["lo"], b - 1)
                    ln2_pe(pe, b, 4 + b % 2)

                def scores(b):
                    pe.wait_ge(ln2["lo"], b + 1)
                    if b >= 2:
                        pe.wait_ge(s_d1, STEPS * (b - 2) + 2)
                    for i in range(TPB):
                        cols = slice(b * BLK + i * P, b * BLK + (i + 1) * P)
                        o = ps[:, 6 + b % 2, i * E:(i + 1) * E]
                        pe.matmul(o, hT_hi[:, cols], gate1_hi[:, :], start=True, stop=False)
                        pe.matmul(o, hT_hi[:, cols], gate1_lo[:, :], start=False, stop=False)
                        last = pe.matmul(o, hT_lo[:, cols], gate1_hi[:, :], start=False, stop=True)
                    last.then_inc(s_sc1, 1)

                def gates_T(b):
                    pe.wait_ge(s_d1, STEPS * (b + 1))
                    if b >= 2:
                        pe.wait_ge(s_gtl, b - 1)
                    for i in range(TPB):
                        last = pe.transpose(ps[0:E, b % 2, i * P:(i + 1) * P], gw[:, b % 2, i, :], ident[:, :])
                    last.then_inc(s_gt_ps, 1)

                output(0)
                output(1)
                norm_T(0)
                output(2)
                norm_T(1)
                scores(0)
                output(3)
                norm_T(2)
                scores(1)
                gates_T(0)
                norm_T(3)
                scores(2)
                gates_T(1)
                scores(3)
                gates_T(2)
                gates_T(3)

            @block.scalar
            def _(act):
                for t in range(NT + LAG1):
                    if t < NT:
                        act.wait_ge(s_cen, t + 1)
                        if t >= 2:
                            act.wait_ge(s_nr, t - 1)
                        act.activation(prb[:, t % 2], cen[:, t % 2], ACT.Exp, scale=SCALE1).then_inc(s_pr, 1)
                    if t >= LAG1:
                        u = t - LAG1
                        for m in range(2):
                            act.wait_ge(s_pT_ps, 2 * u + m + 1)
                            for q in range(4):
                                act.activation(pT[:, 4 * m + q, u * P:(u + 1) * P], ps[:, 6 + m, q * P:(q + 1) * P],
                                               ACT.Copy, accum_out=apart[:, 4 * m + q, u:u + 1]).then_inc(s_pT, 1)
                act.wait_ge(s_y_ps, NT)
                for m in range(2):
                    act.copy(yT[:, m * BLK:(m + 1) * BLK], ps[:, 4 + m, :]).then_inc(s_yT, 1)

                def gate_exp(b):
                    act.wait_ge(s_d1, STEPS * b + 4)
                    act.activation(pd[:, 1, :], pd[:, 0, :], ACT.Exp).then_inc(s_e1, 1)

                def gates_hi(b):
                    act.wait_ge(s_gt_ps, b + 1)
                    if b == 0:
                        act.wait_ge(s_z0, 1)
                    act.copy(gT[0:E, b * BLK:(b + 1) * BLK], ps[0:E, b % 2, :]).then_inc(s_gt, 1)

                ln2_act(act, 0, 4)
                ln2_act(act, 1, 5)
                gate_exp(0)
                ln2_act(act, 2, 4)
                gate_exp(1)
                gates_hi(0)
                ln2_act(act, 3, 5)
                gate_exp(2)
                gates_hi(1)
                gate_exp(3)
                gates_hi(2)
                gates_hi(3)
                act.activation(warm[:, :], pd[0:1, 1, 0:1], ACT.Silu)

            @block.gpsimd
            def _(pool):
                pool.memset(gT[:, :].bitcast(F32), 0.0).then_inc(s_z0, 1)
                pool.wait_ge(s_z0, 1)
                for b in range(NB):
                    xb = X[:, TPB * b:TPB * (b + 1), :]
                    pool.tensor_tensor(xb, xb, b_out[:, :].unsqueeze(1).to_broadcast([P, TPB, D]), ALU.add).then_inc(s_xb, 1)
                    pool.wait_ge(s_xb, NB + b + 1)
                for t in range(NT):
                    pool.wait_ge(s_tr, t + 1)
                    if t >= 3:
                        pool.wait_ge(s_y_ps, t - 2)
                    pool.tensor_tensor(nrm[t % 3][:, :, :], prb[:, t % 2],
                                       trec[:, t % 2, :].unsqueeze(2).to_broadcast([P, H1, A]), ALU.mult).then_inc(s_nr, 1)
                for b in range(NB):
                    ln2_pool(pool, b)

            @block.vector
            def _(dve):
                for t in range(NT + 1):
                    if t < NT:
                        sc = ps[:, 2 * (t % 2):2 * (t % 2) + 2, :].rearrange("p m (h a) -> p (m h) a", a=A)
                        dve.wait_ge(s_ls, t + 1)
                        dve.tensor_reduce(tmax[:, t % 2, :], sc, AX.X, ALU.max).then_inc(s_tm, 1)
                        dve.wait_ge(s_tm, t + 1)
                        if t >= 2:
                            dve.wait_ge(s_pr, t - 1)
                        dve.tensor_tensor(cen[:, t % 2], sc, tmax[:, t % 2, :].unsqueeze(2).to_broadcast([P, H1, A]),
                                          ALU.subtract).then_inc(s_cen, 1)
                    if t >= 1:
                        u = t - 1
                        dve.wait_ge(s_pr, u + 1)
                        dve.tensor_reduce(tsum[:, u % 2, :], prb[:, u % 2], AX.X, ALU.add).then_inc(s_ts, 1)
                        dve.wait_ge(s_ts, u + 1)
                        if u >= 2:
                            dve.wait_ge(s_nr, u - 1)
                        dve.reciprocal(trec[:, u % 2, :], tsum[:, u % 2, :]).then_inc(s_tr, 1)
                dve.wait_ge(s_pT, HP * NT)
                dve.tensor_reduce(asum[:, 0, :], apart[:, :, :], AX.X, ALU.add).then_inc(s_as, 1)
                dve.wait_ge(s_as, 1)
                dve.reciprocal(asum[:, 1, :], asum[:, 0, :]).then_inc(s_as, 1)
                dve.wait_ge(s_as, 2)
                dve.tensor_scalar(asum[:, 2, :], asum[:, 1, :], FMAX, None, ALU.is_le).then_inc(s_as, 1)
                dve.wait_ge(s_as, 3)
                dve.scalar_tensor_tensor(out=asum[:, 3, :], in0=asum[:, 1, :], scalar=FMAX, in1=asum[:, 2, :],
                                         op0=ALU.min, op1=ALU.mult).then_inc(s_as, 1)
                dve.wait_ge(s_as, 4)
                dve.wait_ge(s_z_ps, 1)
                for m in range(2):
                    dve.tensor_tensor(zz[:, 4 * m:4 * (m + 1), :], ps[:, m, :].rearrange("p (h n) -> p h n", h=4),
                                      asum[:, 3, 4 * m:4 * (m + 1)].unsqueeze(2).to_broadcast([P, 4, D]), ALU.mult).then_inc(s_z, 1)

                def stream(b):
                    dve.wait_ge(s_o1_ps, b + 1)
                    dve.wait_ge(s_xb, NB + b + 1)
                    xb = X[:, TPB * b:TPB * (b + 1), :]
                    dve.tensor_tensor(xb, ps[:, 2 + b % 2, :].rearrange("p (i n) -> p i n", i=TPB), xb, ALU.add).then_inc(s_x3, 1)
                    ln2_stats(dve, b)
                    ln2_norm(dve, b)

                done = [0]

                def step(ins):
                    ins.then_inc(s_d1, 1)
                    done[0] += 1
                    dve.wait_ge(s_d1, done[0])

                def gate(b):
                    dve.wait_ge(s_sc1, b + 1)
                    sc1 = ps[:, 6 + b % 2, 0:TPB * E].rearrange("p (t e) -> p t e", t=TPB)
                    for t in range(TPB):
                        last = dve.max(top1[:, t, :], sc1[:, t, :])
                    step(last)
                    for t in range(TPB):
                        last = dve.max_index(idx1[:, t, :], top1[:, t, :], sc1[:, t, :])
                    step(last)
                    step(dve.tensor_copy(idf1[:, :, :], idx1[:, :, :]))
                    step(dve.tensor_tensor(pd[:, 0, :], top1[:, :, 1], top1[:, :, 0], ALU.subtract))
                    dve.wait_ge(s_e1, b + 1)
                    step(dve.tensor_scalar(pd[:, 2, :], pd[:, 1, :], 1.0, None, ALU.add))
                    step(dve.reciprocal(pd[:, 3, :], pd[:, 2, :]))
                    step(dve.tensor_tensor(pd[:, 2, :], pd[:, 1, :], pd[:, 3, :], ALU.mult))
                    io = iota8[:, :].unsqueeze(1).to_broadcast([P, TPB, E])
                    for k, p in ((0, 3), (1, 2)):
                        step(dve.tensor_tensor(eq[:, k, :, :], io, idf1[:, :, k:k + 1].to_broadcast([P, TPB, E]), ALU.is_equal))
                        step(dve.tensor_tensor(eq[:, 2 + k, :, :], eq[:, k, :, :], pd[:, p, :].unsqueeze(2).to_broadcast([P, TPB, E]), ALU.mult))
                    step(dve.tensor_tensor(gw[:, b % 2, :, :], eq[:, 2, :, :], eq[:, 3, :, :], ALU.add))

                def gates_lo(b):
                    cols = slice(b * BLK, (b + 1) * BLK)
                    dve.wait_ge(s_gt, b + 1)
                    dve.tensor_tensor(gT[32:32 + E, cols], ps[0:E, b % 2, :], gT[0:E, cols].bitcast(F32), ALU.subtract).then_inc(s_gtl, 1)

                stream(0)
                stream(1)
                ln2_lo(dve, 0, 4)
                stream(2)
                ln2_lo(dve, 1, 5)
                gate(0)
                stream(3)
                ln2_lo(dve, 2, 4)
                gate(1)
                gates_lo(0)
                ln2_lo(dve, 3, 5)
                gate(2)
                gates_lo(1)
                gate(3)
                gates_lo(2)
                gates_lo(3)
        late.close()

        def sb(name, shape, dt=F32):
            return ctx.enter_context(nc.sbuf_tensor(name, shape, dt))

        act_g = sb("act_g", [P, 2, BLK])
        prod = sb("prod", [P, 2, BLK])
        hid = sb("hid", [P, 2, BLK])
        hid_hi = sb("hid_hi", [P, 4, BLK], F32R)
        hid_lo = sb("hid_lo", [P, 4, BLK], F32R)
        y_T = sb("y_T", [P, BLK])
        s_gp, s_up, s_bp, s_sil, s_pr1, s_hid, s_hhi, s_hlo = (sem(n) for n in ("s_gp", "s_up", "s_bp", "s_sil", "s_pr1", "s_hid", "s_hhi", "s_hlo"))
        s_dn, s_yT1, s_yt_ps, s_x4, s_out = (sem(n) for n in ("s_dn", "s_yT1", "s_yt_ps", "s_x4", "s_out"))
        sp_f = spread[:, :, :].rearrange("p e m -> p (e m)")
        NS = NB * CH
        DLAG = 3
        with nc.Block() as block:
            @block.gpsimd
            def _(pool):
                for n in range(NS):
                    pool.wait_ge(s_hhi, n + 1)
                    if n >= 4:
                        pool.wait_ge(s_dn, n - 3)
                    pool.tensor_tensor(hid_lo[:, n % 4, :], hid[:, n % 2, :], hid_hi[:, n % 4, :].bitcast(F32),
                                       ALU.subtract).then_inc(s_hlo, 1)

            @block.tensor
            def _(pe):
                def split(out_ps, w, x_hi, x_lo, start=True, stop=True):
                    pe.matmul(out_ps, w[0], x_hi, start=start, stop=False)
                    pe.matmul(out_ps, w[1], x_hi, start=False, stop=False)
                    return pe.matmul(out_ps, w[0], x_lo, start=False, stop=stop)

                def gates(n):
                    b, c = n // CH, n % CH
                    if n >= 2:
                        pe.wait_ge(s_hid, n - 1)
                    pe.matmul(ps[:, 4 + n % 2, :], sp_f[:, c * P:(c + 1) * P], gT[:, b * BLK:(b + 1) * BLK],
                              start=True, stop=True).then_inc(s_bp, 1)

                for n in range(NS + DLAG):
                    if n < NS:
                        b, c = n // CH, n % CH
                        cols, part = slice(b * BLK, (b + 1) * BLK), slice(c * P, (c + 1) * P)
                        if n >= 2:
                            pe.wait_ge(s_sil, n - 1)
                        split(ps[:, n % 2, :], (w_hi[0][:, part], w_lo[0][:, part]), hT_hi[:, cols], hT_lo[:, cols]).then_inc(s_gp, 1)
                        if n >= 2:
                            pe.wait_ge(s_pr1, n - 1)
                        split(ps[:, 2 + n % 2, :], (w_hi[1][:, part], w_lo[1][:, part]), hT_hi[:, cols], hT_lo[:, cols]).then_inc(s_up, 1)
                        gates(n)
                    if n >= DLAG:
                        u = n - DLAG
                        b, c = u // CH, u % CH
                        part = slice(c * P, (c + 1) * P)
                        pe.wait_ge(s_hlo, u + 1)
                        if c == 0 and b >= 1:
                            pe.wait_ge(s_yT1, b)
                        split(ps[:, 6, :], (w_hi[2][:, part], w_lo[2][:, part]), hid_hi[:, u % 4, :], hid_lo[:, u % 4, :],
                              start=(c == 0), stop=(c == CH - 1)).then_inc(s_dn, 1)
                        if c == 1 and b >= 1 or u == NS - 1:
                            o = b if u == NS - 1 else b - 1
                            pe.wait_ge(s_yT1, o + 1)
                            if o >= 1:
                                pe.wait_ge(s_x4, o)
                            for i in range(TPB):
                                last = pe.transpose(ps[:, 7, i * P:(i + 1) * P], y_T[:, i * P:(i + 1) * P], ident[:, :])
                            last.then_inc(s_yt_ps, 1)

            @block.scalar
            def _(act):
                def silu(n):
                    act.wait_ge(s_gp, n + 1)
                    if n >= 2:
                        act.wait_ge(s_pr1, n - 1)
                    act.activation(act_g[:, n % 2, :], ps[:, n % 2, :], ACT.Silu).then_inc(s_sil, 1)

                silu(0)
                silu(1)
                for n in range(2, NS + 2):
                    u = n - 2
                    act.wait_ge(s_hid, u + 1)
                    if u >= 4:
                        act.wait_ge(s_dn, u - 3)
                    act.copy(hid_hi[:, u % 4, :], hid[:, u % 2, :]).then_inc(s_hhi, 1)
                    if n < NS:
                        silu(n)
                    if u % CH == 0 and u >= CH or u == NS - 1:
                        o = u // CH if u == NS - 1 else u // CH - 1
                        act.wait_ge(s_dn, CH * (o + 1))
                        if o >= 1:
                            act.wait_ge(s_yt_ps, o)
                        act.copy(y_T[:, :], ps[:, 6, :]).then_inc(s_yT1, 1)

            @block.vector
            def _(dve):
                for n in range(NS):
                    dve.wait_ge(s_up, n + 1)
                    dve.wait_ge(s_sil, n + 1)
                    if n >= 2:
                        dve.wait_ge(s_hid, n - 1)
                    dve.tensor_tensor(prod[:, n % 2, :], ps[:, 2 + n % 2, :], act_g[:, n % 2, :], ALU.mult).then_inc(s_pr1, 1)
                    dve.wait_ge(s_pr1, n + 1)
                    dve.wait_ge(s_bp, n + 1)
                    if n >= 2:
                        dve.wait_ge(s_hlo, n - 1)
                    dve.tensor_tensor(hid[:, n % 2, :], ps[:, 4 + n % 2, :], prod[:, n % 2, :], ALU.mult).then_inc(s_hid, 1)
                    if n % CH == 8 and n > CH or n == NS - 1:
                        o = n // CH if n == NS - 1 else n // CH - 1
                        dve.wait_ge(s_yt_ps, o + 1)
                        xb = X[:, TPB * o:TPB * (o + 1), :]
                        dve.tensor_tensor(xb, ps[:, 7, :].rearrange("p (i n) -> p i n", i=TPB), xb, ALU.add).then_inc(s_x4, 1)

            @block.sync
            def _(sp):
                out_v = out.rearrange("a (t p) d -> p (a t) d", p=P)
                for b in range(NB):
                    sp.wait_ge(s_x4, b + 1)
                    sp.dma_start(out_v[:, TPB * b:TPB * (b + 1), :], X[:, TPB * b:TPB * (b + 1), :]).then_inc(s_out, 16)
                sp.wait_ge(s_out, 16 * NB)


_INS = ['L0_attn_h_t', 'L0_attn_W_DQ', 'L0_attn_b_DQ', 'L0_attn_W_UQ', 'L0_attn_b_UQ', 'L0_attn_W_DKV',
        'L0_attn_b_DKV', 'L0_attn_W_UK', 'L0_attn_b_UK', 'L0_attn_W_UV', 'L0_attn_b_UV', 'L0_attn_W_QR',
        'L0_attn_b_QR', 'L0_attn_W_KR', 'L0_attn_b_KR', 'L0_attn_W_O', 'L0_attn_b_O', 'L0_ffn_gate_w',
        'L0_ffn_down_w', 'L0_ffn_down_b', 'L0_ffn_up_w', 'L0_ffn_up_b', 'L1_attn_W_emb', 'L1_attn_W_anchor',
        'L1_attn_W_out', 'L1_attn_b_out', 'L1_ffn_w_gate', 'L1_ffn_w_g', 'L1_ffn_w_u', 'L1_ffn_w_d']
_OUTS = [((1, 2048, 128), 'float32')]


def kernel(**inputs):
    import numpy as _np
    import concourse.bacc as _bacc
    from concourse import mybir as _mybir
    from concourse.bass_utils import run_bass_kernel_spmd as _run

    nc = _bacc.Bacc("TRN2", target_bir_lowering=False, num_devices=1)
    arrays, tensors = {}, {}
    for name in _INS:
        a = _np.ascontiguousarray(inputs[name])
        arrays[f"in_{name}_dram"] = a
        tensors[name] = nc.dram_tensor(f"in_{name}_dram", a.shape, _mybir.dt.from_np(a.dtype), kind="ExternalInput").ap()
    outs = []
    for i, (shape, dtype) in enumerate(_OUTS):
        dt = _mybir.dt.from_np(_np.dtype(dtype))
        outs.append(nc.dram_tensor(f"out_{i}_dram", shape, dt, kind="ExternalOutput").ap())
    build_kernel(nc, tensors, outs[0])
    r = _run(nc, [arrays], core_ids=[0])
    got = tuple(r.results[0][f"out_{i}_dram"] for i in range(len(_OUTS)))
    return got[0]
```
